# Optimizing a Trainium2 kernel written in Bass

```python
import numpy as np
import jax
import jax.numpy as jnp

def _softmax(x, axis=-1):
    return jax.nn.softmax(x, axis=axis)

def _gelu(x):
    return jax.nn.gelu(x, approximate=True)

def _silu(x):
    return jax.nn.silu(x)

def _sigmoid(x):
    return jax.nn.sigmoid(x)

def _layernorm(x, axis=-1, eps=1e-05):
    m = jnp.mean(x, axis=axis, keepdims=True)
    v = jnp.var(x, axis=axis, keepdims=True)
    return (x - m) / jnp.sqrt(v + eps)

def _scatter_add(tgt, idx, src, axis=0):
    return tgt.at[idx].add(src)

def _segment_sum(src, seg, n):
    return jax.ops.segment_sum(src, seg, n)
kernel_name = 'mk_decoder_preln_d1_seqx_r4_9ea7c8'

def setup_inputs(seed: int=0):
    np.random.seed(seed)
    _w = jnp.asarray

    def _rec_inputs():
        import jax
        import jax.numpy as jnp
        _rk = jax.random.key(seed)
        x = 4.136e-05 + 0.9999 * jax.random.normal(jax.random.fold_in(_rk, 1), (4, 512, 512), jnp.float32)
        _lenS = 512 - jax.random.randint(jax.random.fold_in(_rk, 7), (4,), 0, max(1, 512 // 4) + 1, jnp.int32)
        _lenS2 = 512 - jax.random.randint(jax.random.fold_in(_rk, 8), (4,), 0, max(1, 512 // 4) + 1, jnp.int32)
        _ctx_1024P = jax.random.normal(jax.random.fold_in(_rk, 11), (4, 16, 256), jnp.float32)
        _ctx_1024c = jax.random.dirichlet(jax.random.fold_in(_rk, 511), 0.3 * jnp.ones((16,), jnp.float32), (4, 512))
        _ctx_1024t = jnp.einsum('bsk,bkd->bsd', _ctx_1024c, _ctx_1024P)
        _ctx_1024t = _ctx_1024t * jax.lax.rsqrt(jnp.mean(jnp.square(_ctx_1024t)) + 1e-12) * 0.953939
        ctx_1024 = -0.000292821 + 1.00034 * (_ctx_1024t + 0.3 * jax.random.normal(jax.random.fold_in(_rk, 611), (4, 512, 256), jnp.float32))
        return (x, ctx_1024)
    x, ctx_1024 = _rec_inputs()

    def _L0_attn_setup():
        import math
        import jax, jax.numpy as jnp
        import numpy as np
        MODEL_DIM = 512
        N_HEADS = 32
        N_GROUPS = 8
        R = N_HEADS // N_GROUPS
        HEAD_DIM = MODEL_DIM // N_HEADS
        KV_DIM = MODEL_DIM // R
        B, S = (1, 512)
        key = jax.random.key(seed)
        k1, k2, k3 = jax.random.split(key, 3)
        scale = 0.02
        return {'x': jax.random.normal(k1, (B, S, MODEL_DIM), dtype=jnp.float32), 'w_qkv': jax.random.normal(k2, (MODEL_DIM + 2 * KV_DIM, MODEL_DIM), dtype=jnp.float32) * scale, 'b_qkv': jnp.zeros((MODEL_DIM + 2 * KV_DIM,), dtype=jnp.float32), 'w_out': jax.random.normal(k3, (MODEL_DIM, MODEL_DIM), dtype=jnp.float32) * scale, 'b_out': jnp.zeros((MODEL_DIM,), dtype=jnp.float32)}
    _L0_attn_all = _L0_attn_setup()
    _L0_attn_in = {k: v for k, v in _L0_attn_all.items() if k in ('w_qkv', 'b_qkv', 'w_out', 'b_out')}
    del _L0_attn_all

    def _L0_xattn_setup():
        import jax, jax.numpy as jnp
        import numpy as np
        import math
        B, L, DM = (2, 512, 256)
        DS, DC, EXP = (16, 4, 2)
        DI = EXP * DM
        DR = math.ceil(DM / 16)
        DT_MIN, DT_MAX, DT_FLOOR = (0.001, 0.1, 0.0001)

        def _ssm_forward(hidden_states, z, in_proj_w, conv_w, conv_b, x_proj_w, dt_proj_w, dt_proj_b, A_log, D):
            b = hidden_states.shape[0]
            x = jnp.einsum('ed,bld->bel', in_proj_w, hidden_states)
            xp = jnp.pad(x, ((0, 0), (0, 0), (DC - 1, 0)))
            xc = jax.lax.conv_general_dilated(xp, conv_w[:, None, :], window_strides=(1,), padding='VALID', dimension_numbers=('NCH', 'OIH', 'NCH'), feature_group_count=DI)
            u = jax.nn.silu(xc + conv_b[None, :, None])
            x_dbl = jnp.einsum('ke,bel->bkl', x_proj_w, u)
            dt_lo = x_dbl[:, :DR]
            Bm = x_dbl[:, DR:DR + DS]
            Cm = x_dbl[:, DR + DS:]
            delta = jax.nn.softplus(jnp.einsum('er,brl->bel', dt_proj_w, dt_lo) + dt_proj_b[None, :, None])
            A = -jnp.exp(A_log)

            def step(state, xs):
                d_t, B_t, C_t, u_t = xs
                dA = jnp.exp(d_t[..., None] * A)
                state = state * dA + (d_t * u_t)[..., None] * B_t[:, None, :]
                y_t = jnp.einsum('ben,bn->be', state, C_t)
                return (state, y_t)
            xs = (jnp.moveaxis(delta, -1, 0), jnp.moveaxis(Bm, -1, 0), jnp.moveaxis(Cm, -1, 0), jnp.moveaxis(u, -1, 0))
            state0 = jnp.zeros((b, DI, DS), delta.dtype)
            _, ys = jax.lax.scan(step, state0, xs)
            y = jnp.moveaxis(ys, 0, -1)
            y = y + D[None, :, None] * u
            y = y * jax.nn.silu(z)
            return jnp.swapaxes(y, 1, 2)
        key = jax.random.key(seed)
        ks = jax.random.split(key, 8)
        hidden_states = jax.random.normal(ks[0], (B, L, DM), jnp.float32)
        z = jax.random.normal(ks[1], (B, DI, L), jnp.float32)
        in_proj_w = jax.random.normal(ks[2], (DI, DM), jnp.float32) * DM ** (-0.5)
        conv_w = jax.random.normal(ks[3], (DI, DC), jnp.float32) * DC ** (-0.5)
        conv_b = jnp.zeros((DI,), jnp.float32)
        x_proj_w = jax.random.normal(ks[4], (DR + 2 * DS, DI), jnp.float32) * DI ** (-0.5)
        dt_std = DR ** (-0.5)
        dt_proj_w = jax.random.uniform(ks[5], (DI, DR), jnp.float32, -dt_std, dt_std)
        dt = jnp.exp(jax.random.uniform(ks[6], (DI,), jnp.float32) * (math.log(DT_MAX) - math.log(DT_MIN)) + math.log(DT_MIN))
        dt = jnp.clip(dt, DT_FLOOR)
        dt_proj_b = dt + jnp.log(-jnp.expm1(-dt))
        A_log = jnp.log(jnp.broadcast_to(jnp.arange(1, DS + 1, dtype=jnp.float32), (DI, DS)))
        D = jnp.ones((DI,), jnp.float32)
        return dict(hidden_states=hidden_states, z=z, in_proj_w=in_proj_w, conv_w=conv_w, conv_b=conv_b, x_proj_w=x_proj_w, dt_proj_w=dt_proj_w, dt_proj_b=dt_proj_b, A_log=A_log, D=D)
    _L0_xattn_all = _L0_xattn_setup()
    _L0_xattn_in = {k: v for k, v in _L0_xattn_all.items() if k in ('in_proj_w', 'conv_w', 'conv_b', 'x_proj_w', 'dt_proj_w', 'dt_proj_b', 'A_log', 'D')}
    del _L0_xattn_all

    def _L0_ffn_setup():
        import jax, jax.numpy as jnp
        import numpy as np
        import math
        B, S, D = (2, 512, 512)
        H, HD = (16, 128)
        E, I = (4, 512)
        TOP_K = 2
        ROPE_THETA = 10000.0

        def _layernorm(x, w, b):
            mu = jnp.mean(x, axis=-1, keepdims=True)
            var = jnp.mean(jnp.square(x - mu), axis=-1, keepdims=True)
            return (x - mu) * jax.lax.rsqrt(var + 1e-05) * w + b

        def _rotate_half(x):
            x1, x2 = jnp.split(x, 2, axis=-1)
            return jnp.concatenate((-x2, x1), axis=-1)

        def _attention(h, wq, bq, wk, bk, wv, bv, wo, bo):
            b, s, _ = h.shape
            q = (h @ wq + bq).reshape(b, s, H, HD).transpose(0, 2, 1, 3)
            k = (h @ wk + bk).reshape(b, s, H, HD).transpose(0, 2, 1, 3)
            v = (h @ wv + bv).reshape(b, s, H, HD).transpose(0, 2, 1, 3)
            inv_freq = 1.0 / ROPE_THETA ** (jnp.arange(0, HD, 2, dtype=jnp.float32) / HD)
            freqs = jnp.arange(s, dtype=jnp.float32)[:, None] * inv_freq[None, :]
            emb = jnp.concatenate((freqs, freqs), axis=-1)
            cos = jnp.cos(emb)[None, None]
            sin = jnp.sin(emb)[None, None]
            q = q * cos + _rotate_half(q) * sin
            k = k * cos + _rotate_half(k) * sin
            scores = jnp.einsum('bhqd,bhkd->bhqk', q, k) / math.sqrt(HD)
            causal = jnp.tril(jnp.ones((s, s), bool))
            scores = jnp.where(causal[None, None], scores, jnp.finfo(jnp.float32).min)
            probs = jax.nn.softmax(scores.astype(jnp.float32), axis=-1).astype(q.dtype)
            out = jnp.einsum('bhqk,bhkd->bhqd', probs, v)
            out = out.transpose(0, 2, 1, 3).reshape(b, s, H * HD)
            return out @ wo + bo

        def _moe(h, w_gate, we1, be1, we2, be2):
            b, s, d = h.shape
            x = h.reshape(-1, d)
            t = x.shape[0]
            raw = jax.nn.softmax(x @ w_gate, axis=-1)
            top_vals, top_idx = jax.lax.top_k(raw, TOP_K)
            w = jax.nn.softmax(top_vals, axis=-1)
            comb = jnp.zeros((t, E), x.dtype).at[jnp.arange(t)[:, None], top_idx].add(w)
            hmid = jax.nn.gelu(jnp.einsum('td,edi->tei', x, we1) + be1[None], approximate=False)
            eout = jnp.einsum('tei,eid->ted', hmid, we2) + be2[None]
            out = jnp.einsum('te,ted->td', comb, eout)
            return out.reshape(b, s, d)
        key = jax.random.key(seed)
        ks = jax.random.split(key, 20)
        s = 0.02
        p = {'hidden_states': jax.random.normal(ks[0], (B, S, D), jnp.float32), 'wq': jax.random.normal(ks[1], (D, H * HD), jnp.float32) * s, 'bq': jnp.zeros((H * HD,), jnp.float32), 'wk': jax.random.normal(ks[2], (D, H * HD), jnp.float32) * s, 'bk': jnp.zeros((H * HD,), jnp.float32), 'wv': jax.random.normal(ks[3], (D, H * HD), jnp.float32) * s, 'bv': jnp.zeros((H * HD,), jnp.float32), 'wo': jax.random.normal(ks[4], (H * HD, D), jnp.float32) * s, 'bo': jnp.zeros((D,), jnp.float32), 'ln1_w': jnp.ones((D,), jnp.float32), 'ln1_b': jnp.zeros((D,), jnp.float32), 'ln2_w': jnp.ones((D,), jnp.float32), 'ln2_b': jnp.zeros((D,), jnp.float32), 'w_gate': jax.random.normal(ks[5], (D, E), jnp.float32) * s, 'we1': jax.random.normal(ks[6], (E, D, I), jnp.float32) * s, 'be1': jnp.zeros((E, I), jnp.float32), 'we2': jax.random.normal(ks[7], (E, I, D), jnp.float32) * s, 'be2': jnp.zeros((E, D), jnp.float32)}
        return p
    _L0_ffn_all = _L0_ffn_setup()
    _L0_ffn_in = {k: v for k, v in _L0_ffn_all.items() if k in ('wq', 'bq', 'wk', 'bk', 'wv', 'bv', 'wo', 'bo', 'ln1_w', 'ln1_b', 'ln2_w', 'ln2_b', 'w_gate', 'we1', 'be1', 'we2', 'be2')}
    del _L0_ffn_all
    return {'x': x, 'ctx_1024': ctx_1024, 'L0_attn_w_qkv': _L0_attn_in['w_qkv'], 'L0_attn_b_qkv': _L0_attn_in['b_qkv'], 'L0_attn_w_out': _L0_attn_in['w_out'], 'L0_attn_b_out': _L0_attn_in['b_out'], 'L0_xattn_in_proj_w': _L0_xattn_in['in_proj_w'], 'L0_xattn_conv_w': _L0_xattn_in['conv_w'], 'L0_xattn_conv_b': _L0_xattn_in['conv_b'], 'L0_xattn_x_proj_w': _L0_xattn_in['x_proj_w'], 'L0_xattn_dt_proj_w': _L0_xattn_in['dt_proj_w'], 'L0_xattn_dt_proj_b': _L0_xattn_in['dt_proj_b'], 'L0_xattn_A_log': _L0_xattn_in['A_log'], 'L0_xattn_D': _L0_xattn_in['D'], 'L0_ffn_wq': _L0_ffn_in['wq'], 'L0_ffn_bq': _L0_ffn_in['bq'], 'L0_ffn_wk': _L0_ffn_in['wk'], 'L0_ffn_bk': _L0_ffn_in['bk'], 'L0_ffn_wv': _L0_ffn_in['wv'], 'L0_ffn_bv': _L0_ffn_in['bv'], 'L0_ffn_wo': _L0_ffn_in['wo'], 'L0_ffn_bo': _L0_ffn_in['bo'], 'L0_ffn_ln1_w': _L0_ffn_in['ln1_w'], 'L0_ffn_ln1_b': _L0_ffn_in['ln1_b'], 'L0_ffn_ln2_w': _L0_ffn_in['ln2_w'], 'L0_ffn_ln2_b': _L0_ffn_in['ln2_b'], 'L0_ffn_w_gate': _L0_ffn_in['w_gate'], 'L0_ffn_we1': _L0_ffn_in['we1'], 'L0_ffn_be1': _L0_ffn_in['be1'], 'L0_ffn_we2': _L0_ffn_in['we2'], 'L0_ffn_be2': _L0_ffn_in['be2']}

def reference(x, ctx_1024, L0_attn_w_qkv, L0_attn_b_qkv, L0_attn_w_out, L0_attn_b_out, L0_xattn_in_proj_w, L0_xattn_conv_w, L0_xattn_conv_b, L0_xattn_x_proj_w, L0_xattn_dt_proj_w, L0_xattn_dt_proj_b, L0_xattn_A_log, L0_xattn_D, L0_ffn_wq, L0_ffn_bq, L0_ffn_wk, L0_ffn_bk, L0_ffn_wv, L0_ffn_bv, L0_ffn_wo, L0_ffn_bo, L0_ffn_ln1_w, L0_ffn_ln1_b, L0_ffn_ln2_w, L0_ffn_ln2_b, L0_ffn_w_gate, L0_ffn_we1, L0_ffn_be1, L0_ffn_we2, L0_ffn_be2):
    import jax
    import jax.numpy as jnp

    def _L0_attn_ref(x, w_qkv, b_qkv, w_out, b_out):
        import math
        import jax, jax.numpy as jnp
        import numpy as np
        MODEL_DIM = 512
        N_HEADS = 32
        N_GROUPS = 8
        R = N_HEADS // N_GROUPS
        HEAD_DIM = MODEL_DIM // N_HEADS
        KV_DIM = MODEL_DIM // R
        B, S = (1, 512)
        Bx, Sx, _ = x.shape
        fused = x @ w_qkv.T + b_qkv
        q = fused[..., :MODEL_DIM]
        k = fused[..., MODEL_DIM:MODEL_DIM + KV_DIM]
        v = fused[..., MODEL_DIM + KV_DIM:]
        q = q.reshape(Bx, Sx, N_GROUPS, R, HEAD_DIM).transpose(0, 2, 3, 1, 4)
        k = k.reshape(Bx, Sx, N_GROUPS, HEAD_DIM).transpose(0, 2, 1, 3)
        v = v.reshape(Bx, Sx, N_GROUPS, HEAD_DIM).transpose(0, 2, 1, 3)
        sim = jnp.einsum('bgrsd,bgtd->bgrst', q, k) / math.sqrt(HEAD_DIM)
        attn = jax.nn.softmax(sim, axis=-1)
        out = jnp.einsum('bgrst,bgtd->bgrsd', attn, v)
        out = out.transpose(0, 3, 1, 2, 4).reshape(Bx, Sx, MODEL_DIM)
        return out @ w_out.T + b_out

    def _L0_xattn_ref(hidden_states, z, in_proj_w, conv_w, conv_b, x_proj_w, dt_proj_w, dt_proj_b, A_log, D):
        import jax, jax.numpy as jnp
        import numpy as np
        import math
        B, L, DM = (2, 512, 256)
        DS, DC, EXP = (16, 4, 2)
        DI = EXP * DM
        DR = math.ceil(DM / 16)
        DT_MIN, DT_MAX, DT_FLOOR = (0.001, 0.1, 0.0001)

        def _ssm_forward(hidden_states, z, in_proj_w, conv_w, conv_b, x_proj_w, dt_proj_w, dt_proj_b, A_log, D):
            b = hidden_states.shape[0]
            x = jnp.einsum('ed,bld->bel', in_proj_w, hidden_states)
            xp = jnp.pad(x, ((0, 0), (0, 0), (DC - 1, 0)))
            xc = jax.lax.conv_general_dilated(xp, conv_w[:, None, :], window_strides=(1,), padding='VALID', dimension_numbers=('NCH', 'OIH', 'NCH'), feature_group_count=DI)
            u = jax.nn.silu(xc + conv_b[None, :, None])
            x_dbl = jnp.einsum('ke,bel->bkl', x_proj_w, u)
            dt_lo = x_dbl[:, :DR]
            Bm = x_dbl[:, DR:DR + DS]
            Cm = x_dbl[:, DR + DS:]
            delta = jax.nn.softplus(jnp.einsum('er,brl->bel', dt_proj_w, dt_lo) + dt_proj_b[None, :, None])
            A = -jnp.exp(A_log)

            def step(state, xs):
                d_t, B_t, C_t, u_t = xs
                dA = jnp.exp(d_t[..., None] * A)
                state = state * dA + (d_t * u_t)[..., None] * B_t[:, None, :]
                y_t = jnp.einsum('ben,bn->be', state, C_t)
                return (state, y_t)
            xs = (jnp.moveaxis(delta, -1, 0), jnp.moveaxis(Bm, -1, 0), jnp.moveaxis(Cm, -1, 0), jnp.moveaxis(u, -1, 0))
            state0 = jnp.zeros((b, DI, DS), delta.dtype)
            _, ys = jax.lax.scan(step, state0, xs)
            y = jnp.moveaxis(ys, 0, -1)
            y = y + D[None, :, None] * u
            y = y * jax.nn.silu(z)
            return jnp.swapaxes(y, 1, 2)
        return _ssm_forward(hidden_states, z, in_proj_w, conv_w, conv_b, x_proj_w, dt_proj_w, dt_proj_b, A_log, D)

    def _L0_ffn_ref(hidden_states, wq, bq, wk, bk, wv, bv, wo, bo, ln1_w, ln1_b, ln2_w, ln2_b, w_gate, we1, be1, we2, be2):
        import jax, jax.numpy as jnp
        import numpy as np
        import math
        B, S, D = (2, 512, 512)
        H, HD = (16, 128)
        E, I = (4, 512)
        TOP_K = 2
        ROPE_THETA = 10000.0

        def _layernorm(x, w, b):
            mu = jnp.mean(x, axis=-1, keepdims=True)
            var = jnp.mean(jnp.square(x - mu), axis=-1, keepdims=True)
            return (x - mu) * jax.lax.rsqrt(var + 1e-05) * w + b

        def _rotate_half(x):
            x1, x2 = jnp.split(x, 2, axis=-1)
            return jnp.concatenate((-x2, x1), axis=-1)

        def _attention(h, wq, bq, wk, bk, wv, bv, wo, bo):
            b, s, _ = h.shape
            q = (h @ wq + bq).reshape(b, s, H, HD).transpose(0, 2, 1, 3)
            k = (h @ wk + bk).reshape(b, s, H, HD).transpose(0, 2, 1, 3)
            v = (h @ wv + bv).reshape(b, s, H, HD).transpose(0, 2, 1, 3)
            inv_freq = 1.0 / ROPE_THETA ** (jnp.arange(0, HD, 2, dtype=jnp.float32) / HD)
            freqs = jnp.arange(s, dtype=jnp.float32)[:, None] * inv_freq[None, :]
            emb = jnp.concatenate((freqs, freqs), axis=-1)
            cos = jnp.cos(emb)[None, None]
            sin = jnp.sin(emb)[None, None]
            q = q * cos + _rotate_half(q) * sin
            k = k * cos + _rotate_half(k) * sin
            scores = jnp.einsum('bhqd,bhkd->bhqk', q, k) / math.sqrt(HD)
            causal = jnp.tril(jnp.ones((s, s), bool))
            scores = jnp.where(causal[None, None], scores, jnp.finfo(jnp.float32).min)
            probs = jax.nn.softmax(scores.astype(jnp.float32), axis=-1).astype(q.dtype)
            out = jnp.einsum('bhqk,bhkd->bhqd', probs, v)
            out = out.transpose(0, 2, 1, 3).reshape(b, s, H * HD)
            return out @ wo + bo

        def _moe(h, w_gate, we1, be1, we2, be2):
            b, s, d = h.shape
            x = h.reshape(-1, d)
            t = x.shape[0]
            raw = jax.nn.softmax(x @ w_gate, axis=-1)
            top_vals, top_idx = jax.lax.top_k(raw, TOP_K)
            w = jax.nn.softmax(top_vals, axis=-1)
            comb = jnp.zeros((t, E), x.dtype).at[jnp.arange(t)[:, None], top_idx].add(w)
            hmid = jax.nn.gelu(jnp.einsum('td,edi->tei', x, we1) + be1[None], approximate=False)
            eout = jnp.einsum('tei,eid->ted', hmid, we2) + be2[None]
            out = jnp.einsum('te,ted->td', comb, eout)
            return out.reshape(b, s, d)
        a = _attention(_layernorm(hidden_states, ln1_w, ln1_b), wq, bq, wk, bk, wv, bv, wo, bo)
        h = hidden_states + a
        m = _moe(_layernorm(h, ln2_w, ln2_b), w_gate, we1, be1, we2, be2)
        return h + m
    x = x + _L0_attn_ref(_layernorm(x, axis=-1), L0_attn_w_qkv, L0_attn_b_qkv, L0_attn_w_out, L0_attn_b_out)
    x = x + _L0_xattn_ref(ctx_1024, _layernorm(x, axis=-1), L0_xattn_in_proj_w, L0_xattn_conv_w, L0_xattn_conv_b, L0_xattn_x_proj_w, L0_xattn_dt_proj_w, L0_xattn_dt_proj_b, L0_xattn_A_log, L0_xattn_D)
    x = x + _L0_ffn_ref(_layernorm(x, axis=-1), L0_ffn_wq, L0_ffn_bq, L0_ffn_wk, L0_ffn_bk, L0_ffn_wv, L0_ffn_bv, L0_ffn_wo, L0_ffn_bo, L0_ffn_ln1_w, L0_ffn_ln1_b, L0_ffn_ln2_w, L0_ffn_ln2_b, L0_ffn_w_gate, L0_ffn_we1, L0_ffn_be1, L0_ffn_we2, L0_ffn_be2)
    return x

_drawn_inputs = setup_inputs


def setup_inputs(seed=0):
    import zlib

    import numpy as np

    out = dict(_drawn_inputs(seed))
    spreads = {'L0_attn_b_qkv': (0.0, 0.1),
     'L0_attn_b_out': (0.0, 0.1),
     'L0_xattn_conv_b': (0.0, 0.1),
     'L0_xattn_D': (1.0, 0.2),
     'L0_ffn_bq': (0.0, 0.8),
     'L0_ffn_bk': (0.0, 0.8),
     'L0_ffn_bv': (0.0, 0.1),
     'L0_ffn_bo': (0.0, 0.1),
     'L0_ffn_ln1_w': (1.0, 0.6),
     'L0_ffn_ln1_b': (0.0, 0.324),
     'L0_ffn_ln2_w': (1.0, 0.6),
     'L0_ffn_ln2_b': (0.0, 0.564),
     'L0_ffn_be1': (0.0, 0.8),
     'L0_ffn_be2': (0.0, 0.277)}
    factors = {'L0_attn_w_qkv': 4.86, 'L0_xattn_dt_proj_w': 5.012, 'L0_ffn_wq': 8.0, 'L0_ffn_wk': 8.0}
    for name, (base, spread) in spreads.items():
        noise = np.random.default_rng([zlib.crc32(name.encode()), seed]).standard_normal(out[name].shape)
        drawn = base * np.exp(spread * noise) if base else spread * noise
        out[name] = jnp.asarray(drawn.astype(out[name].dtype))
    for name, factor in factors.items():
        out[name] = (out[name] * factor).astype(out[name].dtype)
    return out
```

```python
from contextlib import ExitStack

import concourse.bass as bass
from concourse import mybir

F32 = mybir.dt.float32
BF16 = mybir.dt.bfloat16
ACT = mybir.ActivationFunctionType
ALU = mybir.AluOpType
AX = mybir.AxisListType

P = 128
B, S, D = 4, 512, 512
T = S // P
KC = D // P
H1, G1, HD1 = 32, 8, 16
R1 = H1 // G1
HPC = P // HD1
QC = H1 // HPC
NS = 6
QPARTS = (0, 0, 1, 1, 0, 2)
KPARTS = (0, 1, 0, 1, 2, 0)
KM = NS * HD1
SCALE1 = 1.0 / float(HD1) ** 0.5
DM, DI, DS, DR, DC = 256, 512, 16, 16, 4
EC = DI // P
NE = 2
NU = EC // NE
H2, HD2 = 16, 128
G2 = 4
SCALE2 = 1.0 / float(HD2) ** 0.5
NEXP = 4
CH = 2048
NRAW, NPAIR = 2, 3
NRING = NRAW + NPAIR

PCOLS, NPAR = {}, 0
for _name, _w in (("bq1", QC), ("bk1", 1), ("conv_w", EC * DC), ("conv_b", EC), ("dt_b", EC),
                  ("a_log", EC * DS), ("ssm_d", EC), ("ln1_w", KC), ("ln1_b", KC), ("ln2_w", KC),
                  ("ln2_b", KC), ("bq2", H2), ("bk2", H2), ("bv2", H2), ("be1", NEXP * KC),
                  ("eps", 1), ("one", 1), ("w_gate", KC * NEXP)):
    PCOLS[_name] = NPAR
    NPAR += _w


def chunk_order():
    out = []
    for s in range(H2 + 2):
        if s < H2 and s % G2 == 0:
            out.append(("v", s // G2, s))
        if s < H2 and s % 2 == 0:
            out.append(("qk", s // 2, s))
        if s > G2 and s % G2 == 1:
            out.append(("wo", s // G2 - 1, s))
    out.append(("w1", 0, H2 + 2))
    for e in range(NEXP):
        if e + 1 < NEXP:
            out.append(("w1", e + 1, H2 + 2 + e))
        out.append(("w2", e, H2 + 2 + e))
    return out


CHUNKS = chunk_order()
CHUNK_AT = {(k, i): n for n, (k, i, _) in enumerate(CHUNKS)}
CHUNK_ROW = {"v": 0, "qk": 4, "wo": 12, "w1": 16, "w2": 20}
SPLIT_IN_STEP = {s: [n for n, c in enumerate(CHUNKS)
                     if n >= NPAIR and c[2] < H2 + 2 and c[2] - 2 == s] for s in range(H2 + 2)}
_moe = [n for n, c in enumerate(CHUNKS) if c[2] >= H2 + 2]
SPLIT_IN_STEP[H2] = [_moe[0]]
SPLIT_IN_STEP[H2 + 1] = _moe[1:3]
SPLIT_IN_EXPERT = {0: [_moe[3]], 1: [_moe[4]], 2: _moe[5:7], 3: [_moe[7]]}

A_HT1, A_V1, A_MAX = 0, KC, KC + 1
A_CH = HPC * T + 1
A_OUT1 = A_MAX + QC * A_CH
A_GATE = A_OUT1 + T
A_HT2 = A_GATE + T
A_V2, A_QK, A_TURN, A_WO = {}, {}, {}, {}
_n = A_HT2 + KC
for _s in range(H2 + 2):
    if _s < H2 and _s % G2 == 0:
        A_V2[_s // G2] = _n
        _n += T
    if _s < H2:
        A_QK[_s] = _n
        _n += 2
    if _s >= 2:
        A_TURN[_s - 2] = _n
        _n += T
    if _s > G2 and _s % G2 == 1:
        A_WO[_s // G2 - 1] = _n
        _n += T
A_HT3 = _n
A_LOGITS = A_HT3 + KC
A_COMB = A_LOGITS + 1
A_BE2 = A_COMB + 1
A_EXP = A_BE2 + T

SEMS = """const_in x_in be2_in raw_in0 raw_in1 stk_out stk_in0 stk_in1 kst_in m_in0 m_in1 ot_in ctx_in dtw_in xd_out b_in0 b_in1 c_in0 c_in1 y_out
 a_full a_free b_full b_free o_full o_free_norm o_free_head
 ln_stats ln_guess ln_rows ht_hi ht_lo f_ready bias_in ch_hi ch_lo pair_out0 pair_out1 pair_out2 pair_in0 pair_in1 pair_in2 pair_in3 pair_in4
 q_part q_rest q_parts m_parts ones pv1 on_hi on_lo z_silu gated
 cx_hi cx_lo pad_zero conv_done u_done sp_log delta_done du_done y_init
 da_done bx_done prod_done y_acc v_hi rope_f rope_hi rope_lo nmax2 exp2 p_norm pt_hi o_hi o_lo
 router_in router_exp comb hm_hi hm_lo seq_done dve_own act_own""".split()


class Count:

    def __init__(self, sem):
        self.sem, self.n = sem, 0

    def one(self):
        self.n += 1
        return self.sem, 1

    def now(self):
        return self.sem, self.n


def build(nc, x, ctx_t, w_qkv, w_out, in_w, xp_w, dt_w, params, bias_rows, be2, chunks, ident, causal,
          rope, out):
    with ExitStack() as ctx:
        def sb(name, shape, dt=F32):
            return ctx.enter_context(nc.sbuf_tensor(name, shape, dt))

        s_ = {n: ctx.enter_context(nc.semaphore(n)) for n in SEMS}
        lo_sem = min(s.num for s in s_.values())
        hi_sem = max(s.num for s in s_.values())
        assert hi_sem - lo_sem + 1 == len(SEMS)

        stk_d = nc.dram_tensor("stk_d", (QC + 1, P, 3, S), BF16, kind="Internal").ap()
        pair_d = nc.dram_tensor("pair_d", (len(CHUNKS), P, 2, CH), BF16, kind="Internal").ap()
        xd_d = nc.dram_tensor("xd_d", (2 * DS, S), F32, kind="Internal").ap()

        identf = sb("identf", [P, P])
        identb = sb("identb", [P, P], BF16)
        causb = sb("causb", [P, P], BF16)
        par = sb("par", [P, NPAR])
        ropet = sb("ropet", [P, 2, S])
        brow = sb("brow", [P, 2 * D + P])
        xpw = sb("xpw", [P, EC, DR + 2 * DS])
        nega = sb("nega", [P, EC * DS])
        wqkv = sb("wqkv", [P, 2, KC, 768], BF16)
        wout = sb("wout", [P, 2, KC, D], BF16)
        inw = sb("inw", [P, 2, DM // P, DI], BF16)
        pair = sb("pair", [P, NRING, 2, CH], BF16)
        raw = pair[:, NPAIR:NRING].rearrange("p n q c -> p (n q c)").bitcast(F32).rearrange(
            "p (n c) -> p n c", n=NRAW)

        xt = sb("xt", [P, T, D])
        hid = sb("hid", [P, T, D])
        ys = sb("ys", [P, EC, S])
        ht = sb("ht", [P, 2, KC, S], BF16)
        bst = sb("bst", [P, T, 6])
        bmv = sb("bmv", [P, T, 2])
        rs = sb("rs", [P, T])
        ra = sb("ra", [P, T])
        rn = sb("rn", [P, T])
        nmx = sb("nmx", [P, T])
        nbs = sb("nbs", [P, T])
        sm = sb("sm", [P, 2, T])
        rc = sb("rc", [P, T])
        nm1 = sb("nm1", [P, 2, HPC * T])
        gt = sb("gt", [P, 8, T, NEXP])
        gv = sb("gv", [P, 4, T])

        REGION = 25088
        region = sb("region", [P, REGION])

        def carve(at, shape, dt=F32):
            n = 1
            for k in shape:
                n *= k
            words = n if dt == F32 else n // 2
            assert at + words <= REGION, at + words
            a = region[:, at:at + words]
            if dt != F32:
                a = a.bitcast(dt)
            if len(shape) > 1:
                names = "abcd"[:len(shape)]
                a = a.rearrange(f"p ({' '.join(names)}) -> p {' '.join(names)}",
                                **{c: k for c, k in zip(names[1:], shape[1:])})
            return a, at + words

        pf, at = carve(0, [T, S])
        xn = pf
        vp0 = at
        vp, at = carve(at, [2, 2, T, D], BF16)
        qr, at = carve(at, [2, 2, 2, S], BF16)
        rp0 = at
        rp, at = carve(at, [2, S])
        rtmp, at = carve(at, [S])
        pt0 = at
        pt, at = carve(at, [2, T, S], BF16)
        of, at = carve(at, [S])
        op0 = at
        op, at = carve(at, [2, G2, S], BF16)
        dl, at = carve(at, [EC, S])
        du, at = carve(at, [EC, S])
        us, _ = carve(at, [EC, S])
        bx, at = carve(at, [2, NE, S])
        da, at = carve(at, [2, NE, S])
        bb, at = carve(at, [2, S])
        cb, at = carve(at, [2, S])
        dg, _ = carve(at, [T, P])
        xd, at = carve(at, [S])
        cxf, at = carve(vp0, [DM // P, S])
        cx, at = carve(at, [2, DM // P, S], BF16)
        xpad, at = carve(at, [2, S + 4])
        dtw, _ = carve(at, [DI])
        acc, _ = carve(rp0, [2, S])
        spt, _ = carve(op0, [3, S])
        h1f, _ = carve(pt0, [KC, S])
        hm, at = carve(vp0, [2, 2, KC, S], BF16)
        gf, _ = carve(at, [KC, S])
        h2f = gf
        combt, at = carve(pt0, [T, P])
        be2s, _ = carve(at, [D])
        qf, at = carve(T * S, [2, S])
        qres, at = carve(at, [2, S])
        qpt, at = carve(at, [2, 3, S], BF16)
        qst, at = carve(at, [2, HPC, S], BF16)
        kst, at = carve(at, [G1, S], BF16)
        vaug, at = carve(at, [T, G1, 2 * HD1])
        pt1, at = carve(at, [2, R1, S])
        on, at = carve(at, [2, S])
        rec, at = carve(at, [2, S])
        onp, at = carve(at, [G1, 2, S], BF16)
        ot, _ = carve(0, [2, KC, S], BF16)
        mf, at = carve(at, [2, P])
        mpt, at = carve(at, [2, 3, P], BF16)

        PS = ctx.enter_context(nc.psum_tensor("PS", [P, 8, 512], F32))

        def bank_a_at(n):
            return PS[:, n % 2] if n < A_HT2 else PS[:, (0, 1, 6)[(n - A_HT2) % 3]]

        def a_before(n):
            return n - 1 if n < A_HT2 else max(A_HT2, n - 2)

        def bank_b_at(n):
            return PS[:, 2 + 2 * (n % 2):4 + 2 * (n % 2)]

        def col(name, i, n=1):
            a = PCOLS[name] + i
            return par[:, a:a + n]

        def pe3(dst, l, r, start, stop):
            nc.tensor.matmul(dst, l(0), r(0), start=start, stop=False)
            nc.tensor.matmul(dst, l(0), r(1), start=False, stop=False)
            return nc.tensor.matmul(dst, l(1), r(0), start=False, stop=stop)

        loads = [(identf[:], ident), (par[:], params), (ropet[:], rope), (xpw[:], xp_w),
                 (brow[:], bias_rows.to_broadcast([P, 2 * D + P]))]
        stages, at = [], 0
        for src, dst in ((w_qkv, wqkv), (w_out, wout), (in_w, inw)):
            n = src.shape[1]
            stages.append((region[:, at:at + n], src, dst[:, 0].rearrange("p k n -> p (k n)"),
                           dst[:, 1].rearrange("p k n -> p (k n)")))
            at += n
        causf = region[:, at:at + P]
        loads += [(st, src) for st, src, _, _ in stages] + [(causf, causal)]

        with nc.Block() as block:
            @block.sync
            def _(sp):
                for dst, src in loads:
                    sp.dma_start(dst, src).then_inc(s_["const_in"], 16)

            @block.scalar
            def _(act):
                act.wait_ge(s_["const_in"], 16 * len(loads))
                for st, _, hi, _ in stages:
                    nc.scalar.activation(hi, st, ACT.Copy).then_inc(s_["act_own"], 1)
                nc.scalar.activation(identb[:], identf[:], ACT.Copy).then_inc(s_["act_own"], 1)
                nc.scalar.activation(causb[:], causf, ACT.Copy).then_inc(s_["act_own"], 1)
                nc.scalar.activation(nega[:], col("a_log", 0, EC * DS), ACT.Exp).then_inc(s_["act_own"], 1)

            @block.vector
            def _(dve):
                for i, (st, _, hi, lo) in enumerate(stages):
                    dve.wait_ge(s_["act_own"], i + 1)
                    nc.vector.tensor_tensor(lo, st, hi, ALU.subtract).then_inc(s_["dve_own"], 1)
                dve.wait_ge(s_["act_own"], len(stages) + 3)
                nc.vector.tensor_scalar(nega[:], nega[:], -1.0, None, ALU.mult).then_inc(s_["dve_own"], 1)

        def fresh():
            nc.all_engine_barrier()
            nc.gpsimd.sem_clear(range(lo_sem, hi_sem + 1))
            nc.all_engine_barrier()

        fresh()

        def run(b, main, ssm, split=False):
            ring = NPAIR if split else NRING
            B_QKV = 0
            B_SC1 = (QC + 1) if main else 0
            B_SSM = B_SC1 + (2 * T * G1 if main else 0)
            B_SC2 = B_SSM + (2 * EC + 1 if ssm is not None else 0)
            B_EXP = B_SC2 + 2 * H2

            with nc.Block() as block:
                def chunk_free(eng, n):
                    kind, i, _ = CHUNKS[n]
                    if kind == "v":
                        eng.wait_ge(s_["a_full"], A_V2[i] + T)
                    elif kind == "qk":
                        eng.wait_ge(s_["a_full"], A_QK[2 * i + 1] + 2)
                    elif kind == "wo":
                        eng.wait_ge(s_["a_full"], A_WO[i] + T)
                    elif kind == "w1":
                        eng.wait_ge(s_["b_full"], B_EXP + KC * (i + 1))
                    else:
                        eng.wait_ge(s_["a_full"], A_EXP + T * (i + 1))

                def chunk_there(eng, n):
                    if split:
                        eng.wait_ge(s_["ch_lo"], n + 1)
                    else:
                        eng.wait_ge(s_[f"pair_in{n % NRING}"], 16 * (n // NRING + 1))

                @block.sync
                def _(sp):
                    def store_pair(n):
                        sp.dma_start(pair_d[n], pair[:, n % NPAIR]).then_inc(s_[f"pair_out{n % NPAIR}"], 16)

                    def load_chunk(n):
                        if not split:
                            if n >= NRING:
                                chunk_free(sp, n - NRING)
                            sp.dma_start(pair[:, n % NRING], pair_d[n]).then_inc(s_[f"pair_in{n % NRING}"], 16)
                            return
                        if n >= NRAW:
                            sp.wait_ge(s_["ch_lo"], n - NRAW + 1)
                            store_pair(n - NRAW)
                        kind, i, _ = CHUNKS[n]
                        sp.dma_start(raw[:, n % NRAW], chunks[CHUNK_ROW[kind] + i]).then_inc(s_[f"raw_in{n % 2}"], 16)

                    def stack(i):
                        sp.wait_ge(s_["q_parts"], i + 1)
                        sp.dma_start(stk_d[i], qpt[:, i % 2]).then_inc(s_["stk_out"], 16)
                        sp.wait_ge(s_["stk_out"], 16 * (i + 1))
                        if i >= 3:
                            sp.wait_ge(s_["pv1"], 2 * T * (i - 2))
                        for j in range(NS):
                            part = QPARTS[j] if i else KPARTS[j]
                            src = stk_d[i, :, part].rearrange("(h d) n -> d h n", d=HD1)
                            dst = qst[HD1 * j:HD1 * (j + 1), (i - 1) % 2] if i else kst[HD1 * j:HD1 * (j + 1)]
                            sp.dma_start(dst, src).then_inc(s_[f"stk_in{(i - 1) % 2}" if i else "kst_in"], 16)

                    def maxima(c):
                        sp.wait_ge(s_["m_parts"], c + 1)
                        for j in range(3):
                            sp.dma_start(qst[KM + j:KM + j + 1, c % 2].rearrange("o h (t n) -> o (h t) n", n=P),
                                         mpt[0:HPC * T, c % 2, j]).then_inc(s_[f"m_in{c % 2}"], 16)

                    if main:
                        sp.dma_start(xt[:], x[b]).then_inc(s_["x_in"], 16)
                        for n in range(NRAW if split else NRING):
                            load_chunk(n)
                        for i in range(3):
                            stack(i)
                        for n in range(NRAW, NPAIR):
                            if split:
                                load_chunk(n)
                        for c in range(QC):
                            maxima(c)
                            if c + 3 < QC + 1:
                                stack(c + 3)
                        sp.wait_ge(s_["on_lo"], G1)
                        for j in range(R1):
                            for odd in range(2):
                                r0 = HD1 * (R1 * odd + j)
                                for part in range(2):
                                    sp.dma_start(ot[r0:r0 + HD1, part],
                                                 onp[32 * j:32 * j + HD1, odd::2, part]).then_inc(s_["ot_in"], 16)
                    if ssm is not None:
                        if main:
                            sp.wait_ge(s_["gated"], EC)
                        sp.dma_start(cxf, ctx_t[ssm]).then_inc(s_["ctx_in"], 16)
                        sp.dma_start(dtw[0:DR], dt_w).then_inc(s_["dtw_in"], 16)
                        sp.wait_ge(s_["b_free"], B_SSM + EC + 1)
                        sp.dma_start(xd_d, xd[DR:DR + 2 * DS]).then_inc(s_["xd_out"], 16)
                    if main:
                        for n in range(ring, len(CHUNKS)):
                            load_chunk(n)
                            if n - ring == CHUNK_AT["wo", 3]:
                                sp.wait_ge(s_["a_free"], A_HT3)
                                sp.dma_start(be2s[0:NEXP], be2).then_inc(s_["be2_in"], 16)
                        if split:
                            sp.wait_ge(s_["ch_lo"], len(CHUNKS))
                            for n in range(len(CHUNKS) - NRAW, len(CHUNKS)):
                                store_pair(n)
                            for k in range(NPAIR):
                                sp.wait_ge(s_[f"pair_out{k}"], 16 * len(range(k, len(CHUNKS), NPAIR)))
                        for t in range(T):
                            sp.wait_ge(s_["seq_done"], t + 1)
                            sp.dma_start(out[b, :, t], xt[:, t]).then_inc(s_["y_out"], 16)
                        sp.wait_ge(s_["y_out"], 16 * T)

                @block.tensor
                def _(pe):
                    A, Bn = Count(s_["a_full"]), Count(s_["b_full"])

                    def bank_a():
                        if A.n >= 2:
                            pe.wait_ge(s_["a_free"], a_before(A.n))
                        return bank_a_at(A.n)

                    def bank_b():
                        if Bn.n >= 2:
                            pe.wait_ge(s_["b_free"], Bn.n - 1)
                        return bank_b_at(Bn.n)

                    def to_features(norms):
                        for k in range(KC):
                            dst = bank_a()
                            pe.wait_ge(s_["ln_rows"], T * norms)
                            for t in range(T):
                                last = nc.tensor.transpose(dst[:, P * t:P * (t + 1)],
                                                           xn[:, t, P * k:P * (k + 1)], identf[:])
                            last.then_inc(*A.one())

                    def feat(k, t=None):
                        c = slice(0, S) if t is None else slice(P * t, P * (t + 1))
                        return lambda part: ht[:, part, k, c]

                    if main:
                        to_features(1)
                        pe.wait_ge(s_["a_free"], A_HT1 + KC)
                        for m in [QC] + list(range(QC)):
                            dst = bank_b()[:, 0]
                            for k in range(KC):
                                last = pe3(dst, lambda q: wqkv[:, q, k, P * m:P * (m + 1)], feat(k),
                                           k == 0, k == KC - 1)
                            last.then_inc(*Bn.one())
                            if m == QC:
                                dst = bank_a()
                                for t in range(T):
                                    for k in range(KC):
                                        last = pe3(dst[:, P * t:P * (t + 1)], feat(k, t),
                                                   lambda q: wqkv[:, q, k, 640:768], k == 0, k == KC - 1)
                                last.then_inc(*A.one())

                        def score_rows(c, i):
                            h, g = i // T, (HPC * c + i // T) // R1
                            t = i % T
                            dst = bank_a()
                            nc.tensor.matmul(dst, qst[0:KM, c % 2, h, P * t:P * (t + 1)], kst[0:KM, g],
                                             start=True, stop=True).then_inc(*A.one())

                        def score_cols(c, g, kt):
                            for r2 in range(2):
                                dst = bank_b()
                                for r in range(2):
                                    last = nc.tensor.matmul(
                                        dst[:, r], kst[0:KM + 3, g, P * kt:P * (kt + 1)],
                                        qst[0:KM + 3, c % 2, R1 * g + 2 * r2 + r - HPC * c],
                                        start=True, stop=True)
                                last.then_inc(*Bn.one())

                        def key_sums(g, kt):
                            if kt == 0 and g >= 2:
                                pe.wait_ge(s_["o_free_norm"], g - 1)
                            pe.wait_ge(s_["b_free"], B_SC1 + 2 * (T * g + kt) + 2)
                            for r in range(R1):
                                last = nc.tensor.matmul(PS[32 * r:32 * r + 32, 6 + g % 2], vaug[:, kt, g],
                                                        pt1[:, kt % 2, r], start=kt == 0, stop=kt == T - 1)
                            last.then_inc(s_["pv1"], 1)

                        pe.wait_ge(s_["kst_in"], 16 * NS)
                        pe.wait_ge(s_["a_free"], A_V1 + 1)
                        pe.wait_ge(s_["ones"], 2)
                        per = HPC * T // (2 * T)
                        for c in range(QC + 1):
                            if c < QC:
                                pe.wait_ge(s_[f"stk_in{c % 2}"], 16 * NS * (c // 2 + 1))
                            for i in range(2 * T):
                                if c < QC:
                                    for j in range(per):
                                        score_rows(c, per * i + j)
                                if c:
                                    pe.wait_ge(s_[f"m_in{(c - 1) % 2}"], 48 * ((c + 1) // 2))
                                    g, kt = 2 * (c - 1) + i // T, i % T
                                    score_cols(c - 1, g, kt)
                                    if i:
                                        key_sums(2 * (c - 1) + (i - 1) // T, (i - 1) % T)
                            if c:
                                key_sums(2 * (c - 1) + 1, T - 1)
                            if c < QC:
                                dst = bank_a()
                                pe.wait_ge(s_["a_free"], A.n)
                                nc.tensor.transpose(dst[0:HPC * T, 0:P], nm1[:, c % 2],
                                                    identf[:]).then_inc(*A.one())
                        for t in range(T):
                            dst = bank_a()
                            pe.wait_ge(s_["ot_in"], 16 * 4 * R1)
                            for k in range(KC):
                                last = pe3(dst, lambda q: ot[:, q, k, P * t:P * (t + 1)],
                                           lambda q: wout[:, q, k], k == 0, k == KC - 1)
                            last.then_inc(*A.one())
                        for t in range(T):
                            dst = bank_a()
                            pe.wait_ge(s_["gated"], EC)
                            for e in range(EC):
                                last = nc.tensor.transpose(dst[:, P * e:P * (e + 1)],
                                                           ys[:, e, P * t:P * (t + 1)], identf[:])
                            last.then_inc(*A.one())
                        to_features(4)

                    if ssm is not None:
                        pe.wait_ge(s_["cx_lo"], 1)
                        for e in range(EC):
                            dst = bank_b()[:, 0]
                            for k in range(DM // P):
                                last = pe3(dst, lambda q: inw[:, q, k, P * e:P * (e + 1)],
                                           lambda q: cx[:, q, k], k == 0, k == DM // P - 1)
                            last.then_inc(*Bn.one())
                        dst = bank_b()[:, 0]
                        pe.wait_ge(s_["u_done"], EC)
                        for e in range(EC):
                            last = nc.tensor.matmul(dst[0:DR + 2 * DS], xpw[:, e], us[:, e],
                                                    start=e == 0, stop=e == EC - 1)
                        last.then_inc(*Bn.one())
                        pe.wait_ge(s_["b_free"], Bn.n)
                        pe.wait_ge(s_["dtw_in"], 16)
                        for e in range(EC):
                            dst = bank_b()[:, 0]
                            nc.tensor.matmul(dst, dtw[0:DR, P * e:P * (e + 1)], xd[0:DR],
                                             start=True, stop=True).then_inc(*Bn.one())
                    if not main:
                        return

                    def project(s):
                        g = s // G2
                        if s == 0:
                            pe.wait_ge(s_["ht_lo"], KC)
                        if s % G2 == 0:
                            n = CHUNK_AT["v", g]
                            chunk_there(pe, n)
                            for t in range(T):
                                dst = bank_a()
                                for k in range(KC):
                                    last = pe3(dst, feat(k, t), lambda q: pair[:, n % ring, q, D * k:D * (k + 1)],
                                               k == 0, k == KC - 1)
                                last.then_inc(*A.one())
                        n = CHUNK_AT["qk", s // 2]
                        chunk_there(pe, n)
                        for w in range(2):
                            dst = bank_a()
                            o = P * (2 * (s % 2) + w)
                            for k in range(KC):
                                last = pe3(dst, lambda q: pair[:, n % ring, q, D * k + o:D * k + o + P],
                                           feat(k), k == 0, k == KC - 1)
                            last.then_inc(*A.one())

                    def turn(h):
                        pe.wait_ge(s_["p_norm"], h + 1)
                        for kt in range(T):
                            dst = bank_a()
                            for t in range(kt, T):
                                last = nc.tensor.matmul(dst[:, P * t:P * (t + 1)], pf[:, t, P * kt:P * (kt + 1)],
                                                        dg[:, t], start=True, stop=True)
                            last.then_inc(*A.one())

                    def scores(h):
                        pe.wait_ge(s_["rope_lo"], 2 * (h + 1))
                        for u in range(2):
                            dst = bank_b()
                            for j in range(2):
                                t = 2 * u + j
                                pe3(dst[:, j, 0:P * (t + 1)], lambda q: qr[:, h % 2, 0, q, P * t:P * (t + 1)],
                                    lambda q: qr[:, h % 2, 1, q, 0:P * (t + 1)], True, False)
                                last = nc.tensor.matmul(dst[:, j, P * t:P * (t + 1)], identb[:], causb[:],
                                                        start=False, stop=True)
                            last.then_inc(*Bn.one())

                    def values(h):
                        if h == 0:
                            pe.wait_ge(s_["o_free_norm"], G1)
                        else:
                            pe.wait_ge(s_["o_free_head"], h)
                        g, hh = h // G2, h % G2
                        pe.wait_ge(s_["a_free"], A_V2[g] + T)
                        for kt in range(T):
                            pe.wait_ge(s_["a_free"], A_TURN[h] + kt + 1)
                            last = pe3(PS[:, 7, P * kt:S],
                                       lambda q: vp[:, g % 2, q, kt, P * hh:P * (hh + 1)],
                                       lambda q: pt[:, q, kt, P * kt:S], kt == 0, kt == T - 1)
                        last.then_inc(s_["o_full"], 1)

                    def project_out(g):
                        n = CHUNK_AT["wo", g]
                        chunk_there(pe, n)
                        pe.wait_ge(s_["o_lo"], G2 * (g + 1))
                        for t in range(T):
                            dst = bank_a()
                            for h in range(G2):
                                last = pe3(dst, lambda q: op[:, q, h, P * t:P * (t + 1)],
                                           lambda q: pair[:, n % ring, q, D * h:D * (h + 1)],
                                           h == 0, h == G2 - 1)
                            last.then_inc(*A.one())

                    for s in range(H2 + 2):
                        if s < H2:
                            project(s)
                        if s >= 2:
                            turn(s - 2)
                        if 1 <= s <= H2:
                            scores(s - 1)
                        if s >= 2:
                            values(s - 2)
                        if s > G2 and s % G2 == 1:
                            project_out(s // G2 - 1)

                    to_features(5)
                    dst = bank_a()
                    pe.wait_ge(s_["a_free"], A_HT3 + KC)
                    for t in range(T):
                        for k in range(KC):
                            last = nc.tensor.matmul(dst[:, NEXP * t:NEXP * (t + 1)],
                                                    h2f[:, k, P * t:P * (t + 1)], col("w_gate", NEXP * k, NEXP),
                                                    start=k == 0, stop=k == KC - 1)
                    last.then_inc(*A.one())

                    def expert_in(e):
                        n = CHUNK_AT["w1", e]
                        chunk_there(pe, n)
                        pe.wait_ge(s_["ht_lo"], 2 * KC)
                        for i in range(KC):
                            dst = bank_b()[:, 0]
                            for k in range(KC):
                                last = pe3(dst, lambda q: pair[:, n % ring, q, D * k + P * i:D * k + P * (i + 1)],
                                           feat(k), k == 0, k == KC - 1)
                            last.then_inc(*Bn.one())

                    def expert_out(e):
                        n = CHUNK_AT["w2", e]
                        chunk_there(pe, n)
                        pe.wait_ge(s_["hm_lo"], KC * (e + 1))
                        for t in range(T):
                            dst = bank_a()
                            for i in range(KC):
                                last = pe3(dst, lambda q: hm[:, e % 2, q, i, P * t:P * (t + 1)],
                                           lambda q: pair[:, n % ring, q, D * i:D * (i + 1)],
                                           i == 0, i == KC - 1)
                            last.then_inc(*A.one())

                    expert_in(0)
                    dst = bank_a()
                    pe.wait_ge(s_["comb"], 1)
                    for t in range(T):
                        last = nc.tensor.transpose(dst[0:NEXP, P * t:P * (t + 1)], gt[:, 7, t], identf[:])
                    last.then_inc(*A.one())
                    pe.wait_ge(s_["be2_in"], 16)
                    for t in range(T):
                        dst = bank_a()
                        pe.wait_ge(s_["a_free"], A_COMB + 1)
                        nc.tensor.matmul(dst, combt[0:NEXP, t], be2s[0:NEXP], start=True,
                                         stop=True).then_inc(*A.one())
                    for e in range(NEXP):
                        if e + 1 < NEXP:
                            expert_in(e + 1)
                        expert_out(e)
                    assert A.n == A_EXP + T * NEXP and Bn.n == B_EXP + KC * NEXP

                @block.scalar
                def _(act):
                    Bf, own = Count(s_["b_free"]), Count(s_["act_own"])

                    def inv_root(n):
                        act.wait_ge(s_["ln_stats"], T * (n + 1))
                        nc.scalar.activation(ra[:], bmv[:, :, 1], ACT.Ln, bias=col("eps", 0)).then_inc(*own.one())
                        act.wait_ge(*own.now())
                        nc.scalar.activation(rs[:], ra[:], ACT.Exp, scale=-0.5).then_inc(s_["ln_guess"], 1)

                    def chunk_hi(n):
                        act.wait_ge(s_[f"raw_in{n % 2}"], 16 * (n // 2 + 1))
                        if n >= NPAIR:
                            chunk_free(act, n - NPAIR)
                            act.wait_ge(s_[f"pair_out{n % NPAIR}"], 16 * (n // NPAIR))
                        nc.scalar.activation(pair[:, n % NPAIR, 0], raw[:, n % NRAW], ACT.Copy).then_inc(s_["ch_hi"], 1)

                    def full_b():
                        act.wait_ge(s_["b_full"], Bf.n + 1)
                        return bank_b_at(Bf.n)

                    if main:
                        inv_root(0)
                        for k in range(KC):
                            act.wait_ge(s_["a_full"], A_HT1 + k + 1)
                            nc.scalar.activation(ht[:, 0, k], bank_a_at(A_HT1 + k), ACT.Copy).then_inc(s_["ht_hi"], 1)
                        for i in range(QC + 1):
                            src = full_b()
                            if i >= 2:
                                act.wait_ge(s_["q_parts"], i - 1)
                                act.wait_ge(s_["stk_out"], 16 * (i - 1))
                            nc.scalar.activation(qf[:, i % 2], src[:, 0], ACT.Identity,
                                                 bias=col("bq1", i - 1) if i else col("bk1", 0)).then_inc(*Bf.one())
                            act.wait_ge(*Bf.now())
                            nc.scalar.activation(qpt[:, i % 2, 0], qf[:, i % 2], ACT.Copy).then_inc(s_["q_part"], 1)
                            act.wait_ge(s_["q_rest"], i + 1)
                            nc.scalar.activation(qpt[:, i % 2, 1], qres[:, i % 2], ACT.Copy).then_inc(s_["q_part"], 1)
                        for n in range(NPAIR if split else 0):
                            chunk_hi(n)

                        def out_hi(g):
                            act.wait_ge(s_["o_free_norm"], g + 1)
                            nc.scalar.activation(onp[:, g, 0], on[:, g % 2], ACT.Copy).then_inc(s_["on_hi"], 1)

                        for g in range(G1):
                            for kt in range(T):
                                for r2 in range(2):
                                    src = full_b()
                                    if r2 == 0 and T * g + kt >= 2:
                                        act.wait_ge(s_["pv1"], T * g + kt - 1)
                                    nc.scalar.activation(pt1[:, kt % 2, 2 * r2:2 * r2 + 2], src, ACT.Exp,
                                                         scale=SCALE1).then_inc(*Bf.one())
                                if kt == 1 and g:
                                    out_hi(g - 1)
                        out_hi(G1 - 1)
                        inv_root(1)
                        act.wait_ge(s_["ln_rows"], 2 * T)
                        nc.scalar.activation(xn, xn, ACT.Silu).then_inc(s_["z_silu"], 1)
                        inv_root(2)
                        inv_root(3)
                        for k in range(KC):
                            act.wait_ge(s_["a_free"], A_HT2 + k + 1)
                            nc.scalar.activation(ht[:, 0, k], h1f[:, k], ACT.Copy).then_inc(s_["ht_hi"], 1)

                    if ssm is not None:
                        act.wait_ge(s_["ctx_in"], 16)
                        nc.scalar.activation(cx[:, 0], cxf, ACT.Copy).then_inc(s_["cx_hi"], 1)

                        def silu(e):
                            act.wait_ge(s_["conv_done"], e + 1)
                            nc.scalar.activation(us[:, e], acc[:, e % 2], ACT.Silu).then_inc(s_["u_done"], 1)

                        act.wait_ge(s_["pad_zero"], 1)
                        for e in range(EC):
                            src = full_b()
                            nc.scalar.activation(xpad[:, e % 2, DC - 1:DC - 1 + S], src[:, 0],
                                                 ACT.Copy).then_inc(*Bf.one())
                            if e:
                                silu(e - 1)
                        silu(EC - 1)
                        src = full_b()
                        nc.scalar.activation(xd[0:DR + 2 * DS], src[0:DR + 2 * DS, 0], ACT.Copy).then_inc(*Bf.one())
                        for e in range(EC):
                            src = full_b()
                            if e:
                                act.wait_ge(s_["delta_done"], e)
                            nc.scalar.activation(spt[:, 0], src[:, 0], ACT.Abs, bias=col("dt_b", e)).then_inc(*own.one())
                            nc.scalar.activation(spt[:, 2], src[:, 0], ACT.Relu, bias=col("dt_b", e)).then_inc(*Bf.one())
                            act.wait_ge(*own.now())
                            nc.scalar.activation(spt[:, 1], spt[:, 0], ACT.Exp, scale=-1.0).then_inc(*own.one())
                            act.wait_ge(*own.now())
                            nc.scalar.activation(spt[:, 0], spt[:, 1], ACT.Ln, bias=col("one", 0)).then_inc(s_["sp_log"], 1)
                        act.wait_ge(s_["xd_out"], 16)

                    def load_state(s):
                        if s >= 2:
                            act.wait_ge(s_["bx_done"], NU * (s - 1))
                            act.wait_ge(s_["prod_done"], NU * (s - 1))
                        nc.scalar.dma_start(bb[:, s % 2], xd_d[s:s + 1].to_broadcast([P, S])).then_inc(s_[f"b_in{s % 2}"], 16)
                        nc.scalar.dma_start(cb[:, s % 2],
                                            xd_d[DS + s:DS + s + 1].to_broadcast([P, S])).then_inc(s_[f"c_in{s % 2}"], 16)

                    def decay(s):
                        if s == 0:
                            act.wait_ge(s_["delta_done"], EC)
                            act.wait_ge(s_["du_done"], EC)
                        for u in range(NU):
                            i = NU * s + u
                            if i >= 2:
                                act.wait_ge(s_["prod_done"], i - 1)
                            for j in range(NE):
                                e = NE * u + j
                                nc.scalar.activation(da[:, i % 2, j, 1:S], dl[:, e, 1:S], ACT.Exp,
                                                     scale=nega[:, DS * e + s:DS * e + s + 1]).then_inc(s_["da_done"], 1)

                    if ssm is not None:
                        load_state(0)
                    for s in range(H2 + 2):
                        if ssm is not None and s < DS:
                            decay(s)
                        if main and s < H2:
                            if s % G2 == 0:
                                for t in range(T):
                                    a = A_V2[s // G2] + t
                                    act.wait_ge(s_["a_full"], a + 1)
                                    nc.scalar.activation(vp[:, s // G2 % 2, 0, t], bank_a_at(a),
                                                         ACT.Copy).then_inc(s_["v_hi"], 1)
                            for w in range(2):
                                act.wait_ge(s_["rope_f"], 2 * s + w + 1)
                                if s >= 2:
                                    act.wait_ge(s_["b_full"], B_SC2 + 2 * (s - 1))
                                nc.scalar.activation(qr[:, s % 2, w, 0], rp[:, w], ACT.Copy).then_inc(s_["rope_hi"], 1)
                        if ssm is not None and s + 1 < DS:
                            load_state(s + 1)
                        if not main:
                            continue
                        if s >= 2:
                            for kt in range(T):
                                a = A_TURN[s - 2] + kt
                                act.wait_ge(s_["a_full"], a + 1)
                                if s >= 3:
                                    act.wait_ge(s_["o_full"], s - 2)
                                nc.scalar.activation(pt[:, 0, kt, P * kt:S], bank_a_at(a)[:, P * kt:S],
                                                     ACT.Copy).then_inc(s_["pt_hi"], 1)
                        if 1 <= s <= H2:
                            h = s - 1
                            for u in range(2):
                                src = full_b()
                                act.wait_ge(s_["nmax2"], 2 * h + u + 1)
                                for j in range(2):
                                    t = 2 * u + j
                                    sem = (s_["exp2"], 1) if j == 0 else Bf.one()
                                    nc.scalar.activation(pf[:, t, 0:P * (t + 1)], src[:, j, 0:P * (t + 1)], ACT.Exp,
                                                         bias=nbs[:, t:t + 1], scale=SCALE2,
                                                         accum_out=sm[:, h % 2, t:t + 1]).then_inc(*sem)
                        if s >= 2:
                            h = s - 2
                            act.wait_ge(s_["o_full"], h + 1)
                            if h:
                                act.wait_ge(s_["o_lo"], h)
                            nc.scalar.activation(of, PS[:, 7], ACT.Identity,
                                                 bias=col("bv2", h)).then_inc(s_["o_free_head"], 1)
                            act.wait_ge(s_["o_free_head"], h + 1)
                            if h >= G2 and h % G2 == 0:
                                act.wait_ge(s_["a_full"], A_WO[h // G2 - 1] + T)
                            nc.scalar.activation(op[:, 0, h % G2], of, ACT.Copy).then_inc(s_["o_hi"], 1)
                        for n in SPLIT_IN_STEP[s] if split else []:
                            chunk_hi(n)
                    if not main:
                        return
                    inv_root(4)
                    for k in range(KC):
                        act.wait_ge(s_["a_free"], A_HT3 + k + 1)
                        nc.scalar.activation(ht[:, 0, k], h2f[:, k], ACT.Copy).then_inc(s_["ht_hi"], 1)
                    for i in range(2):
                        act.wait_ge(s_["router_in"], i + 1)
                        nc.scalar.activation(gt[:, 1 + 2 * i], gt[:, 2 * i], ACT.Exp).then_inc(s_["router_exp"], 1)
                    act.wait_ge(s_["a_full"], A_LOGITS + 1)
                    act.wait_ge(s_["ht_lo"], 2 * KC)
                    for e in range(NEXP):
                        for i in range(KC):
                            src = full_b()
                            if e:
                                act.wait_ge(s_["hm_lo"], KC * (e - 1) + i + 1)
                            nc.scalar.activation(gf[:, i], src[:, 0], ACT.Gelu,
                                                 bias=col("be1", KC * e + i)).then_inc(*Bf.one())
                            if e >= 2:
                                act.wait_ge(s_["a_full"], A_EXP + T * (e - 1))
                            act.wait_ge(*Bf.now())
                            nc.scalar.activation(hm[:, e % 2, 0, i], gf[:, i], ACT.Copy).then_inc(s_["hm_hi"], 1)
                        for n in SPLIT_IN_EXPERT[e] if split else []:
                            chunk_hi(n)

                @block.gpsimd
                def _(pool):
                    def chunk_lo(n):
                        pool.wait_ge(s_["ch_hi"], n + 1)
                        nc.gpsimd.tensor_tensor(pair[:, n % NPAIR, 1], raw[:, n % NRAW], pair[:, n % NPAIR, 0],
                                                ALU.subtract).then_inc(s_["ch_lo"], 1)

                    def add_bias(dst, o, norms):
                        pool.wait_ge(s_["ln_rows"], T * norms)
                        for t in range(T):
                            nc.gpsimd.tensor_tensor(dst[:, t], dst[:, t], brow[:, o:o + D],
                                                    ALU.add).then_inc(s_["bias_in"], 1)

                    def features_lo(f32, n):
                        for k in range(KC):
                            pool.wait_ge(s_["ht_hi"], KC * n + k + 1)
                            nc.gpsimd.tensor_tensor(ht[:, 1, k], f32[:, k], ht[:, 0, k],
                                                    ALU.subtract).then_inc(s_["ht_lo"], 1)

                    if main:
                        nc.gpsimd.memset(vaug[:, :, :, HD1:2 * HD1], 1.0).then_inc(s_["ones"], 1)
                        pool.wait_ge(s_["ones"], 1)
                        nc.gpsimd.memset(kst[KM:KM + 32], 1.0).then_inc(s_["ones"], 1)
                        pool.wait_ge(s_["ones"], 2)
                        add_bias(xt, 0, 1)
                        for n in range(NPAIR if split else 0):
                            chunk_lo(n)
                        features_lo(h1f, 1)
                        add_bias(hid, D, 4)
                    if ssm is not None:
                        pool.wait_ge(s_["cx_hi"], 1)
                        nc.gpsimd.tensor_tensor(cx[:, 1], cxf, cx[:, 0], ALU.subtract).then_inc(s_["cx_lo"], 1)
                    def add_product(i):
                        u = i % NU
                        pool.wait_ge(s_["prod_done"], i + 1)
                        if i >= NU:
                            pool.wait_ge(s_["y_acc"], i - NU + 1)
                        y = ys[:, NE * u:NE * (u + 1)]
                        nc.gpsimd.tensor_tensor(y, y, bx[:, i % 2], ALU.add).then_inc(s_["y_acc"], 1)

                    for s in range(H2 + 2):
                        if main and ssm is not None and s == DS:
                            add_product(NU * DS - 2)
                            add_product(NU * DS - 1)
                        if ssm is not None and s < DS:
                            for u in range(NU):
                                i = NU * s + u
                                if main and i >= 2:
                                    add_product(i - 2)
                                pool.wait_ge(s_[f"b_in{s % 2}"], 16 * (s // 2 + 1))
                                if i == 0:
                                    pool.wait_ge(s_["du_done"], EC)
                                    pool.wait_ge(s_["y_init"], EC)
                                if i >= 2:
                                    pool.wait_ge(s_["y_acc"], i - 1)
                                nc.gpsimd.tensor_tensor(
                                    bx[:, i % 2], du[:, NE * u:NE * (u + 1)],
                                    bb[:, s % 2].unsqueeze(1).to_broadcast([P, NE, S]),
                                    ALU.mult).then_inc(s_["bx_done"], 1)
                        if not main:
                            continue
                        if s < H2:
                            for w in range(2):
                                pool.wait_ge(s_["rope_hi"], 2 * s + w + 1)
                                nc.gpsimd.tensor_tensor(qr[:, s % 2, w, 1], rp[:, w], qr[:, s % 2, w, 0],
                                                        ALU.subtract).then_inc(s_["rope_lo"], 1)
                        if s >= 2:
                            h = s - 2
                            pool.wait_ge(s_["o_hi"], h + 1)
                            nc.gpsimd.tensor_tensor(op[:, 1, h % G2], of, op[:, 0, h % G2],
                                                    ALU.subtract).then_inc(s_["o_lo"], 1)
                        for n in SPLIT_IN_STEP[s] if split else []:
                            chunk_lo(n)
                    if not main:
                        return
                    features_lo(h2f, 2)
                    for e in range(NEXP):
                        for i in range(KC):
                            pool.wait_ge(s_["hm_hi"], KC * e + i + 1)
                            nc.gpsimd.tensor_tensor(hm[:, e % 2, 1, i], gf[:, i], hm[:, e % 2, 0, i],
                                                    ALU.subtract).then_inc(s_["hm_lo"], 1)
                        for n in SPLIT_IN_EXPERT[e] if split else []:
                            chunk_lo(n)

                @block.vector
                def _(dve):
                    Af, own = Count(s_["a_free"]), Count(s_["dve_own"])
                    stats, rows = Count(s_["ln_stats"]), Count(s_["ln_rows"])
                    norms = [0]

                    def full_a():
                        dve.wait_ge(s_["a_full"], Af.n + 1)
                        return bank_a_at(Af.n)

                    def layer_norm(src, dst):
                        for t in range(T):
                            nc.vector.bn_stats(bst[:, t], src[:, t]).then_inc(*own.one())
                        dve.wait_ge(*own.now())
                        for t in range(T):
                            nc.vector.bn_aggr(bmv[:, t], bst[:, t]).then_inc(*stats.one())
                        norms[0] += 1
                        dve.wait_ge(s_["ln_guess"], norms[0])
                        nc.vector.tensor_tensor(rn[:], rs[:], rs[:], ALU.mult).then_inc(*own.one())
                        dve.wait_ge(*own.now())
                        nc.vector.scalar_tensor_tensor(rn[:], bmv[:, :, 1], 1e-5, rn[:], ALU.add,
                                                       ALU.mult).then_inc(*own.one())
                        dve.wait_ge(*own.now())
                        nc.vector.tensor_scalar(rn[:], rn[:], -0.5, 1.5, ALU.mult, ALU.add).then_inc(*own.one())
                        dve.wait_ge(*own.now())
                        nc.vector.tensor_tensor(rs[:], rs[:], rn[:], ALU.mult).then_inc(*own.one())
                        dve.wait_ge(*own.now())
                        for t in range(T):
                            nc.vector.tensor_scalar(dst[:, t], src[:, t], bmv[:, t, 0:1], rs[:, t:t + 1],
                                                    ALU.subtract, ALU.mult).then_inc(*rows.one())

                    def scaled_features(dst, name):
                        for k in range(KC):
                            src = full_a()
                            nc.vector.tensor_scalar(dst[:, k], src, col(name + "_w", k), col(name + "_b", k),
                                                    ALU.mult, ALU.add).then_inc(*Af.one())

                    if main:
                        dve.wait_ge(s_["x_in"], 16)
                        layer_norm(xt, xn)
                        for k in range(KC):
                            src = full_a()
                            dve.wait_ge(s_["ht_hi"], k + 1)
                            nc.vector.tensor_tensor(ht[:, 1, k], src, ht[:, 0, k], ALU.subtract).then_inc(*Af.one())
                        src = full_a()
                        for t in range(T):
                            sem = Af.one() if t == T - 1 else own.one()
                            nc.vector.tensor_tensor(
                                vaug[:, t, :, 0:HD1], src[:, P * t:P * (t + 1)].rearrange("p (g d) -> p g d", d=HD1),
                                brow[:, 2 * D:2 * D + P].rearrange("p (g d) -> p g d", d=HD1),
                                ALU.add).then_inc(*sem)
                        for i in range(QC + 1):
                            dve.wait_ge(s_["q_part"], 2 * i + 1)
                            if i >= 2:
                                dve.wait_ge(s_["q_parts"], i - 1)
                            nc.vector.tensor_tensor(qres[:, i % 2], qf[:, i % 2], qpt[:, i % 2, 0],
                                                    ALU.subtract).then_inc(s_["q_rest"], 1)
                            dve.wait_ge(s_["q_part"], 2 * i + 2)
                            nc.vector.tensor_tensor(qpt[:, i % 2, 2], qres[:, i % 2], qpt[:, i % 2, 1],
                                                    ALU.subtract).then_inc(s_["q_parts"], 1)

                        def normalise(g):
                            dve.wait_ge(s_["pv1"], T * (g + 1))
                            acc1 = PS[:, 6 + g % 2]
                            if g >= 2:
                                dve.wait_ge(s_["on_lo"], g - 1)
                            nc.vector.stream_shuffle(rec[:, g % 2], acc1,
                                                     [HD1 + i % HD1 for i in range(32)]).then_inc(*own.one())
                            dve.wait_ge(*own.now())
                            nc.vector.reciprocal(rec[:, g % 2], rec[:, g % 2]).then_inc(*own.one())
                            dve.wait_ge(*own.now())
                            nc.vector.tensor_tensor(on[:, g % 2], acc1, rec[:, g % 2],
                                                    ALU.mult).then_inc(s_["o_free_norm"], 1)
                            dve.wait_ge(s_["o_free_norm"], g + 1)

                        def split_out(g):
                            dve.wait_ge(s_["on_hi"], g + 1)
                            nc.vector.tensor_tensor(onp[:, g, 1], on[:, g % 2], onp[:, g, 0],
                                                    ALU.subtract).then_inc(s_["on_lo"], 1)

                        per = HPC * T // (2 * T)
                        for c in range(QC + 1):
                            for i in range(2 * T):
                                if c < QC:
                                    for j in range(per * i, per * (i + 1)):
                                        src = full_a()
                                        nc.vector.tensor_reduce(nm1[:, c % 2, j:j + 1], src, AX.X, ALU.max,
                                                                negate=True).then_inc(*Af.one())
                                if c >= 2 and i == T:
                                    split_out(2 * c - 3)
                                if c and i == T:
                                    normalise(2 * c - 2)
                            if c < QC:
                                src = full_a()
                                n = HPC * T
                                if c >= 2:
                                    dve.wait_ge(s_[f"m_in{c % 2}"], 48 * (c // 2))
                                nc.vector.tensor_copy(mpt[0:n, c % 2, 0], src[0:n, 0:P]).then_inc(*own.one())
                                dve.wait_ge(*own.now())
                                nc.vector.tensor_tensor(mf[0:n, 0], src[0:n, 0:P], mpt[0:n, c % 2, 0],
                                                        ALU.subtract).then_inc(*Af.one())
                                dve.wait_ge(*Af.now())
                                nc.vector.tensor_copy(mpt[0:n, c % 2, 1], mf[0:n, 0]).then_inc(*own.one())
                                dve.wait_ge(*own.now())
                                nc.vector.tensor_tensor(mf[0:n, 1], mf[0:n, 0], mpt[0:n, c % 2, 1],
                                                        ALU.subtract).then_inc(*own.one())
                                dve.wait_ge(*own.now())
                                nc.vector.tensor_copy(mpt[0:n, c % 2, 2], mf[0:n, 1]).then_inc(s_["m_parts"], 1)
                            if c:
                                split_out(2 * c - 2)
                                normalise(2 * c - 1)
                        split_out(G1 - 1)
                        dve.wait_ge(s_["bias_in"], T)
                        for t in range(T):
                            src = full_a()
                            nc.vector.tensor_tensor(xt[:, t], src, xt[:, t], ALU.add).then_inc(*Af.one())
                        dve.wait_ge(*Af.now())
                        layer_norm(xt, xn)
                        dve.wait_ge(s_["z_silu"], 1)
                        for e in range(EC):
                            nc.vector.tensor_tensor(ys[:, e], ys[:, e], xn[:, e], ALU.mult).then_inc(s_["gated"], 1)
                        for t in range(T):
                            src = full_a()
                            nc.vector.tensor_tensor(xt[:, t], src, xt[:, t], ALU.add).then_inc(*Af.one())
                        dve.wait_ge(*Af.now())
                        layer_norm(xt, hid)
                        dve.wait_ge(*rows.now())
                        layer_norm(hid, xn)
                        scaled_features(h1f, "ln1")

                    if ssm is not None:
                        nc.vector.memset(da[:, :, :, 0:1], 0.0).then_inc(*own.one())
                        nc.vector.memset(xpad[:, :, 0:DC - 1], 0.0).then_inc(s_["pad_zero"], 1)
                        for e in range(EC):
                            dve.wait_ge(s_["b_free"], B_SSM + e + 1)
                            if e >= 2:
                                dve.wait_ge(s_["u_done"], e - 1)
                            a = acc[:, e % 2]
                            nc.vector.tensor_scalar(a, xpad[:, e % 2, 0:S], col("conv_w", DC * e), col("conv_b", e),
                                                    ALU.mult, ALU.add).then_inc(*own.one())
                            for j in range(1, DC):
                                dve.wait_ge(*own.now())
                                sem = (s_["conv_done"], 1) if j == DC - 1 else own.one()
                                nc.vector.scalar_tensor_tensor(a, xpad[:, e % 2, j:j + S], col("conv_w", DC * e + j),
                                                               a, ALU.mult, ALU.add).then_inc(*sem)
                        dve.wait_ge(s_["u_done"], EC)
                        for e in range(EC):
                            nc.vector.tensor_scalar(ys[:, e], us[:, e], col("ssm_d", e), None,
                                                    ALU.mult).then_inc(s_["y_init"], 1)
                        for e in range(EC):
                            dve.wait_ge(s_["sp_log"], e + 1)
                            nc.vector.tensor_tensor(dl[:, e], spt[:, 2], spt[:, 0], ALU.add).then_inc(s_["delta_done"], 1)
                            dve.wait_ge(s_["delta_done"], e + 1)
                            nc.vector.tensor_tensor(du[:, e], dl[:, e], us[:, e], ALU.mult).then_inc(s_["du_done"], 1)

                    def scan(s, us_=range(NU)):
                        for u in us_:
                            i = NU * s + u
                            k = i % 2
                            dve.wait_ge(s_["bx_done"], i + 1)
                            dve.wait_ge(s_["da_done"], NE * (i + 1))
                            flat = bx[:, k].rearrange("p e n -> p (e n)")
                            nc.vector.tensor_tensor_scan(flat, da[:, k].rearrange("p e n -> p (e n)"), flat, 0.0,
                                                         ALU.mult, ALU.add).then_inc(*own.one())
                            dve.wait_ge(*own.now())
                            dve.wait_ge(s_[f"c_in{s % 2}"], 16 * (s // 2 + 1))
                            nc.vector.tensor_tensor(bx[:, k], bx[:, k], cb[:, s % 2].unsqueeze(1).to_broadcast([P, NE, S]),
                                                    ALU.mult).then_inc(s_["prod_done"], 1)
                            if main:
                                continue
                            dve.wait_ge(s_["prod_done"], i + 1)
                            y = ys[:, NE * u:NE * (u + 1)]
                            if i >= NU:
                                dve.wait_ge(s_["y_acc"], i - NU + 1)
                            nc.vector.tensor_tensor(y, y, bx[:, k], ALU.add).then_inc(s_["y_acc"], 1)

                    for s in range(H2 + 2):
                        if main and s >= 2:
                            h = s - 2
                            dve.wait_ge(s_["b_free"], B_SC2 + 2 * (h + 1))
                            nc.vector.reciprocal(rc[:], sm[:, h % 2]).then_inc(*own.one())
                            dve.wait_ge(*own.now())
                            nc.vector.tensor_tensor(dg, identf[:].unsqueeze(1).to_broadcast([P, T, P]),
                                                    rc[:].unsqueeze(2).to_broadcast([P, T, P]),
                                                    ALU.mult).then_inc(s_["p_norm"], 1)
                        if main and s < H2:
                            if s % G2 == 0:
                                for t in range(T):
                                    src = full_a()
                                    dve.wait_ge(s_["v_hi"], T * (s // G2) + t + 1)
                                    k = s // G2 % 2
                                    nc.vector.tensor_tensor(vp[:, k, 1, t], src, vp[:, k, 0, t],
                                                            ALU.subtract).then_inc(*Af.one())
                            for w in range(2):
                                src = full_a()
                                if s:
                                    dve.wait_ge(s_["rope_lo"], 2 * (s - 1) + w + 1)
                                bias = col("bk2" if w else "bq2", s)
                                nc.vector.scalar_tensor_tensor(rp[:, w], src, bias, ropet[:, 0], ALU.add,
                                                               ALU.mult).then_inc(*own.one())
                                half = P // 2
                                for a, z in ((0, half), (half, 0)):
                                    sem = Af.one() if z == 0 else own.one()
                                    nc.vector.scalar_tensor_tensor(
                                        rtmp[a:a + half], src[z:z + half], bias[z:z + half],
                                        ropet[z:z + half, 1], ALU.add, ALU.mult).then_inc(*sem)
                                dve.wait_ge(*Af.now())
                                nc.vector.tensor_tensor(rp[:, w], rp[:, w], rtmp, ALU.add).then_inc(s_["rope_f"], 1)
                                dve.wait_ge(s_["rope_f"], 2 * s + w + 1)
                        if main and s >= 2:
                            for kt in range(T):
                                src = full_a()
                                dve.wait_ge(s_["pt_hi"], T * (s - 2) + kt + 1)
                                nc.vector.tensor_tensor(pt[:, 1, kt, P * kt:S], src[:, P * kt:S],
                                                        pt[:, 0, kt, P * kt:S], ALU.subtract).then_inc(*Af.one())
                        if main and ssm is not None and s < DS:
                            scan(s, range(1))
                        if main and 1 <= s <= H2:
                            h = s - 1
                            for u in range(2):
                                dve.wait_ge(s_["b_full"], B_SC2 + 2 * h + u + 1)
                                src = bank_b_at(B_SC2 + 2 * h + u)
                                for j in range(2):
                                    t = 2 * u + j
                                    nc.vector.tensor_reduce(nmx[:, t:t + 1], src[:, j, 0:P * (t + 1)], AX.X, ALU.max,
                                                            negate=True).then_inc(*own.one())
                                dve.wait_ge(*own.now())
                                nc.vector.tensor_scalar(nbs[:, 2 * u:2 * u + 2], nmx[:, 2 * u:2 * u + 2], SCALE2, None,
                                                        ALU.mult).then_inc(s_["nmax2"], 1)
                        if main and s > G2 and s % G2 == 1:
                            if s // G2 == 1:
                                dve.wait_ge(s_["bias_in"], 2 * T)
                            for t in range(T):
                                src = full_a()
                                nc.vector.tensor_tensor(hid[:, t], src, hid[:, t], ALU.add).then_inc(*Af.one())
                            dve.wait_ge(*Af.now())
                        if ssm is not None and s < DS:
                            scan(s, range(1, NU) if main else range(NU))
                    if not main:
                        return

                    layer_norm(hid, xn)
                    scaled_features(h2f, "ln2")
                    src = full_a()

                    def step(ins, sem=None):
                        sem = sem or own.one()
                        ins.then_inc(*sem)
                        dve.wait_ge(sem[0], 1 if sem[0] is not own.sem else own.n)

                    def over_e(a):
                        return a.unsqueeze(2).to_broadcast([P, T, NEXP])

                    tt, tr = nc.vector.tensor_tensor, nc.vector.tensor_reduce
                    nc.vector.tensor_copy(gt[:, 4], src[:, 0:T * NEXP].rearrange("p (t e) -> p t e",
                                                                                e=NEXP)).then_inc(*Af.one())
                    dve.wait_ge(*Af.now())
                    step(tr(gv[:, 0], gt[:, 4], AX.X, ALU.max))
                    tt(gt[:, 0], gt[:, 4], over_e(gv[:, 0]), ALU.subtract).then_inc(s_["router_in"], 1)
                    dve.wait_ge(s_["router_exp"], 1)
                    step(tr(gv[:, 1], gt[:, 1], AX.X, ALU.add))
                    step(nc.vector.reciprocal(gv[:, 1], gv[:, 1]))
                    step(tt(gt[:, 4], gt[:, 1], over_e(gv[:, 1]), ALU.mult))
                    for e in range(NEXP):
                        me = gt[:, 4, :, e:e + 1]
                        if e:
                            tt(gt[:, 5, :, 0:e], gt[:, 4, :, 0:e], me.to_broadcast([P, T, e]),
                               ALU.is_ge).then_inc(*own.one())
                        step(tt(gt[:, 5, :, e:NEXP], gt[:, 4, :, e:NEXP], me.to_broadcast([P, T, NEXP - e]),
                                ALU.is_gt))
                        step(tr(gt[:, 6, :, e:e + 1], gt[:, 5], AX.X, ALU.add))
                    step(nc.vector.tensor_scalar(gt[:, 6], gt[:, 6], 1.5, None, ALU.is_lt))
                    step(tr(gv[:, 2], gt[:, 4], AX.X, ALU.max))
                    tt(gt[:, 2], gt[:, 4], over_e(gv[:, 2]), ALU.subtract).then_inc(s_["router_in"], 1)
                    dve.wait_ge(s_["router_exp"], 2)
                    step(tt(gt[:, 5], gt[:, 3], gt[:, 6], ALU.mult))
                    step(tr(gv[:, 3], gt[:, 5], AX.X, ALU.add))
                    step(nc.vector.reciprocal(gv[:, 3], gv[:, 3]))
                    step(tt(gt[:, 7], gt[:, 5], over_e(gv[:, 3]), ALU.mult), (s_["comb"], 1))
                    src = full_a()
                    nc.vector.tensor_copy(combt[0:NEXP].rearrange("p t n -> p (t n)"), src[0:NEXP]).then_inc(*Af.one())
                    for t in range(T):
                        src = full_a()
                        nc.vector.tensor_tensor(hid[:, t], src, hid[:, t], ALU.add).then_inc(*Af.one())
                    for e in range(NEXP):
                        dve.wait_ge(*Af.now())
                        for t in range(T):
                            src = full_a()
                            nc.vector.scalar_tensor_tensor(hid[:, t], src, gt[:, 7, t, e:e + 1], hid[:, t],
                                                           ALU.mult, ALU.add).then_inc(*Af.one())
                    dve.wait_ge(*Af.now())
                    for t in range(T):
                        nc.vector.tensor_tensor(xt[:, t], xt[:, t], hid[:, t], ALU.add).then_inc(s_["seq_done"], 1)
                    assert Af.n == A_EXP + T * NEXP

        run(0, main=False, ssm=0)
        fresh()
        run(0, main=True, ssm=1, split=True)
        fresh()
        with nc.Fori(1, B - 1) as b:
            run(b, main=True, ssm=b + 1)
            fresh()
        run(B - 1, main=True, ssm=None)


def kernel(x, ctx_1024, L0_attn_w_qkv, L0_attn_b_qkv, L0_attn_w_out, L0_attn_b_out, L0_xattn_in_proj_w,
           L0_xattn_conv_w, L0_xattn_conv_b, L0_xattn_x_proj_w, L0_xattn_dt_proj_w, L0_xattn_dt_proj_b,
           L0_xattn_A_log, L0_xattn_D, L0_ffn_wq, L0_ffn_bq, L0_ffn_wk, L0_ffn_bk, L0_ffn_wv, L0_ffn_bv,
           L0_ffn_wo, L0_ffn_bo, L0_ffn_ln1_w, L0_ffn_ln1_b, L0_ffn_ln2_w, L0_ffn_ln2_b, L0_ffn_w_gate,
           L0_ffn_we1, L0_ffn_be1, L0_ffn_we2, L0_ffn_be2):
    import numpy as np
    import concourse.bacc as bacc
    from concourse.bass_utils import run_bass_kernel_spmd

    def tiles(w):
        w = np.asarray(w)
        return np.ascontiguousarray(w.reshape(-1, P, w.shape[1]).transpose(1, 0, 2).reshape(P, -1))

    def cols(v):
        return np.asarray(v).reshape(-1, P).T

    bq = np.asarray(L0_attn_b_qkv)
    fields = {
        "bq1": cols(bq[:D]), "bk1": cols(bq[D:D + P]), "conv_w": tiles(L0_xattn_conv_w),
        "conv_b": cols(L0_xattn_conv_b), "dt_b": cols(L0_xattn_dt_proj_b), "a_log": tiles(L0_xattn_A_log),
        "ssm_d": cols(L0_xattn_D), "ln1_w": cols(L0_ffn_ln1_w), "ln1_b": cols(L0_ffn_ln1_b),
        "ln2_w": cols(L0_ffn_ln2_w), "ln2_b": cols(L0_ffn_ln2_b), "bq2": cols(L0_ffn_bq),
        "bk2": cols(L0_ffn_bk), "bv2": cols(L0_ffn_bv), "be1": cols(np.asarray(L0_ffn_be1).reshape(-1)),
        "eps": np.full((P, 1), 1e-5, np.float32), "one": np.ones((P, 1), np.float32),
        "w_gate": tiles(L0_ffn_w_gate),
    }
    assert list(fields) == list(PCOLS)
    wq, wk, wv, wo = (np.asarray(w) for w in (L0_ffn_wq, L0_ffn_wk, L0_ffn_wv, L0_ffn_wo))
    chunks = [tiles(wv[:, D * g:D * (g + 1)]) for g in range(H2 // G2)]
    for p in range(H2 // 2):
        a, b = 2 * p * HD2, (2 * p + 1) * HD2
        chunks.append(tiles(np.concatenate([wq[:, a:a + HD2], wk[:, a:a + HD2],
                                            wq[:, b:b + HD2], wk[:, b:b + HD2]], axis=1)))
    chunks += [tiles(wo[D * g:D * (g + 1)]) for g in range(H2 // G2)]
    chunks += [tiles(w) for w in np.asarray(L0_ffn_we1)] + [tiles(w) for w in np.asarray(L0_ffn_we2)]

    freq = (np.float32(1.0) / np.float32(10000.0) ** (np.arange(0, HD2, 2, dtype=np.float32) / np.float32(HD2)))
    angle = freq[:, None].astype(np.float32) * np.arange(S, dtype=np.float32)[None, :]
    angle = np.concatenate([angle, angle], axis=0)
    sign = np.where(np.arange(P) < P // 2, 1.0, -1.0).astype(np.float32)[:, None]
    rope = np.stack([np.cos(angle), np.sin(angle) * sign], axis=1).astype(np.float32)
    causal = np.triu(np.full((P, P), -1e30, np.float32), 1)

    arrays = {
        "x": np.ascontiguousarray(np.asarray(x).reshape(B, T, P, D).transpose(0, 2, 1, 3)),
        "ctx_t": np.ascontiguousarray(np.asarray(ctx_1024).transpose(0, 2, 1).reshape(B, DM // P, P, S)
                                      .transpose(0, 2, 1, 3)),
        "w_qkv": tiles(np.asarray(L0_attn_w_qkv).T),
        "w_out": tiles(np.asarray(L0_attn_w_out).T),
        "in_w": tiles(np.asarray(L0_xattn_in_proj_w).T),
        "xp_w": tiles(np.asarray(L0_xattn_x_proj_w).T).reshape(P, EC, DR + 2 * DS),
        "dt_w": np.ascontiguousarray(np.asarray(L0_xattn_dt_proj_w).T),
        "params": np.ascontiguousarray(np.concatenate(list(fields.values()), axis=1)),
        "bias_rows": np.concatenate([np.asarray(L0_attn_b_out), np.asarray(L0_ffn_bo), bq[D + P:]])[None, :],
        "be2": np.asarray(L0_ffn_be2),
        "chunks": np.stack(chunks),
        "ident": np.eye(P, dtype=np.float32),
        "causal": causal,
        "rope": rope,
    }
    nc = bacc.Bacc("TRN2", target_bir_lowering=False, num_devices=1)
    aps = {n: nc.dram_tensor(n, a.shape, mybir.dt.from_np(a.dtype), kind="ExternalInput").ap()
           for n, a in arrays.items()}
    aps["out"] = nc.dram_tensor("out", (B, P, T, D), F32, kind="ExternalOutput").ap()
    build(nc, **aps)
    r = run_bass_kernel_spmd(nc, [arrays], core_ids=[0])
    return r.results[0]["out"].transpose(0, 2, 1, 3).reshape(B, S, D)
```

```python
from contextlib import ExitStack

import concourse.bass as bass
from concourse import mybir

F32 = mybir.dt.float32
BF16 = mybir.dt.bfloat16
ACT = mybir.ActivationFunctionType
ALU = mybir.AluOpType
AX = mybir.AxisListType

P = 128
B, S, D = 4, 512, 512
T = S // P
KC = D // P
H1, G1, HD1 = 32, 8, 16
R1 = H1 // G1
HPC = P // HD1
QC = H1 // HPC
NS = 6
QPARTS = (0, 0, 1, 1, 0, 2)
KPARTS = (0, 1, 0, 1, 2, 0)
NQ = 3
KM = NS * HD1
SCALE1 = 1.0 / float(HD1) ** 0.5
DM, DI, DS, DR, DC = 256, 512, 16, 16, 4
EC = DI // P
EPS = 1e-5
NE = 2
NU = EC // NE
H2, HD2 = 16, 128
G2 = 4
SCALE2 = 1.0 / float(HD2) ** 0.5
NEXP = 4
CH = 2048
NRAW, NPAIR = 2, 3
NRING = NRAW + NPAIR

PCOLS, NPAR = {}, 0
for _name, _w in (("bq1", QC), ("bk1", 1), ("conv_w", EC * DC), ("conv_b", EC), ("dt_b", EC),
                  ("a_log", EC * DS), ("ssm_d", EC), ("ln1_w", KC), ("ln1_b", KC), ("ln2_w", KC),
                  ("ln2_b", KC), ("bq2", H2), ("bk2", H2), ("bv2", H2), ("be1", NEXP * KC),
                  ("one", 1), ("w_gate", KC * NEXP)):
    PCOLS[_name] = NPAR
    NPAR += _w


def chunk_order():
    out = []
    for s in range(H2 + 3):
        if s < H2 and s % G2 == 0:
            out.append(("v", s // G2, s))
        if s < H2 and s % 2 == 0:
            out.append(("qk", s // 2, s))
        if s > G2 and s % G2 == 2:
            out.append(("wo", s // G2 - 1, s))
    out.append(("w1", 0, H2 + 2))
    for e in range(NEXP):
        if e + 1 < NEXP:
            out.append(("w1", e + 1, H2 + 2 + e))
        out.append(("w2", e, H2 + 2 + e))
    return out


CHUNKS = chunk_order()
CHUNK_AT = {(k, i): n for n, (k, i, _) in enumerate(CHUNKS)}
CHUNK_ROW = {"v": 0, "qk": 4, "wo": 12, "w1": 16, "w2": 20}
SPLIT_IN_STEP = {s: [n for n, c in enumerate(CHUNKS)
                     if n >= NPAIR and c[0] in ("v", "qk", "wo") and min(c[2], H2 + 1) - 2 == s]
                 for s in range(H2 + 2)}
_moe = [n for n, c in enumerate(CHUNKS) if c[0] in ("w1", "w2")]
SPLIT_IN_STEP[H2] = [_moe[0]]
SPLIT_IN_STEP[H2 + 1] = _moe[1:3]
SPLIT_IN_EXPERT = {0: [_moe[3]], 1: [_moe[4]], 2: _moe[5:7], 3: [_moe[7]]}

A_HT1, A_V1, A_MAX = 0, KC, KC + 1
A_CH = HPC * T + 1
JC, JLAG = 2 * T, 2
JROWS = HPC * T // JC
JCOLS = JC + JLAG
A_OUT1 = A_MAX + QC * A_CH
A_GATE = A_OUT1 + T
A_HT2 = A_GATE + T


def ring_a_units(s):
    out = []
    if s < H2 and s % G2 == 0:
        out += [("v", s // G2, t) for t in range(T)]
    if s < H2:
        out += [("qk", s, w) for w in range(2)]
    for t in range(T):
        if 2 <= s < H2 + 2:
            out.append(("turn", s - 2, t))
        if s > G2 and s % G2 == 2:
            out.append(("wo", s // G2 - 1, t))
    return out


A_AT, _n = {}, A_HT2 + KC
for _s in range(H2 + 3):
    for _u in ring_a_units(_s):
        A_AT[_u] = _n
        _n += 1
A_HT3 = _n
A_LOGITS = A_HT3 + KC
A_COMB = A_LOGITS + 1
A_BE2 = A_COMB + 1
A_EXP = A_BE2 + T

NUNIT = NU * DS
SCAN_ALONE = [list(range(NU * _s, NU * (_s + 1))) for _s in range(DS)]
SCAN_BESIDE, _n = [], 0
for _s in range(H2 + 2 + NEXP):
    _k = 2 if _s >= H2 + 2 or len(ring_a_units(_s)) > T + 2 else 1
    _k = min(_k, NUNIT - _n - (2 * NEXP if _s < H2 + 2 else 0))
    SCAN_BESIDE.append(list(range(_n, _n + _k)))
    _n += _k
assert _n == NUNIT

SEMS = """const_in x_in be2_in raw_in0 raw_in1 stk_out stk_in0 stk_in1 stk_in2 kst_in m_in0 m_in1 ot_in ctx_in dtw_in xd_out b_in0 b_in1 c_in0 c_in1 y_out
 a_full a_free b_full b_free o_full o_free_norm o_free_head
 ln_stats ln_guess ln_rows ht_hi ht_lo bias_in ch_hi ch_lo pair_out0 pair_out1 pair_out2 pair_in0 pair_in1 pair_in2 pair_in3 pair_in4
 q_part q_rest q_parts m_parts ones pv1 on_hi on_lo z_silu gated
 cx_hi cx_lo pad_zero conv_done u_done sp_log delta_done du_done y_init
 da_done bx_done prod_done y_acc v_hi rope_f rope_hi rope_lo nmax2 exp2 p_norm pt_hi o_hi o_lo
 router_in router_exp comb hm_hi hm_lo x_added dve_own act_own""".split()


class Count:

    def __init__(self, sem):
        self.sem, self.n = sem, 0

    def one(self):
        self.n += 1
        return self.sem, 1

    def now(self):
        return self.sem, self.n


def build(nc, x, ctx_t, w_qkv, w_out, in_w, xp_w, dt_w, params, bias_rows, be2, chunks, ident, causal,
          rope, out):
    with ExitStack() as ctx:
        def sb(name, shape, dt=F32):
            return ctx.enter_context(nc.sbuf_tensor(name, shape, dt))

        s_ = {n: ctx.enter_context(nc.semaphore(n)) for n in SEMS}
        lo_sem = min(s.num for s in s_.values())
        hi_sem = max(s.num for s in s_.values())
        assert hi_sem - lo_sem + 1 == len(SEMS)

        stk_d = nc.dram_tensor("stk_d", (QC + 1, P, 3, S), BF16, kind="Internal").ap()
        pair_d = nc.dram_tensor("pair_d", (len(CHUNKS), P, 2, CH), BF16, kind="Internal").ap()
        xd_d = nc.dram_tensor("xd_d", (2 * DS, S), F32, kind="Internal").ap()

        identf = sb("identf", [P, P])
        identb = sb("identb", [P, P], BF16)
        causb = sb("causb", [P, P], BF16)
        par = sb("par", [P, NPAR])
        ropet = sb("ropet", [P, 2, S])
        brow = sb("brow", [P, 2 * D + P])
        xpw = sb("xpw", [P, EC, DR + 2 * DS])
        nega = sb("nega", [P, EC * DS])
        wqkv = sb("wqkv", [P, 2, KC, 768], BF16)
        wout = sb("wout", [P, 2, KC, D], BF16)
        inw = sb("inw", [P, 2, DM // P, DI], BF16)
        pair = sb("pair", [P, NRING, 2, CH], BF16)
        raw = pair[:, NPAIR:NRING].rearrange("p n q c -> p (n q c)").bitcast(F32).rearrange(
            "p (n c) -> p n c", n=NRAW)

        xt = sb("xt", [P, T, D])
        hid = sb("hid", [P, T, D])
        ys = sb("ys", [P, EC, S])
        ht = sb("ht", [P, 2, KC, S], BF16)
        bst = sb("bst", [P, T, 6])
        bmv = sb("bmv", [P, T, 2])
        rs = sb("rs", [P, 2, T])
        vv = sb("vv", [P, 2, T])
        ra = sb("ra", [P, 2, T])
        rn = sb("rn", [P, 2, T])
        nmx = sb("nmx", [P, T])
        nbs = sb("nbs", [P, T])
        sm = sb("sm", [P, 2, T])
        rc = sb("rc", [P, T])
        nm1 = sb("nm1", [P, 2, HPC * T])
        gt = sb("gt", [P, 8, T, NEXP])
        gv = sb("gv", [P, 4, T])

        REGION = 25088
        region = sb("region", [P, REGION])

        def carve(at, shape, dt=F32):
            n = 1
            for k in shape:
                n *= k
            words = n if dt == F32 else n // 2
            assert at + words <= REGION, at + words
            a = region[:, at:at + words]
            if dt != F32:
                a = a.bitcast(dt)
            if len(shape) > 1:
                names = "abcd"[:len(shape)]
                a = a.rearrange(f"p ({' '.join(names)}) -> p {' '.join(names)}",
                                **{c: k for c, k in zip(names[1:], shape[1:])})
            return a, at + words

        pf, at = carve(0, [T, S])
        xn = pf
        vp0 = at
        vp, at = carve(at, [2, 2, T, D], BF16)
        qr, at = carve(at, [2, 2, 2, S], BF16)
        rp0 = at
        rp, at = carve(at, [2, S])
        rtmp, at = carve(at, [S])
        pt0 = at
        pt, at = carve(at, [2, T, S], BF16)
        of, at = carve(at, [S])
        op0 = at
        op, at = carve(at, [2, G2, S], BF16)
        dl, at = carve(at, [EC, S])
        du, at = carve(at, [EC, S])
        us, _ = carve(op0, [EC, S])
        bx, at = carve(at, [2, NE, S])
        da, at = carve(at, [2, NE, S])
        bb, at = carve(at, [2, S])
        cb, at = carve(at, [2, S])
        dg0 = at
        dg, _ = carve(at, [T, P])
        xd, at = carve(at, [S])
        cxf, at = carve(vp0, [DM // P, S])
        cx, at = carve(at, [2, DM // P, S], BF16)
        xpad, at = carve(at, [2, S + 4])
        dtw, _ = carve(dg0 - DI, [DI])
        acc, _ = carve(rp0, [2, S])
        spt, _ = carve(vp0 + 3584, [2, 3, S])
        h1f, _ = carve(pt0, [KC, S])
        hm, at = carve(vp0, [2, 2, KC, S], BF16)
        gf, _ = carve(at, [KC, S])
        h2f = gf
        combt, at = carve(pt0, [T, P])
        be2s, _ = carve(at, [D])
        qf, at = carve(T * S, [2, S])
        qres, at = carve(at, [2, S])
        qpt, at = carve(at, [2, 3, S], BF16)
        qst, at = carve(at, [NQ - 1, HPC, S], BF16)
        kst, at = carve(at, [G1, S], BF16)
        vaug, at = carve(at, [T, G1, 2 * HD1])
        pt1, at = carve(at, [2, R1, S])
        on, at = carve(at, [2, S])
        rec, at = carve(at, [2, S])
        onp, at = carve(at, [G1, 2, S], BF16)
        ot, _ = carve(0, [2, KC, S], BF16)
        mf, at = carve(at, [2, P])
        mpt, at = carve(at, [2, 3, P], BF16)

        qst2 = hid[:].rearrange("p t d -> p (t d)").bitcast(BF16).rearrange("p (h n) -> p h n", n=S)

        def qstack(c):
            return qst[:, c % NQ] if c % NQ < NQ - 1 else qst2

        PS = ctx.enter_context(nc.psum_tensor("PS", [P, 8, 512], F32))

        def bank_a_at(n):
            return PS[:, n % 2] if n < A_HT2 else PS[:, (0, 1, 6)[(n - A_HT2) % 3]]

        def a_before(n):
            return n - 1 if n < A_HT2 else max(A_HT2, n - 2)

        def bank_b_at(n):
            return PS[:, 2 + 2 * (n % 2):4 + 2 * (n % 2)]

        def col(name, i, n=1):
            a = PCOLS[name] + i
            return par[:, a:a + n]

        def pe3(dst, l, r, start, stop):
            nc.tensor.matmul(dst, l(0), r(0), start=start, stop=False)
            nc.tensor.matmul(dst, l(0), r(1), start=False, stop=False)
            return nc.tensor.matmul(dst, l(1), r(0), start=False, stop=stop)

        loads = [(identf[:], ident), (par[:], params), (ropet[:], rope), (xpw[:], xp_w),
                 (brow[:], bias_rows.to_broadcast([P, 2 * D + P]))]
        stages, at = [], 0
        for src, dst in ((w_qkv, wqkv), (w_out, wout), (in_w, inw)):
            n = src.shape[1]
            stages.append((region[:, at:at + n], src, dst[:, 0].rearrange("p k n -> p (k n)"),
                           dst[:, 1].rearrange("p k n -> p (k n)")))
            at += n
        causf = region[:, at:at + P]
        loads += [(st, src) for st, src, _, _ in stages] + [(causf, causal)]

        with nc.Block() as block:
            @block.sync
            def _(sp):
                for dst, src in loads:
                    sp.dma_start(dst, src).then_inc(s_["const_in"], 16)

            @block.scalar
            def _(act):
                act.wait_ge(s_["const_in"], 16 * len(loads))
                for st, _, hi, _ in stages:
                    nc.scalar.activation(hi, st, ACT.Copy).then_inc(s_["act_own"], 1)
                nc.scalar.activation(identb[:], identf[:], ACT.Copy).then_inc(s_["act_own"], 1)
                nc.scalar.activation(causb[:], causf, ACT.Copy).then_inc(s_["act_own"], 1)
                nc.scalar.activation(nega[:], col("a_log", 0, EC * DS), ACT.Exp).then_inc(s_["act_own"], 1)

            @block.vector
            def _(dve):
                for i, (st, _, hi, lo) in enumerate(stages):
                    dve.wait_ge(s_["act_own"], i + 1)
                    nc.vector.tensor_tensor(lo, st, hi, ALU.subtract).then_inc(s_["dve_own"], 1)
                dve.wait_ge(s_["act_own"], len(stages) + 3)
                nc.vector.tensor_scalar(nega[:], nega[:], -1.0, None, ALU.mult).then_inc(s_["dve_own"], 1)

        def fresh():
            nc.all_engine_barrier()
            nc.gpsimd.sem_clear(range(lo_sem, hi_sem + 1))
            nc.all_engine_barrier()

        fresh()

        def run(b, main, ssm, split=False):
            ring = NPAIR if split else NRING
            scans = [] if ssm is None else SCAN_BESIDE if main else SCAN_ALONE
            scans = scans + [[]] * (H2 + 2 + NEXP - len(scans))
            after = ssm
            STATS_GATE, STATS_TWICE, STATS_MOE, STATS_AFTER = 1, 3, 4, 5 if main else 1
            ROWS_GATE, ROWS_HID, ROWS_XN, ROWS_MOE = T, 2 * T, 3 * T, 4 * T
            B_SC1 = (QC + 1) if main else 0
            B_SSM = B_SC1 + (2 * T * G1 if main else 0)
            B_SC2 = B_SSM + (2 * EC + 1 if ssm is not None else 0)
            B_EXP = B_SC2 + 2 * H2

            with nc.Block() as block:
                def chunk_free(eng, n):
                    kind, i, _ = CHUNKS[n]
                    if kind == "v":
                        eng.wait_ge(s_["a_full"], A_AT["v", i, T - 1] + 1)
                    elif kind == "qk":
                        eng.wait_ge(s_["a_full"], A_AT["qk", 2 * i + 1, 1] + 1)
                    elif kind == "wo":
                        eng.wait_ge(s_["a_full"], A_AT["wo", i, T - 1] + 1)
                    elif kind == "w1":
                        eng.wait_ge(s_["b_full"], B_EXP + KC * (i + 1))
                    else:
                        eng.wait_ge(s_["a_full"], A_EXP + T * (i + 1))

                def chunk_there(eng, n):
                    if split:
                        eng.wait_ge(s_["ch_lo"], n + 1)
                    else:
                        eng.wait_ge(s_[f"pair_in{n % NRING}"], 16 * (n // NRING + 1))

                @block.sync
                def _(sp):
                    def store_pair(n):
                        sp.dma_start(pair_d[n], pair[:, n % NPAIR]).then_inc(s_[f"pair_out{n % NPAIR}"], 16)

                    def load_chunk(n):
                        if not split:
                            if n >= NRING:
                                chunk_free(sp, n - NRING)
                            sp.dma_start(pair[:, n % NRING], pair_d[n]).then_inc(s_[f"pair_in{n % NRING}"], 16)
                            return
                        if n >= NRAW:
                            sp.wait_ge(s_["ch_lo"], n - NRAW + 1)
                            store_pair(n - NRAW)
                        kind, i, _ = CHUNKS[n]
                        sp.dma_start(raw[:, n % NRAW], chunks[CHUNK_ROW[kind] + i]).then_inc(s_[f"raw_in{n % 2}"], 16)

                    def stack_out(i):
                        sp.wait_ge(s_["q_parts"], i + 1)
                        sp.dma_start(stk_d[i], qpt[:, i % 2]).then_inc(s_["stk_out"], 16)
                        sp.wait_ge(s_["stk_out"], 16 * (i + 1))

                    def stack_in(i):
                        if i > NQ:
                            sp.wait_ge(s_["pv1"], JC * (i - NQ))
                        for j in range(NS):
                            part = QPARTS[j] if i else KPARTS[j]
                            src = stk_d[i, :, part].rearrange("(h d) n -> d h n", d=HD1)
                            dst = qstack(i - 1)[HD1 * j:HD1 * (j + 1)] if i else kst[HD1 * j:HD1 * (j + 1)]
                            sp.dma_start(dst, src).then_inc(s_[f"stk_in{(i - 1) % NQ}" if i else "kst_in"], 16)

                    def maxima(c):
                        sp.wait_ge(s_["m_parts"], c + 1)
                        for j in range(3):
                            sp.dma_start(qstack(c)[KM + j:KM + j + 1].rearrange("o h (t n) -> o (h t) n", n=P),
                                         mpt[0:HPC * T, c % 2, j]).then_inc(s_[f"m_in{c % 2}"], 16)

                    if not main:
                        sp.dma_start(xt[:], x[after]).then_inc(s_["x_in"], 16)
                    if main:
                        for n in range(NRAW if split else NRING):
                            load_chunk(n)
                        for i in range(QC + 1):
                            stack_out(i)
                            if i <= NQ:
                                stack_in(i)
                    if ssm is not None:
                        sp.dma_start(cxf, ctx_t[ssm]).then_inc(s_["ctx_in"], 16)
                        sp.dma_start(dtw[0:DR], dt_w).then_inc(s_["dtw_in"], 16)
                    if main:
                        for n in range(NRAW, NPAIR):
                            if split:
                                load_chunk(n)
                        for c in range(QC):
                            maxima(c)
                            if c and c + NQ < QC + 1:
                                stack_in(c + NQ)
                        sp.wait_ge(s_["on_lo"], G1)
                        for j in range(R1):
                            for odd in range(2):
                                r0 = HD1 * (R1 * odd + j)
                                for part in range(2):
                                    sp.dma_start(ot[r0:r0 + HD1, part],
                                                 onp[32 * j:32 * j + HD1, odd::2, part]).then_inc(s_["ot_in"], 16)
                    if ssm is not None:
                        sp.wait_ge(s_["b_free"], B_SSM + EC + 1)
                        sp.dma_start(xd_d, xd[DR:DR + 2 * DS]).then_inc(s_["xd_out"], 16)
                    if main:
                        for n in range(ring, len(CHUNKS)):
                            load_chunk(n)
                            if n - ring == CHUNK_AT["wo", 3]:
                                sp.wait_ge(s_["a_free"], A_HT3)
                                sp.dma_start(be2s[0:NEXP], be2).then_inc(s_["be2_in"], 16)
                            if n - ring == CHUNK_AT["w1", 0] and after is not None:
                                sp.wait_ge(s_["x_added"], T)
                                sp.dma_start(xt[:], x[after]).then_inc(s_["x_in"], 16)
                        if split:
                            sp.wait_ge(s_["ch_lo"], len(CHUNKS))
                            for n in range(len(CHUNKS) - NRAW, len(CHUNKS)):
                                store_pair(n)
                            for k in range(NPAIR):
                                sp.wait_ge(s_[f"pair_out{k}"], 16 * len(range(k, len(CHUNKS), NPAIR)))
                        for t in range(T):
                            sp.wait_ge(s_["a_free"], A_EXP + T * (NEXP - 1) + t + 1)
                            sp.dma_start(out[b, :, t], hid[:, t]).then_inc(s_["y_out"], 16)
                        sp.wait_ge(s_["y_out"], 16 * T)

                @block.tensor
                def _(pe):
                    A, Bn = Count(s_["a_full"]), Count(s_["b_full"])

                    def bank_a():
                        if A.n >= 2:
                            pe.wait_ge(s_["a_free"], a_before(A.n))
                        return bank_a_at(A.n)

                    def bank_b():
                        if Bn.n >= 2:
                            pe.wait_ge(s_["b_free"], Bn.n - 1)
                        return bank_b_at(Bn.n)

                    def to_features(rows):
                        for k in range(KC):
                            dst = bank_a()
                            if rows:
                                pe.wait_ge(s_["ln_rows"], rows)
                            for t in range(T):
                                last = nc.tensor.transpose(dst[:, P * t:P * (t + 1)],
                                                           xn[:, t, P * k:P * (k + 1)], identf[:])
                            last.then_inc(*A.one())

                    def feat(k, t=None):
                        c = slice(0, S) if t is None else slice(P * t, P * (t + 1))
                        return lambda part: ht[:, part, k, c]

                    if main:
                        to_features(0)
                        pe.wait_ge(s_["a_free"], A_HT1 + KC)
                        for m in [QC] + list(range(QC)):
                            dst = bank_b()[:, 0]
                            for k in range(KC):
                                last = pe3(dst, lambda q: wqkv[:, q, k, P * m:P * (m + 1)], feat(k),
                                           k == 0, k == KC - 1)
                            last.then_inc(*Bn.one())
                            if m == QC:
                                dst = bank_a()
                                for t in range(T):
                                    for k in range(KC):
                                        last = pe3(dst[:, P * t:P * (t + 1)], feat(k, t),
                                                   lambda q: wqkv[:, q, k, 640:768], k == 0, k == KC - 1)
                                last.then_inc(*A.one())

                        def score_rows(i):
                            c, h, t = i // (HPC * T), i // T % HPC, i % T
                            dst = bank_a()
                            if i % (HPC * T) == 0:
                                pe.wait_ge(s_[f"stk_in{c % NQ}"], 16 * NS * (c // NQ + 1))
                            nc.tensor.matmul(dst, qstack(c)[0:KM, h, P * t:P * (t + 1)],
                                             kst[0:KM, (HPC * c + h) // R1],
                                             start=True, stop=True).then_inc(*A.one())

                        def score_cols(n, r2):
                            g, kt = n // T, n % T
                            c = R1 * g // HPC
                            dst = bank_b()
                            if n % JC == 0 and r2 == 0:
                                pe.wait_ge(s_[f"m_in{c % 2}"], 48 * (c // 2 + 1))
                            for r in range(2):
                                last = nc.tensor.matmul(
                                    dst[:, r], kst[0:KM + 3, g, P * kt:P * (kt + 1)],
                                    qstack(c)[0:KM + 3, R1 * g + 2 * r2 + r - HPC * c],
                                    start=True, stop=True)
                            last.then_inc(*Bn.one())

                        def key_sums(n):
                            g, kt = n // T, n % T
                            if kt == 0 and g >= 2:
                                pe.wait_ge(s_["o_free_norm"], g - 1)
                            pe.wait_ge(s_["b_free"], B_SC1 + 2 * n + 2)
                            for r in range(R1):
                                last = nc.tensor.matmul(PS[32 * r:32 * r + 32, 6 + g % 2], vaug[:, kt, g],
                                                        pt1[:, kt % 2, r], start=kt == 0, stop=kt == T - 1)
                            last.then_inc(s_["pv1"], 1)

                        pe.wait_ge(s_["kst_in"], 16 * NS)
                        pe.wait_ge(s_["a_free"], A_V1 + 1)
                        pe.wait_ge(s_["ones"], 2)
                        for j in range(JCOLS + T * G1 + 1):
                            n = j - JCOLS
                            rows = list(range(JROWS * j, JROWS * (j + 1))) if j < JC * QC else []
                            turn_maxima = j % JC == 0 and 0 < j <= JC * QC
                            for r2 in range(2):
                                if rows and not turn_maxima:
                                    score_rows(rows.pop(0))
                                if 0 <= n < T * G1:
                                    score_cols(n, r2)
                            if turn_maxima:
                                dst = bank_a()
                                pe.wait_ge(s_["a_free"], A.n)
                                nc.tensor.transpose(dst[0:HPC * T, 0:P], nm1[:, (j // JC - 1) % 2],
                                                    identf[:]).then_inc(*A.one())
                            while len(rows) > 1:
                                score_rows(rows.pop(0))
                            if 0 <= n - 1 < T * G1:
                                key_sums(n - 1)
                            if rows:
                                score_rows(rows.pop(0))
                    def in_project():
                        pe.wait_ge(s_["cx_lo"], 1)
                        for e in range(EC):
                            dst = bank_b()[:, 0]
                            for k in range(DM // P):
                                last = pe3(dst, lambda q: inw[:, q, k, P * e:P * (e + 1)],
                                           lambda q: cx[:, q, k], k == 0, k == DM // P - 1)
                            last.then_inc(*Bn.one())

                    def x_project():
                        dst = bank_b()[:, 0]
                        pe.wait_ge(s_["u_done"], EC)
                        for e in range(EC):
                            last = nc.tensor.matmul(dst[0:DR + 2 * DS], xpw[:, e], us[:, e],
                                                    start=e == 0, stop=e == EC - 1)
                        last.then_inc(*Bn.one())

                    def dt_project(e):
                        dst = bank_b()[:, 0]
                        pe.wait_ge(s_["b_free"], B_SSM + EC + 1)
                        pe.wait_ge(s_["dtw_in"], 16)
                        nc.tensor.matmul(dst, dtw[0:DR, P * e:P * (e + 1)], xd[0:DR],
                                         start=True, stop=True).then_inc(*Bn.one())

                    if ssm is not None:
                        in_project()
                        x_project()
                    if main:
                        for t in range(T):
                            dst = bank_a()
                            pe.wait_ge(s_["ot_in"], 16 * 4 * R1)
                            for k in range(KC):
                                last = pe3(dst, lambda q: ot[:, q, k, P * t:P * (t + 1)],
                                           lambda q: wout[:, q, k], k == 0, k == KC - 1)
                            last.then_inc(*A.one())
                    if ssm is not None:
                        for e in range(EC - 1):
                            dt_project(e)
                    if main:
                        for t in range(T):
                            dst = bank_a()
                            pe.wait_ge(s_["gated"], EC)
                            for e in range(EC):
                                last = nc.tensor.transpose(dst[:, P * e:P * (e + 1)],
                                                           ys[:, e, P * t:P * (t + 1)], identf[:])
                            last.then_inc(*A.one())
                    if ssm is not None:
                        dt_project(EC - 1)
                    if not main:
                        return
                    to_features(ROWS_XN)

                    def project(s):
                        g = s // G2
                        if s == 0:
                            pe.wait_ge(s_["ht_lo"], KC)
                        if s % G2 == 0:
                            n = CHUNK_AT["v", g]
                            chunk_there(pe, n)
                            for t in range(T):
                                dst = bank_a()
                                for k in range(KC):
                                    last = pe3(dst, feat(k, t), lambda q: pair[:, n % ring, q, D * k:D * (k + 1)],
                                               k == 0, k == KC - 1)
                                last.then_inc(*A.one())
                        n = CHUNK_AT["qk", s // 2]
                        chunk_there(pe, n)
                        for w in range(2):
                            dst = bank_a()
                            o = P * (2 * (s % 2) + w)
                            for k in range(KC):
                                last = pe3(dst, lambda q: pair[:, n % ring, q, D * k + o:D * k + o + P],
                                           feat(k), k == 0, k == KC - 1)
                            last.then_inc(*A.one())

                    def turn(h, kt):
                        pe.wait_ge(s_["p_norm"], h + 1)
                        dst = bank_a()
                        for t in range(kt, T):
                            last = nc.tensor.matmul(dst[:, P * t:P * (t + 1)], pf[:, t, P * kt:P * (kt + 1)],
                                                    dg[:, t], start=True, stop=True)
                        last.then_inc(*A.one())

                    def scores(h):
                        pe.wait_ge(s_["rope_lo"], 2 * (h + 1))
                        for u in range(2):
                            dst = bank_b()
                            for j in range(2):
                                t = 2 * u + j
                                pe3(dst[:, j, 0:P * (t + 1)], lambda q: qr[:, h % 2, 0, q, P * t:P * (t + 1)],
                                    lambda q: qr[:, h % 2, 1, q, 0:P * (t + 1)], True, False)
                                last = nc.tensor.matmul(dst[:, j, P * t:P * (t + 1)], identb[:], causb[:],
                                                        start=False, stop=True)
                            last.then_inc(*Bn.one())

                    def values(h):
                        if h == 0:
                            pe.wait_ge(s_["o_free_norm"], G1)
                        else:
                            pe.wait_ge(s_["o_free_head"], h)
                        g, hh = h // G2, h % G2
                        pe.wait_ge(s_["a_free"], A_AT["v", g, T - 1] + 1)
                        for kt in range(T):
                            pe.wait_ge(s_["a_free"], A_AT["turn", h, kt] + 1)
                            last = pe3(PS[:, 7, P * kt:S],
                                       lambda q: vp[:, g % 2, q, kt, P * hh:P * (hh + 1)],
                                       lambda q: pt[:, q, kt, P * kt:S], kt == 0, kt == T - 1)
                        last.then_inc(s_["o_full"], 1)

                    def project_out(g, t):
                        n = CHUNK_AT["wo", g]
                        chunk_there(pe, n)
                        pe.wait_ge(s_["o_lo"], G2 * (g + 1))
                        dst = bank_a()
                        for h in range(G2):
                            last = pe3(dst, lambda q: op[:, q, h, P * t:P * (t + 1)],
                                       lambda q: pair[:, n % ring, q, D * h:D * (h + 1)],
                                       h == 0, h == G2 - 1)
                        last.then_inc(*A.one())

                    for s in range(H2 + 3):
                        if s < H2:
                            project(s)
                        for t in range(T):
                            if 2 <= s < H2 + 2:
                                turn(s - 2, t)
                            if t == 0 and 1 <= s <= H2:
                                scores(s - 1)
                            if s > G2 and s % G2 == 2:
                                project_out(s // G2 - 1, t)
                        if 2 <= s < H2 + 2:
                            values(s - 2)

                    to_features(ROWS_MOE)
                    dst = bank_a()
                    pe.wait_ge(s_["a_free"], A_HT3 + KC)
                    for t in range(T):
                        for k in range(KC):
                            last = nc.tensor.matmul(dst[:, NEXP * t:NEXP * (t + 1)],
                                                    h2f[:, k, P * t:P * (t + 1)], col("w_gate", NEXP * k, NEXP),
                                                    start=k == 0, stop=k == KC - 1)
                    last.then_inc(*A.one())

                    def expert_in(e):
                        n = CHUNK_AT["w1", e]
                        chunk_there(pe, n)
                        pe.wait_ge(s_["ht_lo"], 2 * KC)
                        for i in range(KC):
                            dst = bank_b()[:, 0]
                            for k in range(KC):
                                last = pe3(dst, lambda q: pair[:, n % ring, q, D * k + P * i:D * k + P * (i + 1)],
                                           feat(k), k == 0, k == KC - 1)
                            last.then_inc(*Bn.one())

                    def expert_out(e):
                        n = CHUNK_AT["w2", e]
                        chunk_there(pe, n)
                        pe.wait_ge(s_["hm_lo"], KC * (e + 1))
                        for t in range(T):
                            dst = bank_a()
                            for i in range(KC):
                                last = pe3(dst, lambda q: hm[:, e % 2, q, i, P * t:P * (t + 1)],
                                           lambda q: pair[:, n % ring, q, D * i:D * (i + 1)],
                                           i == 0, i == KC - 1)
                            last.then_inc(*A.one())

                    expert_in(0)
                    dst = bank_a()
                    pe.wait_ge(s_["comb"], 1)
                    for t in range(T):
                        last = nc.tensor.transpose(dst[0:NEXP, P * t:P * (t + 1)], gt[:, 7, t], identf[:])
                    last.then_inc(*A.one())
                    pe.wait_ge(s_["be2_in"], 16)
                    for t in range(T):
                        dst = bank_a()
                        pe.wait_ge(s_["a_free"], A_COMB + 1)
                        nc.tensor.matmul(dst, combt[0:NEXP, t], be2s[0:NEXP], start=True,
                                         stop=True).then_inc(*A.one())
                    for e in range(NEXP):
                        if e + 1 < NEXP:
                            expert_in(e + 1)
                        expert_out(e)
                    assert A.n == A_EXP + T * NEXP and Bn.n == B_EXP + KC * NEXP

                @block.scalar
                def _(act):
                    Bf, own = Count(s_["b_free"]), Count(s_["act_own"])

                    def inv_root(stats, w=1):
                        act.wait_ge(s_["ln_stats"], stats)
                        nc.scalar.activation(ra[:, 0:w], vv[:, 0:w], ACT.Ln).then_inc(*own.one())
                        act.wait_ge(*own.now())
                        nc.scalar.activation(rs[:, 0:w], ra[:, 0:w], ACT.Exp, scale=-0.5).then_inc(s_["ln_guess"], 1)

                    def pad_in(e):
                        src = full_b()
                        if e < 2:
                            if main:
                                act.wait_ge(s_["stk_out"], 16 * (QC + 1))
                            act.wait_ge(s_["pad_zero"], 1)
                        nc.scalar.activation(xpad[:, e % 2, DC - 1:DC - 1 + S], src[:, 0],
                                             ACT.Copy).then_inc(*Bf.one())

                    def silu(e):
                        act.wait_ge(s_["conv_done"], e + 1)
                        nc.scalar.activation(us[:, e], acc[:, e % 2], ACT.Silu).then_inc(s_["u_done"], 1)

                    def softplus(e):
                        src = full_b()
                        k = e % 2
                        if e >= 2:
                            act.wait_ge(s_["delta_done"], e - 1)
                        nc.scalar.activation(spt[:, k, 0], src[:, 0], ACT.Abs, bias=col("dt_b", e)).then_inc(*own.one())
                        nc.scalar.activation(spt[:, k, 2], src[:, 0], ACT.Relu, bias=col("dt_b", e)).then_inc(*Bf.one())
                        act.wait_ge(*own.now())
                        nc.scalar.activation(spt[:, k, 1], spt[:, k, 0], ACT.Exp, scale=-1.0).then_inc(*own.one())
                        act.wait_ge(*own.now())
                        nc.scalar.activation(spt[:, k, 0], spt[:, k, 1], ACT.Ln, bias=col("one", 0)).then_inc(s_["sp_log"], 1)

                    def chunk_hi(n):
                        act.wait_ge(s_[f"raw_in{n % 2}"], 16 * (n // 2 + 1))
                        if n >= NPAIR:
                            chunk_free(act, n - NPAIR)
                            act.wait_ge(s_[f"pair_out{n % NPAIR}"], 16 * (n // NPAIR))
                        nc.scalar.activation(pair[:, n % NPAIR, 0], raw[:, n % NRAW], ACT.Copy).then_inc(s_["ch_hi"], 1)

                    def full_b():
                        act.wait_ge(s_["b_full"], Bf.n + 1)
                        return bank_b_at(Bf.n)

                    if not main:
                        inv_root(STATS_AFTER)
                        act.wait_ge(s_["ctx_in"], 16)
                        nc.scalar.activation(cx[:, 0], cxf, ACT.Copy).then_inc(s_["cx_hi"], 1)
                        pad_in(0)
                        pad_in(1)
                    if main:
                        for k in range(KC):
                            act.wait_ge(s_["a_full"], A_HT1 + k + 1)
                            nc.scalar.activation(ht[:, 0, k], bank_a_at(A_HT1 + k), ACT.Copy).then_inc(s_["ht_hi"], 1)
                        for i in range(QC + 1):
                            src = full_b()
                            if i >= 2:
                                act.wait_ge(s_["q_parts"], i - 1)
                                act.wait_ge(s_["stk_out"], 16 * (i - 1))
                            nc.scalar.activation(qf[:, i % 2], src[:, 0], ACT.Identity,
                                                 bias=col("bq1", i - 1) if i else col("bk1", 0)).then_inc(*Bf.one())
                            act.wait_ge(*Bf.now())
                            nc.scalar.activation(qpt[:, i % 2, 0], qf[:, i % 2], ACT.Copy).then_inc(s_["q_part"], 1)
                            act.wait_ge(s_["q_rest"], i + 1)
                            nc.scalar.activation(qpt[:, i % 2, 1], qres[:, i % 2], ACT.Copy).then_inc(s_["q_part"], 1)
                        for n in range(NPAIR if split else 0):
                            chunk_hi(n)

                        def out_hi(g):
                            act.wait_ge(s_["o_free_norm"], g + 1)
                            nc.scalar.activation(onp[:, g, 0], on[:, g % 2], ACT.Copy).then_inc(s_["on_hi"], 1)

                        for g in range(G1):
                            for kt in range(T):
                                for r2 in range(2):
                                    src = full_b()
                                    if r2 == 0 and T * g + kt >= 2:
                                        act.wait_ge(s_["pv1"], T * g + kt - 1)
                                    nc.scalar.activation(pt1[:, kt % 2, 2 * r2:2 * r2 + 2], src, ACT.Exp,
                                                         scale=SCALE1).then_inc(*Bf.one())
                                if kt == T - 1 and g:
                                    out_hi(g - 1)
                            if g == 0 and ssm is not None:
                                act.wait_ge(s_["ctx_in"], 16)
                                nc.scalar.activation(cx[:, 0], cxf, ACT.Copy).then_inc(s_["cx_hi"], 1)
                        if ssm is not None:
                            pad_in(0)
                            pad_in(1)
                        out_hi(G1 - 1)
                    if ssm is not None:
                        silu(0)
                        for e in range(2, EC):
                            pad_in(e)
                            silu(e - 1)
                        silu(EC - 1)
                        src = full_b()
                        nc.scalar.activation(xd[0:DR + 2 * DS], src[0:DR + 2 * DS, 0], ACT.Copy).then_inc(*Bf.one())
                        softplus(0)
                    if main:
                        inv_root(STATS_GATE)
                        act.wait_ge(s_["ln_rows"], ROWS_GATE)
                        nc.scalar.activation(xn, xn, ACT.Silu).then_inc(s_["z_silu"], 1)
                    if ssm is not None:
                        softplus(1)
                    if main:
                        inv_root(STATS_TWICE, 2)
                    if ssm is not None:
                        softplus(2)
                    if main:
                        for k in range(KC):
                            act.wait_ge(s_["a_free"], A_HT2 + k + 1)
                            nc.scalar.activation(ht[:, 0, k], h1f[:, k], ACT.Copy).then_inc(s_["ht_hi"], 1)
                    if ssm is not None:
                        softplus(3)
                        act.wait_ge(s_["xd_out"], 16)

                    def load_state(s):
                        if s >= 2:
                            act.wait_ge(s_["bx_done"], NU * (s - 1))
                            act.wait_ge(s_["prod_done"], NU * (s - 1))
                        nc.scalar.dma_start(bb[:, s % 2], xd_d[s:s + 1].to_broadcast([P, S])).then_inc(s_[f"b_in{s % 2}"], 16)
                        nc.scalar.dma_start(cb[:, s % 2],
                                            xd_d[DS + s:DS + s + 1].to_broadcast([P, S])).then_inc(s_[f"c_in{s % 2}"], 16)

                    def decays(step):
                        for i in scans[step]:
                            s, u = divmod(i, NU)
                            if i == 0:
                                act.wait_ge(s_["delta_done"], EC)
                                act.wait_ge(s_["du_done"], EC)
                                act.wait_ge(s_["y_init"], EC)
                            if i >= 2:
                                act.wait_ge(s_["prod_done"], i - 1)
                            for j in range(NE):
                                e = NE * u + j
                                nc.scalar.activation(da[:, i % 2, j, 1:S], dl[:, e, 1:S], ACT.Exp,
                                                     scale=nega[:, DS * e + s:DS * e + s + 1]).then_inc(s_["da_done"], 1)

                    def load_states(step):
                        for i in scans[step]:
                            if i and i % NU == 0:
                                load_state(i // NU)

                    if ssm is not None:
                        load_state(0)
                    for s in range(H2 + 2):
                        decays(s)
                        if main and s < H2:
                            if s % G2 == 0:
                                for t in range(T):
                                    a = A_AT["v", s // G2, t]
                                    act.wait_ge(s_["a_full"], a + 1)
                                    nc.scalar.activation(vp[:, s // G2 % 2, 0, t], bank_a_at(a),
                                                         ACT.Copy).then_inc(s_["v_hi"], 1)
                            for w in range(2):
                                act.wait_ge(s_["rope_f"], 2 * s + w + 1)
                                if s >= 2:
                                    act.wait_ge(s_["b_full"], B_SC2 + 2 * (s - 1))
                                nc.scalar.activation(qr[:, s % 2, w, 0], rp[:, w], ACT.Copy).then_inc(s_["rope_hi"], 1)
                        load_states(s + 1)
                        if not main:
                            continue
                        if s >= 2:
                            for kt in range(T):
                                a = A_AT["turn", s - 2, kt]
                                act.wait_ge(s_["a_full"], a + 1)
                                if s >= 3:
                                    act.wait_ge(s_["o_full"], s - 2)
                                nc.scalar.activation(pt[:, 0, kt, P * kt:S], bank_a_at(a)[:, P * kt:S],
                                                     ACT.Copy).then_inc(s_["pt_hi"], 1)
                        if 1 <= s <= H2:
                            h = s - 1
                            for u in range(2):
                                src = full_b()
                                act.wait_ge(s_["nmax2"], 2 * h + u + 1)
                                for j in range(2):
                                    t = 2 * u + j
                                    sem = (s_["exp2"], 1) if j == 0 else Bf.one()
                                    nc.scalar.activation(pf[:, t, 0:P * (t + 1)], src[:, j, 0:P * (t + 1)], ACT.Exp,
                                                         bias=nbs[:, t:t + 1], scale=SCALE2,
                                                         accum_out=sm[:, h % 2, t:t + 1]).then_inc(*sem)
                        if s >= 2:
                            h = s - 2
                            act.wait_ge(s_["o_full"], h + 1)
                            if h:
                                act.wait_ge(s_["o_lo"], h)
                            nc.scalar.activation(of, PS[:, 7], ACT.Identity,
                                                 bias=col("bv2", h)).then_inc(s_["o_free_head"], 1)
                            act.wait_ge(s_["o_free_head"], h + 1)
                            if h >= G2 and h % G2 == 0:
                                act.wait_ge(s_["a_full"], A_AT["wo", h // G2 - 1, T - 1] + 1)
                            nc.scalar.activation(op[:, 0, h % G2], of, ACT.Copy).then_inc(s_["o_hi"], 1)
                        for n in SPLIT_IN_STEP[s] if split else []:
                            chunk_hi(n)
                    if not main:
                        return
                    inv_root(STATS_MOE)
                    for k in range(KC):
                        act.wait_ge(s_["a_free"], A_HT3 + k + 1)
                        nc.scalar.activation(ht[:, 0, k], h2f[:, k], ACT.Copy).then_inc(s_["ht_hi"], 1)
                    for i in range(2):
                        act.wait_ge(s_["router_in"], i + 1)
                        nc.scalar.activation(gt[:, 1 + 2 * i], gt[:, 2 * i], ACT.Exp).then_inc(s_["router_exp"], 1)
                    act.wait_ge(s_["a_full"], A_LOGITS + 1)
                    act.wait_ge(s_["ht_lo"], 2 * KC)
                    for e in range(NEXP):
                        for i in range(KC):
                            src = full_b()
                            if e:
                                act.wait_ge(s_["hm_lo"], KC * (e - 1) + i + 1)
                            nc.scalar.activation(gf[:, i], src[:, 0], ACT.Gelu,
                                                 bias=col("be1", KC * e + i)).then_inc(*Bf.one())
                            if e >= 2:
                                act.wait_ge(s_["a_full"], A_EXP + T * (e - 1))
                            act.wait_ge(*Bf.now())
                            nc.scalar.activation(hm[:, e % 2, 0, i], gf[:, i], ACT.Copy).then_inc(s_["hm_hi"], 1)
                        if e == 2 and after is not None:
                            inv_root(STATS_AFTER)
                        decays(H2 + 2 + e)
                        if e + 1 < NEXP:
                            load_states(H2 + 3 + e)
                        for n in SPLIT_IN_EXPERT[e] if split else []:
                            chunk_hi(n)

                @block.gpsimd
                def _(pool):
                    def chunk_lo(n):
                        pool.wait_ge(s_["ch_hi"], n + 1)
                        nc.gpsimd.tensor_tensor(pair[:, n % NPAIR, 1], raw[:, n % NRAW], pair[:, n % NPAIR, 0],
                                                ALU.subtract).then_inc(s_["ch_lo"], 1)

                    def add_bias(dst, o, rows):
                        if rows:
                            pool.wait_ge(s_["ln_rows"], rows)
                        for t in range(T):
                            nc.gpsimd.tensor_tensor(dst[:, t], dst[:, t], brow[:, o:o + D],
                                                    ALU.add).then_inc(s_["bias_in"], 1)

                    def features_lo(f32, n):
                        for k in range(KC):
                            pool.wait_ge(s_["ht_hi"], KC * n + k + 1)
                            nc.gpsimd.tensor_tensor(ht[:, 1, k], f32[:, k], ht[:, 0, k],
                                                    ALU.subtract).then_inc(s_["ht_lo"], 1)

                    if main:
                        nc.gpsimd.memset(vaug[:, :, :, HD1:2 * HD1], 1.0).then_inc(s_["ones"], 1)
                        pool.wait_ge(s_["ones"], 1)
                        nc.gpsimd.memset(kst[KM:KM + 32], 1.0).then_inc(s_["ones"], 1)
                        pool.wait_ge(s_["ones"], 2)
                        add_bias(xt, 0, 0)
                        for n in range(NPAIR if split else 0):
                            chunk_lo(n)
                    if ssm is not None:
                        pool.wait_ge(s_["cx_hi"], 1)
                        nc.gpsimd.tensor_tensor(cx[:, 1], cxf, cx[:, 0], ALU.subtract).then_inc(s_["cx_lo"], 1)
                    if main:
                        for g in range(G1):
                            pool.wait_ge(s_["on_hi"], g + 1)
                            nc.gpsimd.tensor_tensor(onp[:, g, 1], on[:, g % 2], onp[:, g, 0],
                                                    ALU.subtract).then_inc(s_["on_lo"], 1)
                        features_lo(h1f, 1)
                        add_bias(hid, D, ROWS_XN)

                    def add_product(i):
                        u = i % NU
                        pool.wait_ge(s_["prod_done"], i + 1)
                        if i >= NU:
                            pool.wait_ge(s_["y_acc"], i - NU + 1)
                        y = ys[:, NE * u:NE * (u + 1)]
                        nc.gpsimd.tensor_tensor(y, y, bx[:, i % 2], ALU.add).then_inc(s_["y_acc"], 1)

                    def inputs(step):
                        for i in scans[step]:
                            s, u = divmod(i, NU)
                            if main and i >= 2:
                                add_product(i - 2)
                            pool.wait_ge(s_[f"b_in{s % 2}"], 16 * (s // 2 + 1))
                            if i == 0:
                                pool.wait_ge(s_["du_done"], EC)
                                pool.wait_ge(s_["y_init"], EC)
                            if i >= 2:
                                pool.wait_ge(s_["y_acc"], i - 1)
                            nc.gpsimd.tensor_tensor(
                                bx[:, i % 2], du[:, NE * u:NE * (u + 1)],
                                bb[:, s % 2].unsqueeze(1).to_broadcast([P, NE, S]),
                                ALU.mult).then_inc(s_["bx_done"], 1)

                    for s in range(H2 + 2):
                        inputs(s)
                        if not main:
                            continue
                        if s < H2:
                            for w in range(2):
                                pool.wait_ge(s_["rope_hi"], 2 * s + w + 1)
                                nc.gpsimd.tensor_tensor(qr[:, s % 2, w, 1], rp[:, w], qr[:, s % 2, w, 0],
                                                        ALU.subtract).then_inc(s_["rope_lo"], 1)
                        if s >= 2:
                            h = s - 2
                            pool.wait_ge(s_["o_hi"], h + 1)
                            nc.gpsimd.tensor_tensor(op[:, 1, h % G2], of, op[:, 0, h % G2],
                                                    ALU.subtract).then_inc(s_["o_lo"], 1)
                        for n in SPLIT_IN_STEP[s] if split else []:
                            chunk_lo(n)
                    if not main:
                        return
                    pool.wait_ge(s_["ln_rows"], ROWS_MOE)
                    for t in range(T):
                        nc.gpsimd.tensor_tensor(hid[:, t], hid[:, t], xt[:, t], ALU.add).then_inc(s_["x_added"], 1)
                    features_lo(h2f, 2)
                    for e in range(NEXP):
                        for i in range(KC):
                            pool.wait_ge(s_["hm_hi"], KC * e + i + 1)
                            nc.gpsimd.tensor_tensor(hm[:, e % 2, 1, i], gf[:, i], hm[:, e % 2, 0, i],
                                                    ALU.subtract).then_inc(s_["hm_lo"], 1)
                        inputs(H2 + 2 + e)
                        for n in SPLIT_IN_EXPERT[e] if split else []:
                            chunk_lo(n)

                    if ssm is not None:
                        add_product(NUNIT - 2)
                        add_product(NUNIT - 1)

                @block.vector
                def _(dve):
                    Af, own = Count(s_["a_free"]), Count(s_["dve_own"])
                    stats, rows = Count(s_["ln_stats"]), Count(s_["ln_rows"])
                    norms = [0]

                    def full_a():
                        dve.wait_ge(s_["a_full"], Af.n + 1)
                        return bank_a_at(Af.n)

                    def norm_stats(src, twice=False):
                        for t in range(T):
                            nc.vector.bn_stats(bst[:, t], src[:, t]).then_inc(*own.one())
                        dve.wait_ge(*own.now())
                        for t in range(T):
                            nc.vector.bn_aggr(bmv[:, t], bst[:, t]).then_inc(*own.one())
                        dve.wait_ge(*own.now())
                        nc.vector.tensor_scalar(vv[:, 0], bmv[:, :, 1], EPS, None, ALU.add).then_inc(*stats.one())
                        if twice:
                            nc.vector.tensor_scalar(vv[:, 1], bmv[:, :, 1], 1.0 + EPS, EPS * EPS, ALU.mult,
                                                    ALU.add).then_inc(*stats.one())

                    def norm_rows(src, dsts):
                        norms[0] += 1
                        w = len(dsts)
                        dve.wait_ge(s_["ln_guess"], norms[0])
                        nc.vector.tensor_tensor(rn[:, 0:w], rs[:, 0:w], rs[:, 0:w], ALU.mult).then_inc(*own.one())
                        dve.wait_ge(*own.now())
                        nc.vector.tensor_tensor(rn[:, 0:w], vv[:, 0:w], rn[:, 0:w], ALU.mult).then_inc(*own.one())
                        dve.wait_ge(*own.now())
                        nc.vector.tensor_scalar(rn[:, 0:w], rn[:, 0:w], -0.5, 1.5, ALU.mult,
                                                ALU.add).then_inc(*own.one())
                        dve.wait_ge(*own.now())
                        nc.vector.tensor_tensor(rs[:, 0:w], rs[:, 0:w], rn[:, 0:w], ALU.mult).then_inc(*own.one())
                        dve.wait_ge(*own.now())
                        for k, dst in enumerate(dsts):
                            for t in range(T):
                                nc.vector.tensor_scalar(dst[:, t], src[:, t], bmv[:, t, 0:1], rs[:, k, t:t + 1],
                                                        ALU.subtract, ALU.mult).then_inc(*rows.one())

                    def scaled_features(dst, name):
                        for k in range(KC):
                            src = full_a()
                            nc.vector.tensor_scalar(dst[:, k], src, col(name + "_w", k), col(name + "_b", k),
                                                    ALU.mult, ALU.add).then_inc(*Af.one())

                    if main:
                        for k in range(KC):
                            src = full_a()
                            dve.wait_ge(s_["ht_hi"], k + 1)
                            nc.vector.tensor_tensor(ht[:, 1, k], src, ht[:, 0, k], ALU.subtract).then_inc(*Af.one())
                        src = full_a()
                        for t in range(T):
                            sem = Af.one() if t == T - 1 else own.one()
                            nc.vector.tensor_tensor(
                                vaug[:, t, :, 0:HD1], src[:, P * t:P * (t + 1)].rearrange("p (g d) -> p g d", d=HD1),
                                brow[:, 2 * D:2 * D + P].rearrange("p (g d) -> p g d", d=HD1),
                                ALU.add).then_inc(*sem)
                        for i in range(QC + 1):
                            dve.wait_ge(s_["q_part"], 2 * i + 1)
                            if i >= 2:
                                dve.wait_ge(s_["q_parts"], i - 1)
                            nc.vector.tensor_tensor(qres[:, i % 2], qf[:, i % 2], qpt[:, i % 2, 0],
                                                    ALU.subtract).then_inc(s_["q_rest"], 1)
                            dve.wait_ge(s_["q_part"], 2 * i + 2)
                            nc.vector.tensor_tensor(qpt[:, i % 2, 2], qres[:, i % 2], qpt[:, i % 2, 1],
                                                    ALU.subtract).then_inc(s_["q_parts"], 1)

                        def normalise(g, r):
                            acc1 = PS[:, 6 + g % 2]
                            if r == 0:
                                dve.wait_ge(s_["pv1"], T * (g + 1))
                                nc.vector.stream_shuffle(rec[:, g % 2], acc1,
                                                         [HD1 + i % HD1 for i in range(32)]).then_inc(*own.one())
                                dve.wait_ge(*own.now())
                            part = rec[:, g % 2, P * r:P * (r + 1)]
                            nc.vector.reciprocal(part, part).then_inc(*own.one())
                            if r == 3:
                                dve.wait_ge(*own.now())
                                if g >= 2:
                                    dve.wait_ge(s_["on_lo"], g - 1)
                                nc.vector.tensor_tensor(on[:, g % 2], acc1, rec[:, g % 2],
                                                        ALU.mult).then_inc(s_["o_free_norm"], 1)

                        def split_maxima(c):
                            src = full_a()
                            n = HPC * T
                            if c >= 2:
                                dve.wait_ge(s_[f"m_in{c % 2}"], 48 * (c // 2))
                            nc.vector.tensor_copy(mpt[0:n, c % 2, 0], src[0:n, 0:P]).then_inc(*own.one())
                            dve.wait_ge(*own.now())
                            nc.vector.tensor_tensor(mf[0:n, 0], src[0:n, 0:P], mpt[0:n, c % 2, 0],
                                                    ALU.subtract).then_inc(*Af.one())
                            dve.wait_ge(*Af.now())
                            nc.vector.tensor_copy(mpt[0:n, c % 2, 1], mf[0:n, 0]).then_inc(*own.one())
                            dve.wait_ge(*own.now())
                            nc.vector.tensor_tensor(mf[0:n, 1], mf[0:n, 0], mpt[0:n, c % 2, 1],
                                                    ALU.subtract).then_inc(*own.one())
                            dve.wait_ge(*own.now())
                            nc.vector.tensor_copy(mpt[0:n, c % 2, 2], mf[0:n, 1]).then_inc(s_["m_parts"], 1)

                        norm_at = JCOLS + T + 1
                        for j in range(norm_at + T * (G1 - 1) + 2):
                            if j % JC == 0 and 0 < j <= JC * QC:
                                split_maxima(j // JC - 1)
                            g, r = divmod(j - norm_at, T)
                            for q in range(2):
                                if j < JC * QC:
                                    for i in range(JROWS // 2):
                                        src = full_a()
                                        i += JROWS * j + JROWS // 2 * q
                                        c, i = divmod(i, HPC * T)
                                        nc.vector.tensor_reduce(nm1[:, c % 2, i:i + 1], src, AX.X, ALU.max,
                                                                negate=True).then_inc(*Af.one())
                                if g >= 0 and r < 2:
                                    normalise(g, 2 * r + q)

                    def conv(e):
                        dve.wait_ge(s_["b_free"], B_SSM + e + 1)
                        if e >= 2:
                            dve.wait_ge(s_["u_done"], e - 1)
                        a = acc[:, e % 2]
                        nc.vector.tensor_scalar(a, xpad[:, e % 2, 0:S], col("conv_w", DC * e), col("conv_b", e),
                                                ALU.mult, ALU.add).then_inc(*own.one())
                        for j in range(1, DC):
                            dve.wait_ge(*own.now())
                            sem = (s_["conv_done"], 1) if j == DC - 1 else own.one()
                            nc.vector.scalar_tensor_tensor(a, xpad[:, e % 2, j:j + S], col("conv_w", DC * e + j),
                                                           a, ALU.mult, ALU.add).then_inc(*sem)

                    def delta(e):
                        dve.wait_ge(s_["sp_log"], e + 1)
                        k = e % 2
                        nc.vector.tensor_tensor(dl[:, e], spt[:, k, 2], spt[:, k, 0],
                                                ALU.add).then_inc(s_["delta_done"], 1)
                        dve.wait_ge(s_["delta_done"], e + 1)
                        nc.vector.tensor_tensor(du[:, e], dl[:, e], us[:, e], ALU.mult).then_inc(s_["du_done"], 1)

                    if ssm is not None:
                        if not main:
                            dve.wait_ge(s_["x_in"], 16)
                            norm_stats(xt)
                            norm_rows(xt, [xn])
                        else:
                            dve.wait_ge(s_["stk_out"], 16 * (QC + 1))
                        nc.vector.memset(xpad[:, :, 0:DC - 1], 0.0).then_inc(s_["pad_zero"], 1)
                        for e in range(EC):
                            conv(e)
                    if main:
                        dve.wait_ge(s_["bias_in"], T)
                        for t in range(T):
                            src = full_a()
                            nc.vector.tensor_tensor(xt[:, t], src, xt[:, t], ALU.add).then_inc(*Af.one())
                        dve.wait_ge(*Af.now())
                        norm_stats(xt)
                    if ssm is not None:
                        delta(0)
                    if main:
                        norm_rows(xt, [xn])
                        if ssm is not None:
                            nc.vector.memset(da[:, :, :, 0:1], 0.0).then_inc(*own.one())
                        dve.wait_ge(s_["z_silu"], 1)
                        for e in range(EC):
                            nc.vector.tensor_tensor(ys[:, e], ys[:, e], xn[:, e], ALU.mult).then_inc(s_["gated"], 1)
                        for t in range(T):
                            src = full_a()
                            nc.vector.tensor_tensor(xt[:, t], src, xt[:, t], ALU.add).then_inc(*Af.one())
                        dve.wait_ge(*Af.now())
                        norm_stats(xt, twice=True)
                    if ssm is not None:
                        delta(1)
                    if main:
                        norm_rows(xt, [hid, xn])
                    if ssm is not None:
                        delta(2)
                    if main:
                        scaled_features(h1f, "ln1")
                    if ssm is not None:
                        if not main:
                            nc.vector.memset(da[:, :, :, 0:1], 0.0).then_inc(*own.one())
                        for e in range(EC):
                            nc.vector.tensor_scalar(ys[:, e], us[:, e], col("ssm_d", e), None,
                                                    ALU.mult).then_inc(s_["y_init"], 1)
                        delta(3)

                    def scan(i):
                        s, u = divmod(i, NU)
                        k = i % 2
                        dve.wait_ge(s_["bx_done"], i + 1)
                        dve.wait_ge(s_["da_done"], NE * (i + 1))
                        flat = bx[:, k].rearrange("p e n -> p (e n)")
                        nc.vector.tensor_tensor_scan(flat, da[:, k].rearrange("p e n -> p (e n)"), flat, 0.0,
                                                     ALU.mult, ALU.add).then_inc(*own.one())
                        dve.wait_ge(*own.now())
                        dve.wait_ge(s_[f"c_in{s % 2}"], 16 * (s // 2 + 1))
                        nc.vector.tensor_tensor(bx[:, k], bx[:, k], cb[:, s % 2].unsqueeze(1).to_broadcast([P, NE, S]),
                                                ALU.mult).then_inc(s_["prod_done"], 1)
                        if main:
                            return
                        dve.wait_ge(s_["prod_done"], i + 1)
                        y = ys[:, NE * u:NE * (u + 1)]
                        if i >= NU:
                            dve.wait_ge(s_["y_acc"], i - NU + 1)
                        nc.vector.tensor_tensor(y, y, bx[:, k], ALU.add).then_inc(s_["y_acc"], 1)

                    def diagonals(h):
                        dve.wait_ge(s_["b_free"], B_SC2 + 2 * (h + 1))
                        nc.vector.reciprocal(rc[:], sm[:, h % 2]).then_inc(*own.one())
                        dve.wait_ge(*own.now())
                        nc.vector.tensor_tensor(dg, identf[:].unsqueeze(1).to_broadcast([P, T, P]),
                                                rc[:].unsqueeze(2).to_broadcast([P, T, P]),
                                                ALU.mult).then_inc(s_["p_norm"], 1)

                    def v_lo(g):
                        for t in range(T):
                            src = full_a()
                            dve.wait_ge(s_["v_hi"], T * g + t + 1)
                            nc.vector.tensor_tensor(vp[:, g % 2, 1, t], src, vp[:, g % 2, 0, t],
                                                    ALU.subtract).then_inc(*Af.one())

                    def rope_in(s, w):
                        src = full_a()
                        if s:
                            dve.wait_ge(s_["rope_lo"], 2 * (s - 1) + w + 1)
                        bias = col("bk2" if w else "bq2", s)
                        nc.vector.scalar_tensor_tensor(rp[:, w], src, bias, ropet[:, 0], ALU.add,
                                                       ALU.mult).then_inc(*own.one())
                        half = P // 2
                        for a, z in ((0, half), (half, 0)):
                            sem = Af.one() if z == 0 else own.one()
                            nc.vector.scalar_tensor_tensor(
                                rtmp[a:a + half], src[z:z + half], bias[z:z + half],
                                ropet[z:z + half, 1], ALU.add, ALU.mult).then_inc(*sem)
                        dve.wait_ge(*Af.now())
                        nc.vector.tensor_tensor(rp[:, w], rp[:, w], rtmp, ALU.add).then_inc(s_["rope_f"], 1)
                        dve.wait_ge(s_["rope_f"], 2 * s + w + 1)

                    def turned_lo(h, kt):
                        src = full_a()
                        dve.wait_ge(s_["pt_hi"], T * h + kt + 1)
                        nc.vector.tensor_tensor(pt[:, 1, kt, P * kt:S], src[:, P * kt:S],
                                                pt[:, 0, kt, P * kt:S], ALU.subtract).then_inc(*Af.one())

                    def row_maxima(h):
                        for u in range(2):
                            dve.wait_ge(s_["b_full"], B_SC2 + 2 * h + u + 1)
                            src = bank_b_at(B_SC2 + 2 * h + u)
                            for j in range(2):
                                t = 2 * u + j
                                nc.vector.tensor_reduce(nmx[:, t:t + 1], src[:, j, 0:P * (t + 1)], AX.X, ALU.max,
                                                        negate=True).then_inc(*own.one())
                            dve.wait_ge(*own.now())
                            nc.vector.tensor_scalar(nbs[:, 2 * u:2 * u + 2], nmx[:, 2 * u:2 * u + 2], SCALE2, None,
                                                    ALU.mult).then_inc(s_["nmax2"], 1)

                    def add_out(g, t):
                        if t == 0:
                            if g:
                                dve.wait_ge(s_["a_free"], A_AT["wo", g - 1, T - 1] + 1)
                            else:
                                dve.wait_ge(s_["bias_in"], 2 * T)
                        src = full_a()
                        nc.vector.tensor_tensor(hid[:, t], src, hid[:, t], ALU.add).then_inc(*Af.one())

                    for s in range(H2 + 3 if main else DS):
                        if main and 2 <= s < H2 + 2:
                            diagonals(s - 2)
                        if main and s < H2:
                            if s % G2 == 0:
                                v_lo(s // G2)
                            for w in range(2):
                                rope_in(s, w)
                        units = list(scans[s]) if s < H2 + 2 else []
                        for t in range(T if main else 0):
                            if 2 <= s < H2 + 2:
                                turned_lo(s - 2, t)
                            if t == 0 and 1 <= s <= H2:
                                row_maxima(s - 1)
                            if s > G2 and s % G2 == 2:
                                if units and t:
                                    scan(units.pop(0))
                                add_out(s // G2 - 1, t)
                        for i in units:
                            scan(i)
                    if not main:
                        return
                    dve.wait_ge(*Af.now())

                    norm_stats(hid)
                    norm_rows(hid, [xn])
                    scaled_features(h2f, "ln2")
                    src = full_a()

                    def step(ins, sem=None):
                        sem = sem or own.one()
                        ins.then_inc(*sem)
                        dve.wait_ge(sem[0], 1 if sem[0] is not own.sem else own.n)

                    def over_e(a):
                        return a.unsqueeze(2).to_broadcast([P, T, NEXP])

                    tt, tr = nc.vector.tensor_tensor, nc.vector.tensor_reduce
                    nc.vector.tensor_copy(gt[:, 4], src[:, 0:T * NEXP].rearrange("p (t e) -> p t e",
                                                                                e=NEXP)).then_inc(*Af.one())
                    dve.wait_ge(*Af.now())
                    step(tr(gv[:, 0], gt[:, 4], AX.X, ALU.max))
                    tt(gt[:, 0], gt[:, 4], over_e(gv[:, 0]), ALU.subtract).then_inc(s_["router_in"], 1)
                    dve.wait_ge(s_["router_exp"], 1)
                    step(tr(gv[:, 1], gt[:, 1], AX.X, ALU.add))
                    step(nc.vector.reciprocal(gv[:, 1], gv[:, 1]))
                    step(tt(gt[:, 4], gt[:, 1], over_e(gv[:, 1]), ALU.mult))
                    for e in range(NEXP):
                        me = gt[:, 4, :, e:e + 1]
                        if e:
                            tt(gt[:, 5, :, 0:e], gt[:, 4, :, 0:e], me.to_broadcast([P, T, e]),
                               ALU.is_ge).then_inc(*own.one())
                        step(tt(gt[:, 5, :, e:NEXP], gt[:, 4, :, e:NEXP], me.to_broadcast([P, T, NEXP - e]),
                                ALU.is_gt))
                        step(tr(gt[:, 6, :, e:e + 1], gt[:, 5], AX.X, ALU.add))
                    step(nc.vector.tensor_scalar(gt[:, 6], gt[:, 6], 1.5, None, ALU.is_lt))
                    step(tr(gv[:, 2], gt[:, 4], AX.X, ALU.max))
                    tt(gt[:, 2], gt[:, 4], over_e(gv[:, 2]), ALU.subtract).then_inc(s_["router_in"], 1)
                    dve.wait_ge(s_["router_exp"], 2)
                    step(tt(gt[:, 5], gt[:, 3], gt[:, 6], ALU.mult))
                    step(tr(gv[:, 3], gt[:, 5], AX.X, ALU.add))
                    step(nc.vector.reciprocal(gv[:, 3], gv[:, 3]))
                    step(tt(gt[:, 7], gt[:, 5], over_e(gv[:, 3]), ALU.mult), (s_["comb"], 1))
                    src = full_a()
                    nc.vector.tensor_copy(combt[0:NEXP].rearrange("p t n -> p (t n)"), src[0:NEXP]).then_inc(*Af.one())
                    dve.wait_ge(s_["x_added"], T)
                    for t in range(T):
                        src = full_a()
                        nc.vector.tensor_tensor(hid[:, t], src, hid[:, t], ALU.add).then_inc(*Af.one())
                    for e in range(NEXP):
                        if e == 1 and after is not None:
                            dve.wait_ge(s_["x_in"], 16)
                            norm_stats(xt)
                        for i in scans[H2 + 2 + e]:
                            scan(i)
                        dve.wait_ge(*Af.now())
                        for t in range(T):
                            src = full_a()
                            nc.vector.scalar_tensor_tensor(hid[:, t], src, gt[:, 7, t, e:e + 1], hid[:, t],
                                                           ALU.mult, ALU.add).then_inc(*Af.one())
                        if e == 1 and after is not None:
                            norm_rows(xt, [xn])
                    assert Af.n == A_EXP + T * NEXP

        run(0, main=False, ssm=0)
        fresh()
        run(0, main=True, ssm=1, split=True)
        fresh()
        with nc.Fori(1, B - 1) as b:
            run(b, main=True, ssm=b + 1)
            fresh()
        run(B - 1, main=True, ssm=None)


def kernel(x, ctx_1024, L0_attn_w_qkv, L0_attn_b_qkv, L0_attn_w_out, L0_attn_b_out, L0_xattn_in_proj_w,
           L0_xattn_conv_w, L0_xattn_conv_b, L0_xattn_x_proj_w, L0_xattn_dt_proj_w, L0_xattn_dt_proj_b,
           L0_xattn_A_log, L0_xattn_D, L0_ffn_wq, L0_ffn_bq, L0_ffn_wk, L0_ffn_bk, L0_ffn_wv, L0_ffn_bv,
           L0_ffn_wo, L0_ffn_bo, L0_ffn_ln1_w, L0_ffn_ln1_b, L0_ffn_ln2_w, L0_ffn_ln2_b, L0_ffn_w_gate,
           L0_ffn_we1, L0_ffn_be1, L0_ffn_we2, L0_ffn_be2):
    import numpy as np
    import concourse.bacc as bacc
    from concourse.bass_utils import run_bass_kernel_spmd

    def tiles(w):
        w = np.asarray(w)
        return np.ascontiguousarray(w.reshape(-1, P, w.shape[1]).transpose(1, 0, 2).reshape(P, -1))

    def cols(v):
        return np.asarray(v).reshape(-1, P).T

    bq = np.asarray(L0_attn_b_qkv)
    fields = {
        "bq1": cols(bq[:D]), "bk1": cols(bq[D:D + P]), "conv_w": tiles(L0_xattn_conv_w),
        "conv_b": cols(L0_xattn_conv_b), "dt_b": cols(L0_xattn_dt_proj_b), "a_log": tiles(L0_xattn_A_log),
        "ssm_d": cols(L0_xattn_D), "ln1_w": cols(L0_ffn_ln1_w), "ln1_b": cols(L0_ffn_ln1_b),
        "ln2_w": cols(L0_ffn_ln2_w), "ln2_b": cols(L0_ffn_ln2_b), "bq2": cols(L0_ffn_bq),
        "bk2": cols(L0_ffn_bk), "bv2": cols(L0_ffn_bv), "be1": cols(np.asarray(L0_ffn_be1).reshape(-1)),
        "one": np.ones((P, 1), np.float32),
        "w_gate": tiles(L0_ffn_w_gate),
    }
    assert list(fields) == list(PCOLS)
    wq, wk, wv, wo = (np.asarray(w) for w in (L0_ffn_wq, L0_ffn_wk, L0_ffn_wv, L0_ffn_wo))
    chunks = [tiles(wv[:, D * g:D * (g + 1)]) for g in range(H2 // G2)]
    for p in range(H2 // 2):
        a, b = 2 * p * HD2, (2 * p + 1) * HD2
        chunks.append(tiles(np.concatenate([wq[:, a:a + HD2], wk[:, a:a + HD2],
                                            wq[:, b:b + HD2], wk[:, b:b + HD2]], axis=1)))
    chunks += [tiles(wo[D * g:D * (g + 1)]) for g in range(H2 // G2)]
    chunks += [tiles(w) for w in np.asarray(L0_ffn_we1)] + [tiles(w) for w in np.asarray(L0_ffn_we2)]

    freq = (np.float32(1.0) / np.float32(10000.0) ** (np.arange(0, HD2, 2, dtype=np.float32) / np.float32(HD2)))
    angle = freq[:, None].astype(np.float32) * np.arange(S, dtype=np.float32)[None, :]
    angle = np.concatenate([angle, angle], axis=0)
    sign = np.where(np.arange(P) < P // 2, 1.0, -1.0).astype(np.float32)[:, None]
    rope = np.stack([np.cos(angle), np.sin(angle) * sign], axis=1).astype(np.float32)
    causal = np.triu(np.full((P, P), -1e30, np.float32), 1)

    arrays = {
        "x": np.ascontiguousarray(np.asarray(x).reshape(B, T, P, D).transpose(0, 2, 1, 3)),
        "ctx_t": np.ascontiguousarray(np.asarray(ctx_1024).transpose(0, 2, 1).reshape(B, DM // P, P, S)
                                      .transpose(0, 2, 1, 3)),
        "w_qkv": tiles(np.asarray(L0_attn_w_qkv).T),
        "w_out": tiles(np.asarray(L0_attn_w_out).T),
        "in_w": tiles(np.asarray(L0_xattn_in_proj_w).T),
        "xp_w": tiles(np.asarray(L0_xattn_x_proj_w).T).reshape(P, EC, DR + 2 * DS),
        "dt_w": np.ascontiguousarray(np.asarray(L0_xattn_dt_proj_w).T),
        "params": np.ascontiguousarray(np.concatenate(list(fields.values()), axis=1)),
        "bias_rows": np.concatenate([np.asarray(L0_attn_b_out), np.asarray(L0_ffn_bo), bq[D + P:]])[None, :],
        "be2": np.asarray(L0_ffn_be2),
        "chunks": np.stack(chunks),
        "ident": np.eye(P, dtype=np.float32),
        "causal": causal,
        "rope": rope,
    }
    nc = bacc.Bacc("TRN2", target_bir_lowering=False, num_devices=1)
    aps = {n: nc.dram_tensor(n, a.shape, mybir.dt.from_np(a.dtype), kind="ExternalInput").ap()
           for n, a in arrays.items()}
    aps["out"] = nc.dram_tensor("out", (B, P, T, D), F32, kind="ExternalOutput").ap()
    build(nc, **aps)
    r = run_bass_kernel_spmd(nc, [arrays], core_ids=[0])
    return r.results[0]["out"].transpose(0, 2, 1, 3).reshape(B, S, D)
```

```python
from contextlib import ExitStack

import concourse.bass as bass
from concourse import mybir

F32 = mybir.dt.float32
BF16 = mybir.dt.bfloat16
ACT = mybir.ActivationFunctionType
ALU = mybir.AluOpType
AX = mybir.AxisListType

P = 128
B, S, D = 4, 512, 512
T = S // P
KC = D // P
H1, G1, HD1 = 32, 8, 16
R1 = H1 // G1
HPC = P // HD1
QC = H1 // HPC
NS = 6
QPARTS = (0, 0, 1, 1, 0, 2)
KPARTS = (0, 1, 0, 1, 2, 0)
NQ = 3
KM = NS * HD1
SCALE1 = 1.0 / float(HD1) ** 0.5
DM, DI, DS, DR, DC = 256, 512, 16, 16, 4
EC = DI // P
EPS = 1e-5
NE = 2
NU = EC // NE
H2, HD2 = 16, 128
G2 = 4
SCALE2 = 1.0 / float(HD2) ** 0.5
NEXP = 4
CH = 2048
NRAW, NPAIR = 2, 3
NRING = NRAW + NPAIR

PCOLS, NPAR = {}, 0
for _name, _w in (("bq1", QC), ("bk1", 1), ("conv_w", EC * DC), ("conv_b", EC), ("dt_b", EC),
                  ("a_log", EC * DS), ("ssm_d", EC), ("ln1_w", KC), ("ln1_b", KC), ("ln2_w", KC),
                  ("ln2_b", KC), ("bq2", H2), ("bk2", H2), ("bv2", H2), ("be1", NEXP * KC),
                  ("one", 1), ("w_gate", KC * NEXP)):
    PCOLS[_name] = NPAR
    NPAR += _w


STEPS = H2 + 3
WO_STEP = {min(G2 * _g + G2 + 3, STEPS - 1): _g for _g in range(H2 // G2)}


def chunk_order():
    out = []
    for s in range(STEPS):
        if s < H2 and s % G2 == 0:
            out.append(("v", s // G2, s))
        if s < H2 and s % 2 == 0:
            out.append(("qk", s // 2, s))
        if s in WO_STEP:
            out.append(("wo", WO_STEP[s], s))
    out.append(("w1", 0, STEPS))
    for e in range(NEXP):
        if e + 1 < NEXP:
            out.append(("w1", e + 1, STEPS + e))
        out.append(("w2", e, STEPS + e))
    return out


CHUNKS = chunk_order()
CHUNK_AT = {(k, i): n for n, (k, i, _) in enumerate(CHUNKS)}
CHUNK_ROW = {"v": 0, "qk": 4, "wo": 12, "w1": 16, "w2": 20}
SPLIT_IN_STEP = {s: [n for n, c in enumerate(CHUNKS)
                     if n >= NPAIR and c[0] in ("v", "qk", "wo") and min(c[2], H2 + 1) - 2 == s]
                 for s in range(H2 + 2)}
_moe = [n for n, c in enumerate(CHUNKS) if c[0] in ("w1", "w2")]
SPLIT_IN_STEP[H2] = [_moe[0]]
SPLIT_IN_STEP[STEPS - 2] = [_moe[1]]
SPLIT_IN_STEP[STEPS - 1] = [_moe[2]]
SPLIT_IN_EXPERT = {0: [_moe[3]], 1: [_moe[4]], 2: _moe[5:7], 3: [_moe[7]]}

A_V1, A_MAX = 0, 1
A_CH = HPC * T + 1
JC, JLAG = 2 * T, 2
JROWS = HPC * T // JC
JCOLS = JC + JLAG
A_OUT1 = A_MAX + QC * A_CH
A_GATE = A_OUT1 + T
A_HT2 = A_GATE + T


def ring_a_units(s):
    out = []
    if s < H2 and s % G2 == 0:
        out += [("v", s // G2, t) for t in range(T)]
    if s < H2:
        out += [("qk", s, w) for w in range(2)]
    for t in range(T):
        if 2 <= s < H2 + 2:
            out.append(("turn", s - 2, t))
        if s in WO_STEP:
            out.append(("wo", WO_STEP[s], t))
    return out


A_AT, _n = {}, A_HT2 + KC
for _s in range(STEPS):
    for _u in ring_a_units(_s):
        A_AT[_u] = _n
        _n += 1
A_HT3 = _n
A_LOGITS = A_HT3 + KC
A_COMB = A_LOGITS + 1
A_BE2 = A_COMB + 1
A_EXP = A_BE2 + T
A_NEXT = A_EXP + T * (NEXP - 1)

NUNIT = NU * DS
SCAN_ALONE = [list(range(NU * _s, NU * (_s + 1))) for _s in range(DS)]
SCAN_BESIDE, _n = [], 0
for _s in range(STEPS + NEXP):
    _k = 2 if _s >= STEPS or len(ring_a_units(_s)) > T + 2 else 1
    _k = min(_k, NUNIT - _n - (2 * NEXP if _s < STEPS else 0))
    SCAN_BESIDE.append(list(range(_n, _n + _k)))
    _n += _k
assert _n == NUNIT

Y_BANKS = (3, 5, 6, 7)

SEMS = """const_in x_in be2_in raw_in0 raw_in1 stk_out0 stk_out1 stk_out2 stk_out3 stk_out4 stk_in0 stk_in1
stk_in2 kst_in m_in0 m_in1 ot_in ctx_in dtw_in xd_out b_in0 b_in1 c_in0 c_in1 y_out a_full a_free
b_full b_free o_full o_free_norm on_done o_free_head ln_stats ln_guess ln_rows ht_hi ht_lo next_hi
bias_in ch_hi ch_lo pair_out0 pair_out1 pair_out2 pair_in0 pair_in1 pair_in2 pair_in3 pair_in4
q_part q_rest q_parts m_parts ones pv1 on_hi on_lo z_silu gated cx_hi cx_lo pad_zero conv_done
u_done sp_log delta_done du_done y_init da_done bx_done prod_done y_acc v_hi rope_in rope_f rope_hi
rope_lo nmax2 exp2 p_norm pt_hi o_hi o_lo router_in router_exp comb hm_hi hm_lo x_added dve_own
act_own
""".split()


class Count:

    def __init__(self, sem):
        self.sem, self.n = sem, 0

    def one(self):
        self.n += 1
        return self.sem, 1

    def now(self):
        return self.sem, self.n


def build(nc, x, ctx_t, w_qkv, w_out, in_w, xp_w, dt_w, params, bias_rows, be2, chunks, ident, causal,
          rope, out):
    with ExitStack() as ctx:
        def sb(name, shape, dt=F32):
            return ctx.enter_context(nc.sbuf_tensor(name, shape, dt))

        s_ = {n: ctx.enter_context(nc.semaphore(n)) for n in SEMS}
        lo_sem = min(s.num for s in s_.values())
        hi_sem = max(s.num for s in s_.values())
        assert hi_sem - lo_sem + 1 == len(SEMS)

        stk_d = nc.dram_tensor("stk_d", (QC + 1, P, 3, S), BF16, kind="Internal").ap()
        pair_d = nc.dram_tensor("pair_d", (len(CHUNKS), P, 2, CH), BF16, kind="Internal").ap()
        xd_d = nc.dram_tensor("xd_d", (2 * DS, S), F32, kind="Internal").ap()

        identf = sb("identf", [P, P])
        identb = sb("identb", [P, P], BF16)
        causb = sb("causb", [P, P], BF16)
        par = sb("par", [P, NPAR])
        ropet = sb("ropet", [P, 2, S])
        brow = sb("brow", [P, 2 * D + P])
        xpw = sb("xpw", [P, EC, DR + 2 * DS])
        nega = sb("nega", [P, EC * DS])
        wqkv = sb("wqkv", [P, 2, KC, 768], BF16)
        wout = sb("wout", [P, 2, KC, D], BF16)
        inw = sb("inw", [P, 2, DM // P, DI], BF16)
        pair = sb("pair", [P, NRING, 2, CH], BF16)
        raw = pair[:, NPAIR:NRING].rearrange("p n q c -> p (n q c)").bitcast(F32).rearrange(
            "p (n c) -> p n c", n=NRAW)

        xt = sb("xt", [P, T, D])
        hid = sb("hid", [P, T, D])
        ys = sb("ys", [P, EC, S])
        ht = sb("ht", [P, 2, KC, S], BF16)
        bst = sb("bst", [P, T, 6])
        bmv = sb("bmv", [P, T, 2])
        rs = sb("rs", [P, 2, T])
        vv = sb("vv", [P, 2, T])
        ra = sb("ra", [P, 2, T])
        rn = sb("rn", [P, 2, T])
        nmx = sb("nmx", [P, T])
        nbs = sb("nbs", [P, T])
        sm = sb("sm", [P, 2, T])
        rc = sb("rc", [P, T])
        nm1 = sb("nm1", [P, 2, HPC * T])
        gt = sb("gt", [P, 8, T, NEXP])
        gv = sb("gv", [P, 4, T])
        rcol = sb("rcol", [P, S // 32])

        REGION = 25088
        region = sb("region", [P, REGION])

        def carve(at, shape, dt=F32):
            n = 1
            for k in shape:
                n *= k
            words = n if dt == F32 else n // 2
            assert at + words <= REGION, at + words
            a = region[:, at:at + words]
            if dt != F32:
                a = a.bitcast(dt)
            if len(shape) > 1:
                names = "abcd"[:len(shape)]
                a = a.rearrange(f"p ({' '.join(names)}) -> p {' '.join(names)}",
                                **{c: k for c, k in zip(names[1:], shape[1:])})
            return a, at + words

        pf, at = carve(0, [T, S])
        xn = pf
        vp0 = at
        vp, at = carve(at, [2, 2, T, D], BF16)
        qr, at = carve(at, [2, 2, 2, S], BF16)
        rp0 = at
        rp, at = carve(at, [2, S])
        rtmp, at = carve(at, [S])
        pt0 = at
        pt, at = carve(at, [2, T, S], BF16)
        of, at = carve(at, [S])
        op0 = at
        op, at = carve(at, [2, G2, S], BF16)
        dl, at = carve(at, [EC, S])
        du, at = carve(at, [EC, S])
        us, _ = carve(op0, [EC, S])
        bx, at = carve(at, [2, NE, S])
        da, at = carve(at, [2, NE, S])
        bb, at = carve(at, [2, S])
        cb, at = carve(at, [2, S])
        dg0 = at
        dg, _ = carve(at, [T, P])
        xd, at = carve(at, [S])
        cxf, at = carve(vp0, [DM // P, S])
        cx, at = carve(at, [2, DM // P, S], BF16)
        xpad, at = carve(at, [2, S + 4])
        dtw, _ = carve(dg0 - DI, [DI])
        acc, _ = carve(rp0, [2, S])
        spt, _ = carve(vp0 + 3584, [2, 3, S])
        h1f, _ = carve(pt0, [KC, S])
        bx_more, _ = carve(pt0, [2, NE, S])
        hm, at = carve(vp0, [2, 2, KC, S], BF16)
        gf, _ = carve(at, [KC, S])
        h2f = gf
        combt, at = carve(pt0, [T, P])
        be2s, _ = carve(at, [D])
        qf, at = carve(T * S, [2, S])
        qres, at = carve(at, [2, S])
        qpt, at = carve(at, [2, 3, S], BF16)
        qst, at = carve(at, [NQ - 1, HPC, S], BF16)
        kst, at = carve(at, [G1, S], BF16)
        vaug, at = carve(at, [T, G1, 2 * HD1])
        qpt_more, _ = carve(at, [QC - 1, 3, S], BF16)
        pt1, at = carve(at, [2, R1, S])
        on, at = carve(at, [2, S])
        rec, at = carve(at, [2, S])
        onp, at = carve(at, [2, 2, G1 // 2, S], BF16)
        ot, _ = carve(0, [2, KC, S], BF16)
        mf, at = carve(at, [2, P])
        mpt, at = carve(at, [2, 3, P], BF16)

        def qparts(i):
            return qpt[:, i] if i < 2 else qpt_more[:, i - 2]

        qst2 = hid[:].rearrange("p t d -> p (t d)").bitcast(BF16).rearrange("p (h n) -> p h n", n=S)

        def halves(a):
            return a.rearrange("p (a n) -> p a n", a=2)

        rother = (halves(rtmp), pf[:, 0:2, S // 2:S])

        def qstack(c):
            return qst[:, c % NQ] if c % NQ < NQ - 1 else qst2

        PS = ctx.enter_context(nc.psum_tensor("PS", [P, 8, 512], F32))

        def bank_a_at(n):
            return PS[:, n % 2] if n < A_HT2 else PS[:, (0, 1, 6)[(n - A_HT2) % 3]]

        def a_before(n):
            return n - 1 if n < A_HT2 else max(A_HT2, n - 2)

        def bank_b_at(n):
            return PS[:, 2 + 2 * (n % 2):4 + 2 * (n % 2)]

        def col(name, i, n=1):
            a = PCOLS[name] + i
            return par[:, a:a + n]

        def pe3(dst, l, r, start, stop):
            nc.tensor.matmul(dst, l(0), r(0), start=start, stop=False)
            nc.tensor.matmul(dst, l(0), r(1), start=False, stop=False)
            return nc.tensor.matmul(dst, l(1), r(0), start=False, stop=stop)

        loads = [(identf[:], ident), (par[:], params), (ropet[:], rope), (xpw[:], xp_w),
                 (brow[:], bias_rows.to_broadcast([P, 2 * D + P]))]
        stages, at = [], 0
        for src, dst in ((w_qkv, wqkv), (w_out, wout), (in_w, inw)):
            n = src.shape[1]
            stages.append((region[:, at:at + n], src, dst[:, 0].rearrange("p k n -> p (k n)"),
                           dst[:, 1].rearrange("p k n -> p (k n)")))
            at += n
        causf = region[:, at:at + P]
        loads += [(st, src) for st, src, _, _ in stages] + [(causf, causal)]

        with nc.Block() as block:
            @block.sync
            def _(sp):
                for dst, src in loads:
                    sp.dma_start(dst, src).then_inc(s_["const_in"], 16)

            @block.scalar
            def _(act):
                act.wait_ge(s_["const_in"], 16 * len(loads))
                for st, _, hi, _ in stages:
                    nc.scalar.activation(hi, st, ACT.Copy).then_inc(s_["act_own"], 1)
                nc.scalar.activation(identb[:], identf[:], ACT.Copy).then_inc(s_["act_own"], 1)
                nc.scalar.activation(causb[:], causf, ACT.Copy).then_inc(s_["act_own"], 1)
                nc.scalar.activation(nega[:], col("a_log", 0, EC * DS), ACT.Exp).then_inc(s_["act_own"], 1)

            @block.vector
            def _(dve):
                for i, (st, _, hi, lo) in enumerate(stages):
                    dve.wait_ge(s_["act_own"], i + 1)
                    nc.vector.tensor_tensor(lo, st, hi, ALU.subtract).then_inc(s_["dve_own"], 1)
                dve.wait_ge(s_["act_own"], len(stages) + 3)
                nc.vector.tensor_scalar(nega[:], nega[:], -1.0, None, ALU.mult).then_inc(s_["dve_own"], 1)

        def fresh():
            nc.all_engine_barrier()
            nc.gpsimd.sem_clear(range(lo_sem, hi_sem + 1))
            nc.all_engine_barrier()

        fresh()

        def run(b, main, ssm, split=False):
            ring = NPAIR if split else NRING
            scans = [] if ssm is None else SCAN_BESIDE if main else SCAN_ALONE
            scans = scans + [[]] * (STEPS + NEXP - len(scans))
            n_bx = 2 if main else 4

            def bx_at(i):
                return bx[:, i % n_bx] if i % n_bx < 2 else bx_more[:, i % n_bx - 2]

            after = ssm
            STATS_GATE, STATS_TWICE, STATS_MOE, STATS_AFTER = 1, 3, 4, 5 if main else 1
            ROWS_GATE, ROWS_XN, ROWS_HID, ROWS_MOE, ROWS_AFTER = T, 2 * T, 3 * T, 4 * T, 5 * T if main else T
            next_at = A_NEXT if main else 0
            skip = KC if after is not None else 0

            def a_expert(e):
                return A_EXP + T * e + (skip if e == NEXP - 1 else 0)

            B_SC1 = (QC + 1) if main else 0
            B_SSM = B_SC1 + (2 * T * G1 if main else 0)
            B_SC2 = B_SSM + (2 * EC + 1 if ssm is not None else 0)
            B_EXP = B_SC2 + 2 * H2

            with nc.Block() as block:
                def chunk_free(eng, n):
                    kind, i, _ = CHUNKS[n]
                    if kind == "v":
                        eng.wait_ge(s_["a_full"], A_AT["v", i, T - 1] + 1)
                    elif kind == "qk":
                        eng.wait_ge(s_["a_full"], A_AT["qk", 2 * i + 1, 1] + 1)
                    elif kind == "wo":
                        eng.wait_ge(s_["a_full"], A_AT["wo", i, T - 1] + 1)
                    elif kind == "w1":
                        eng.wait_ge(s_["b_full"], B_EXP + KC * (i + 1))
                    else:
                        eng.wait_ge(s_["a_full"], a_expert(i) + T)

                def chunk_there(eng, n):
                    if split:
                        eng.wait_ge(s_["ch_lo"], n + 1)
                    else:
                        eng.wait_ge(s_[f"pair_in{n % NRING}"], 16 * (n // NRING + 1))

                @block.sync
                def _(sp):
                    def store_pair(n):
                        sp.dma_start(pair_d[n], pair[:, n % NPAIR]).then_inc(s_[f"pair_out{n % NPAIR}"], 16)

                    def load_chunk(n):
                        if not split:
                            if n >= NRING:
                                chunk_free(sp, n - NRING)
                            sp.dma_start(pair[:, n % NRING], pair_d[n]).then_inc(s_[f"pair_in{n % NRING}"], 16)
                            return
                        if n >= NRAW:
                            sp.wait_ge(s_["ch_lo"], n - NRAW + 1)
                            store_pair(n - NRAW)
                        kind, i, _ = CHUNKS[n]
                        sp.dma_start(raw[:, n % NRAW], chunks[CHUNK_ROW[kind] + i]).then_inc(s_[f"raw_in{n % 2}"], 16)

                    def stack_out(i):
                        sp.wait_ge(s_["q_parts"], i + 1)
                        sp.dma_start(stk_d[i], qparts(i)).then_inc(s_[f"stk_out{i}"], 16)

                    def stack_in(i):
                        sp.wait_ge(s_[f"stk_out{i}"], 16)
                        if i > NQ:
                            sp.wait_ge(s_["pv1"], JC * (i - NQ))
                        for j in range(NS):
                            part = QPARTS[j] if i else KPARTS[j]
                            src = stk_d[i, :, part].rearrange("(h d) n -> d h n", d=HD1)
                            dst = qstack(i - 1)[HD1 * j:HD1 * (j + 1)] if i else kst[HD1 * j:HD1 * (j + 1)]
                            sp.dma_start(dst, src).then_inc(s_[f"stk_in{(i - 1) % NQ}" if i else "kst_in"], 16)

                    def maxima(c):
                        sp.wait_ge(s_["m_parts"], c + 1)
                        for j in range(3):
                            sp.dma_start(qstack(c)[KM + j:KM + j + 1].rearrange("o h (t n) -> o (h t) n", n=P),
                                         mpt[0:HPC * T, c % 2, j]).then_inc(s_[f"m_in{c % 2}"], 16)

                    if not main:
                        sp.dma_start(xt[:], x[after]).then_inc(s_["x_in"], 16)
                    if main:
                        for n in range(NRAW if split else NRING):
                            load_chunk(n)
                        stack_out(0)
                        for i in range(QC + 1):
                            if i < QC:
                                stack_out(i + 1)
                            if i <= NQ:
                                stack_in(i)
                    if ssm is not None:
                        for i in range(QC + 1 if main else 0):
                            sp.wait_ge(s_[f"stk_out{i}"], 16)
                        sp.dma_start(cxf, ctx_t[ssm]).then_inc(s_["ctx_in"], 16)
                        sp.dma_start(dtw[0:DR], dt_w).then_inc(s_["dtw_in"], 16)
                    if main:
                        for n in range(NRAW, NPAIR):
                            if split:
                                load_chunk(n)
                        for c in range(QC):
                            maxima(c)
                            if c and c + NQ < QC + 1:
                                stack_in(c + NQ)
                        for odd in range(2):
                            sp.wait_ge(s_["on_lo"], G1 - 1 + odd)
                            for j in range(R1):
                                r0 = HD1 * (R1 * odd + j)
                                sp.dma_start(ot[r0:r0 + HD1],
                                             onp[32 * j:32 * j + HD1, odd]).then_inc(s_["ot_in"], 16)
                    if ssm is not None:
                        sp.wait_ge(s_["b_free"], B_SSM + EC + 1)
                        sp.dma_start(xd_d, xd[DR:DR + 2 * DS]).then_inc(s_["xd_out"], 16)
                    if main:
                        for n in range(ring, len(CHUNKS)):
                            load_chunk(n)
                            if n - ring == CHUNK_AT["wo", 3]:
                                sp.wait_ge(s_["a_free"], A_HT3)
                                sp.dma_start(be2s[0:NEXP], be2).then_inc(s_["be2_in"], 16)
                            if n - ring == CHUNK_AT["w1", 0] and after is not None:
                                sp.wait_ge(s_["x_added"], T)
                                sp.dma_start(xt[:], x[after]).then_inc(s_["x_in"], 16)
                        if split:
                            sp.wait_ge(s_["ch_lo"], len(CHUNKS))
                            for n in range(len(CHUNKS) - NRAW, len(CHUNKS)):
                                store_pair(n)
                            for k in range(NPAIR):
                                sp.wait_ge(s_[f"pair_out{k}"], 16 * len(range(k, len(CHUNKS), NPAIR)))
                        for t in range(T):
                            sp.wait_ge(s_["a_free"], a_expert(NEXP - 1) + t + 1)
                            sp.dma_start(out[b, :, t], hid[:, t]).then_inc(s_["y_out"], 16)
                        sp.wait_ge(s_["y_out"], 16 * T)

                @block.tensor
                def _(pe):
                    A, Bn = Count(s_["a_full"]), Count(s_["b_full"])

                    def bank_a():
                        if A.n >= 2:
                            pe.wait_ge(s_["a_free"], a_before(A.n))
                        return bank_a_at(A.n)

                    def bank_b():
                        if Bn.n >= 2:
                            pe.wait_ge(s_["b_free"], Bn.n - 1)
                        return bank_b_at(Bn.n)

                    def to_features(rows):
                        for k in range(KC):
                            dst = bank_a()
                            pe.wait_ge(s_["ln_rows"], rows)
                            for t in range(T):
                                last = nc.tensor.transpose(dst[:, P * t:P * (t + 1)],
                                                           xn[:, t, P * k:P * (k + 1)], identf[:])
                            last.then_inc(*A.one())

                    def feat(k, t=None):
                        c = slice(0, S) if t is None else slice(P * t, P * (t + 1))
                        return lambda part: ht[:, part, k, c]

                    if main:
                        for m in [QC] + list(range(QC)):
                            dst = bank_b()[:, 0]
                            for k in range(KC):
                                last = pe3(dst, lambda q: wqkv[:, q, k, P * m:P * (m + 1)], feat(k),
                                           k == 0, k == KC - 1)
                            last.then_inc(*Bn.one())
                            if m == QC:
                                dst = bank_a()
                                for t in range(T):
                                    for k in range(KC):
                                        last = pe3(dst[:, P * t:P * (t + 1)], feat(k, t),
                                                   lambda q: wqkv[:, q, k, 640:768], k == 0, k == KC - 1)
                                last.then_inc(*A.one())

                        def score_rows(i):
                            c, h, t = i // (HPC * T), i // T % HPC, i % T
                            dst = bank_a()
                            if i % (HPC * T) == 0:
                                pe.wait_ge(s_[f"stk_in{c % NQ}"], 16 * NS * (c // NQ + 1))
                            nc.tensor.matmul(dst, qstack(c)[0:KM, h, P * t:P * (t + 1)],
                                             kst[0:KM, (HPC * c + h) // R1],
                                             start=True, stop=True).then_inc(*A.one())

                        def score_cols(n, r2):
                            g, kt = n // T, n % T
                            c = R1 * g // HPC
                            dst = bank_b()
                            if n % JC == 0 and r2 == 0:
                                pe.wait_ge(s_[f"m_in{c % 2}"], 48 * (c // 2 + 1))
                            for r in range(2):
                                last = nc.tensor.matmul(
                                    dst[:, r], kst[0:KM + 3, g, P * kt:P * (kt + 1)],
                                    qstack(c)[0:KM + 3, R1 * g + 2 * r2 + r - HPC * c],
                                    start=True, stop=True)
                            last.then_inc(*Bn.one())

                        def key_sums(n):
                            g, kt = n // T, n % T
                            if kt == 0 and g >= 2:
                                pe.wait_ge(s_["o_free_norm"], g - 1)
                            pe.wait_ge(s_["b_free"], B_SC1 + 2 * n + 2)
                            for r in range(R1):
                                last = nc.tensor.matmul(PS[32 * r:32 * r + 32, 6 + g % 2], vaug[:, kt, g],
                                                        pt1[:, kt % 2, r], start=kt == 0, stop=kt == T - 1)
                            last.then_inc(s_["pv1"], 1)

                        pe.wait_ge(s_["kst_in"], 16 * NS)
                        pe.wait_ge(s_["a_free"], A_V1 + 1)
                        pe.wait_ge(s_["ones"], 2)
                        for j in range(JCOLS + T * G1 + 1):
                            n = j - JCOLS
                            rows = list(range(JROWS * j, JROWS * (j + 1))) if j < JC * QC else []
                            turn_maxima = j % JC == 0 and 0 < j <= JC * QC
                            for r2 in range(2):
                                if rows and not turn_maxima:
                                    score_rows(rows.pop(0))
                                if 0 <= n < T * G1:
                                    score_cols(n, r2)
                            if turn_maxima:
                                dst = bank_a()
                                pe.wait_ge(s_["a_free"], A.n)
                                nc.tensor.transpose(dst[0:HPC * T, 0:P], nm1[:, (j // JC - 1) % 2],
                                                    identf[:]).then_inc(*A.one())
                            while len(rows) > 1:
                                score_rows(rows.pop(0))
                            if 0 <= n - 1 < T * G1:
                                key_sums(n - 1)
                            if rows:
                                score_rows(rows.pop(0))
                    def in_project():
                        pe.wait_ge(s_["cx_lo"], 1)
                        for e in range(EC):
                            dst = bank_b()[:, 0]
                            for k in range(DM // P):
                                last = pe3(dst, lambda q: inw[:, q, k, P * e:P * (e + 1)],
                                           lambda q: cx[:, q, k], k == 0, k == DM // P - 1)
                            last.then_inc(*Bn.one())

                    def x_project():
                        dst = bank_b()[:, 0]
                        pe.wait_ge(s_["u_done"], EC)
                        for e in range(EC):
                            last = nc.tensor.matmul(dst[0:DR + 2 * DS], xpw[:, e], us[:, e],
                                                    start=e == 0, stop=e == EC - 1)
                        last.then_inc(*Bn.one())

                    def dt_project(e):
                        dst = bank_b()[:, 0]
                        pe.wait_ge(s_["b_free"], B_SSM + EC + 1)
                        pe.wait_ge(s_["dtw_in"], 16)
                        nc.tensor.matmul(dst, dtw[0:DR, P * e:P * (e + 1)], xd[0:DR],
                                         start=True, stop=True).then_inc(*Bn.one())

                    if ssm is not None:
                        in_project()
                    if main:
                        for t in range(T):
                            dst = bank_a()
                            pe.wait_ge(s_["ot_in"], 16 * 2 * R1)
                            for k in range(KC):
                                last = pe3(dst, lambda q: ot[:, q, k, P * t:P * (t + 1)],
                                           lambda q: wout[:, q, k], k == 0, k == KC - 1)
                            last.then_inc(*A.one())
                    if ssm is not None:
                        x_project()
                        for e in range(2):
                            dt_project(e)
                    if main:
                        for t in range(T):
                            dst = bank_a()
                            pe.wait_ge(s_["gated"], EC)
                            for e in range(EC):
                                last = nc.tensor.transpose(dst[:, P * e:P * (e + 1)],
                                                           ys[:, e, P * t:P * (t + 1)], identf[:])
                            last.then_inc(*A.one())
                    if ssm is not None:
                        for e in range(2, EC):
                            dt_project(e)
                    if not main:
                        to_features(ROWS_AFTER)
                        for i in range(NUNIT):
                            s, u = divmod(i, NU)
                            pe.wait_ge(s_["prod_done"], i + 1)
                            for j in range(NE):
                                last = nc.tensor.matmul(PS[:, Y_BANKS[NE * u + j]], identf[:], bx_at(i)[:, j],
                                                        start=s == 0, stop=s == DS - 1)
                            last.then_inc(s_["y_acc"], 1)
                        return
                    to_features(ROWS_XN)

                    def project(s):
                        g = s // G2
                        if s == 0:
                            pe.wait_ge(s_["ht_lo"], KC)
                        if s % G2 == 0:
                            n = CHUNK_AT["v", g]
                            chunk_there(pe, n)
                            for t in range(T):
                                dst = bank_a()
                                for k in range(KC):
                                    last = pe3(dst, feat(k, t), lambda q: pair[:, n % ring, q, D * k:D * (k + 1)],
                                               k == 0, k == KC - 1)
                                last.then_inc(*A.one())
                        n = CHUNK_AT["qk", s // 2]
                        chunk_there(pe, n)
                        for w in range(2):
                            dst = bank_a()
                            o = P * (2 * (s % 2) + w)
                            for k in range(KC):
                                last = pe3(dst, lambda q: pair[:, n % ring, q, D * k + o:D * k + o + P],
                                           feat(k), k == 0, k == KC - 1)
                            last.then_inc(*A.one())

                    def turn(h, kt):
                        pe.wait_ge(s_["p_norm"], h + 1)
                        dst = bank_a()
                        for t in range(kt, T):
                            last = nc.tensor.matmul(dst[:, P * t:P * (t + 1)], pf[:, t, P * kt:P * (kt + 1)],
                                                    dg[:, t], start=True, stop=True)
                        last.then_inc(*A.one())

                    def scores(h):
                        pe.wait_ge(s_["rope_lo"], 2 * (h + 1))
                        for u in range(2):
                            dst = bank_b()
                            for j in range(2):
                                t = 2 * u + j
                                pe3(dst[:, j, 0:P * (t + 1)], lambda q: qr[:, h % 2, 0, q, P * t:P * (t + 1)],
                                    lambda q: qr[:, h % 2, 1, q, 0:P * (t + 1)], True, False)
                                last = nc.tensor.matmul(dst[:, j, P * t:P * (t + 1)], identb[:], causb[:],
                                                        start=False, stop=True)
                            last.then_inc(*Bn.one())

                    def values(h):
                        if h == 0:
                            pe.wait_ge(s_["o_free_norm"], G1)
                        else:
                            pe.wait_ge(s_["o_free_head"], h)
                        g, hh = h // G2, h % G2
                        pe.wait_ge(s_["a_free"], A_AT["v", g, T - 1] + 1)
                        for kt in range(T):
                            pe.wait_ge(s_["a_free"], A_AT["turn", h, kt] + 1)
                            last = pe3(PS[:, 7, P * kt:S],
                                       lambda q: vp[:, g % 2, q, kt, P * hh:P * (hh + 1)],
                                       lambda q: pt[:, q, kt, P * kt:S], kt == 0, kt == T - 1)
                        last.then_inc(s_["o_full"], 1)

                    def project_out(g, t):
                        n = CHUNK_AT["wo", g]
                        chunk_there(pe, n)
                        pe.wait_ge(s_["o_lo"], G2 * (g + 1))
                        dst = bank_a()
                        for h in range(G2):
                            last = pe3(dst, lambda q: op[:, q, h, P * t:P * (t + 1)],
                                       lambda q: pair[:, n % ring, q, D * h:D * (h + 1)],
                                       h == 0, h == G2 - 1)
                        last.then_inc(*A.one())

                    def project_out_last(g):
                        n = CHUNK_AT["wo", g]
                        chunk_there(pe, n)
                        pe.wait_ge(s_["o_lo"], G2 * (g + 1) - 1)

                        def add_head(dst, t, h):
                            return pe3(dst, lambda q: op[:, q, h, P * t:P * (t + 1)],
                                       lambda q: pair[:, n % ring, q, D * h:D * (h + 1)], h == 0, h == G2 - 1)

                        for t in range(T - 1):
                            pe.wait_ge(s_["a_free"], a_before(A.n + t))
                            for h in range(G2 - 1):
                                add_head(bank_a_at(A.n + t), t, h)
                        pe.wait_ge(s_["o_lo"], G2 * (g + 1))
                        for t in range(T - 1):
                            add_head(bank_a_at(A.n), t, G2 - 1).then_inc(*A.one())
                        dst = bank_a()
                        for h in range(G2):
                            last = add_head(dst, T - 1, h)
                        last.then_inc(*A.one())

                    for s in range(STEPS):
                        if s < H2:
                            project(s)
                        if s >= 3:
                            values(s - 3)
                        for t in range(T):
                            if 2 <= s < H2 + 2:
                                turn(s - 2, t)
                            if t == 0 and 1 <= s <= H2:
                                scores(s - 1)
                            if s in WO_STEP and s < STEPS - 1:
                                project_out(WO_STEP[s], t)
                    project_out_last(H2 // G2 - 1)

                    to_features(ROWS_MOE)
                    dst = bank_a()
                    pe.wait_ge(s_["a_free"], A_HT3 + KC)
                    for t in range(T):
                        for k in range(KC):
                            last = nc.tensor.matmul(dst[:, NEXP * t:NEXP * (t + 1)],
                                                    h2f[:, k, P * t:P * (t + 1)], col("w_gate", NEXP * k, NEXP),
                                                    start=k == 0, stop=k == KC - 1)
                    last.then_inc(*A.one())

                    def expert_in(e):
                        n = CHUNK_AT["w1", e]
                        chunk_there(pe, n)
                        pe.wait_ge(s_["ht_lo"], 2 * KC)
                        for i in range(KC):
                            dst = bank_b()[:, 0]
                            for k in range(KC):
                                last = pe3(dst, lambda q: pair[:, n % ring, q, D * k + P * i:D * k + P * (i + 1)],
                                           feat(k), k == 0, k == KC - 1)
                            last.then_inc(*Bn.one())

                    def expert_out(e):
                        n = CHUNK_AT["w2", e]
                        chunk_there(pe, n)
                        pe.wait_ge(s_["hm_lo"], KC * (e + 1))
                        for t in range(T):
                            dst = bank_a()
                            for i in range(KC):
                                last = pe3(dst, lambda q: hm[:, e % 2, q, i, P * t:P * (t + 1)],
                                           lambda q: pair[:, n % ring, q, D * i:D * (i + 1)],
                                           i == 0, i == KC - 1)
                            last.then_inc(*A.one())

                    expert_in(0)
                    dst = bank_a()
                    pe.wait_ge(s_["comb"], 1)
                    for t in range(T):
                        last = nc.tensor.transpose(dst[0:NEXP, P * t:P * (t + 1)], gt[:, 7, t], identf[:])
                    last.then_inc(*A.one())
                    pe.wait_ge(s_["be2_in"], 16)
                    for t in range(T):
                        dst = bank_a()
                        pe.wait_ge(s_["a_free"], A_COMB + 1)
                        nc.tensor.matmul(dst, combt[0:NEXP, t], be2s[0:NEXP], start=True,
                                         stop=True).then_inc(*A.one())
                    for e in range(NEXP):
                        if e + 1 < NEXP:
                            expert_in(e + 1)
                        elif after is not None:
                            to_features(ROWS_AFTER)
                        expert_out(e)
                    assert A.n == a_expert(NEXP - 1) + T and Bn.n == B_EXP + KC * NEXP

                @block.scalar
                def _(act):
                    Bf, own = Count(s_["b_free"]), Count(s_["act_own"])

                    def inv_root(stats, w=1):
                        act.wait_ge(s_["ln_stats"], stats)
                        nc.scalar.activation(ra[:, 0:w], vv[:, 0:w], ACT.Ln).then_inc(*own.one())
                        act.wait_ge(*own.now())
                        nc.scalar.activation(rs[:, 0:w], ra[:, 0:w], ACT.Exp, scale=-0.5).then_inc(s_["ln_guess"], 1)

                    def pad_in(e):
                        src = full_b()
                        if e < 2:
                            act.wait_ge(s_["pad_zero"], 1)
                        nc.scalar.activation(xpad[:, e % 2, DC - 1:DC - 1 + S], src[:, 0],
                                             ACT.Copy).then_inc(*Bf.one())

                    def silu(e):
                        act.wait_ge(s_["conv_done"], e + 1)
                        nc.scalar.activation(us[:, e], acc[:, e % 2], ACT.Silu).then_inc(s_["u_done"], 1)

                    def softplus(e):
                        src = full_b()
                        k = e % 2
                        if e >= 2:
                            act.wait_ge(s_["delta_done"], e - 1)
                        nc.scalar.activation(spt[:, k, 0], src[:, 0], ACT.Abs, bias=col("dt_b", e)).then_inc(*own.one())
                        nc.scalar.activation(spt[:, k, 2], src[:, 0], ACT.Relu, bias=col("dt_b", e)).then_inc(*Bf.one())
                        act.wait_ge(*own.now())
                        nc.scalar.activation(spt[:, k, 1], spt[:, k, 0], ACT.Exp, scale=-1.0).then_inc(*own.one())
                        act.wait_ge(*own.now())
                        nc.scalar.activation(spt[:, k, 0], spt[:, k, 1], ACT.Ln, bias=col("one", 0)).then_inc(s_["sp_log"], 1)

                    def features_next():
                        for k in range(KC):
                            act.wait_ge(s_["a_full"], next_at + k + 1)
                            nc.scalar.activation(ht[:, 0, k], bank_a_at(next_at + k),
                                                 ACT.Copy).then_inc(s_["next_hi"], 1)

                    def chunk_hi(n):
                        act.wait_ge(s_[f"raw_in{n % 2}"], 16 * (n // 2 + 1))
                        if n >= NPAIR:
                            chunk_free(act, n - NPAIR)
                            act.wait_ge(s_[f"pair_out{n % NPAIR}"], 16 * (n // NPAIR))
                        nc.scalar.activation(pair[:, n % NPAIR, 0], raw[:, n % NRAW], ACT.Copy).then_inc(s_["ch_hi"], 1)

                    def full_b():
                        act.wait_ge(s_["b_full"], Bf.n + 1)
                        return bank_b_at(Bf.n)

                    if not main:
                        inv_root(STATS_AFTER)
                        act.wait_ge(s_["ctx_in"], 16)
                        nc.scalar.activation(cx[:, 0], cxf, ACT.Copy).then_inc(s_["cx_hi"], 1)
                        pad_in(0)
                        pad_in(1)
                    if main:
                        for i in range(QC + 1):
                            src = full_b()
                            if i >= 2:
                                act.wait_ge(s_["q_parts"], i - 1)
                            nc.scalar.activation(qf[:, i % 2], src[:, 0], ACT.Identity,
                                                 bias=col("bq1", i - 1) if i else col("bk1", 0)).then_inc(*Bf.one())
                            act.wait_ge(*Bf.now())
                            nc.scalar.activation(qparts(i)[:, 0], qf[:, i % 2], ACT.Copy).then_inc(s_["q_part"], 1)
                            act.wait_ge(s_["q_rest"], i + 1)
                            nc.scalar.activation(qparts(i)[:, 1], qres[:, i % 2], ACT.Copy).then_inc(s_["q_part"], 1)
                        for n in range(NPAIR if split else 0):
                            chunk_hi(n)

                        def out_hi(g):
                            act.wait_ge(s_["on_done"], g + 1)
                            nc.scalar.activation(onp[:, g % 2, 0, g // 2], on[:, g % 2], ACT.Copy).then_inc(s_["on_hi"], 1)

                        for g in range(G1):
                            for kt in range(T):
                                for r2 in range(2):
                                    src = full_b()
                                    if g == 0 and kt == 0 and r2 == 0:
                                        for i in range(QC + 1):
                                            act.wait_ge(s_[f"stk_out{i}"], 16)
                                    if r2 == 0 and T * g + kt >= 2:
                                        act.wait_ge(s_["pv1"], T * g + kt - 1)
                                    nc.scalar.activation(pt1[:, kt % 2, 2 * r2:2 * r2 + 2], src, ACT.Exp,
                                                         scale=SCALE1).then_inc(*Bf.one())
                                if kt == T - 1 and g:
                                    out_hi(g - 1)
                            if g == 0 and ssm is not None:
                                act.wait_ge(s_["ctx_in"], 16)
                                nc.scalar.activation(cx[:, 0], cxf, ACT.Copy).then_inc(s_["cx_hi"], 1)
                        if ssm is not None:
                            pad_in(0)
                            pad_in(1)
                        out_hi(G1 - 1)
                    if ssm is not None:
                        silu(0)
                        for e in range(2, EC):
                            pad_in(e)
                            silu(e - 1)
                        silu(EC - 1)
                    if main:
                        inv_root(STATS_GATE)
                    if ssm is not None:
                        src = full_b()
                        nc.scalar.activation(xd[0:DR + 2 * DS], src[0:DR + 2 * DS, 0], ACT.Copy).then_inc(*Bf.one())
                    if main:
                        for t in range(T):
                            act.wait_ge(s_["ln_rows"], ROWS_GATE - T + t + 1)
                            nc.scalar.activation(xn[:, t], xn[:, t], ACT.Silu).then_inc(s_["z_silu"], 1)
                    if ssm is not None:
                        softplus(0)
                        softplus(1)
                    if main:
                        inv_root(STATS_TWICE, 2)
                    if ssm is not None:
                        softplus(2)
                    if main:
                        for k in range(KC):
                            act.wait_ge(s_["a_free"], A_HT2 + k + 1)
                            nc.scalar.activation(ht[:, 0, k], h1f[:, k], ACT.Copy).then_inc(s_["ht_hi"], 1)
                    if ssm is not None:
                        softplus(3)
                        if not main:
                            features_next()
                        act.wait_ge(s_["xd_out"], 16)

                    def load_state(s):
                        if s >= 2:
                            act.wait_ge(s_["bx_done"], NU * (s - 1))
                            act.wait_ge(s_["prod_done"], NU * (s - 1))
                        nc.scalar.dma_start(bb[:, s % 2], xd_d[s:s + 1].to_broadcast([P, S])).then_inc(s_[f"b_in{s % 2}"], 16)
                        nc.scalar.dma_start(cb[:, s % 2],
                                            xd_d[DS + s:DS + s + 1].to_broadcast([P, S])).then_inc(s_[f"c_in{s % 2}"], 16)

                    def decays(step):
                        for i in scans[step]:
                            s, u = divmod(i, NU)
                            if i == 0:
                                act.wait_ge(s_["delta_done"], EC)
                                act.wait_ge(s_["du_done"], EC)
                                if main:
                                    act.wait_ge(s_["y_init"], EC)
                            if i >= 2:
                                act.wait_ge(s_["prod_done"], i - 1)
                            for j in range(NE):
                                e = NE * u + j
                                nc.scalar.activation(da[:, i % 2, j, 1:S], dl[:, e, 1:S], ACT.Exp,
                                                     scale=nega[:, DS * e + s:DS * e + s + 1]).then_inc(s_["da_done"], 1)

                    def load_states(step):
                        for i in scans[step]:
                            if i and i % NU == 0:
                                load_state(i // NU)

                    if ssm is not None:
                        load_state(0)
                    for s in range(STEPS):
                        decays(s)
                        if main and s < H2:
                            if s % G2 == 0:
                                for t in range(T):
                                    a = A_AT["v", s // G2, t]
                                    act.wait_ge(s_["a_full"], a + 1)
                                    nc.scalar.activation(vp[:, s // G2 % 2, 0, t], bank_a_at(a),
                                                         ACT.Copy).then_inc(s_["v_hi"], 1)
                        load_states(s + 1)
                        if not main:
                            continue
                        if 2 <= s < H2 + 2:
                            for kt in range(T):
                                a = A_AT["turn", s - 2, kt]
                                act.wait_ge(s_["a_full"], a + 1)
                                if s >= 3:
                                    act.wait_ge(s_["o_full"], s - 2)
                                nc.scalar.activation(pt[:, 0, kt, P * kt:S], bank_a_at(a)[:, P * kt:S],
                                                     ACT.Copy).then_inc(s_["pt_hi"], 1)
                        if s < H2:
                            for w in range(2):
                                act.wait_ge(s_["rope_f"], 2 * s + w + 1)
                                if s >= 2:
                                    act.wait_ge(s_["b_full"], B_SC2 + 2 * (s - 1))
                                nc.scalar.activation(qr[:, s % 2, w, 0], rp[:, w], ACT.Copy).then_inc(s_["rope_hi"], 1)
                        if s >= 3:
                            h = s - 3
                            act.wait_ge(s_["o_full"], h + 1)
                            if h:
                                act.wait_ge(s_["o_lo"], h)
                            nc.scalar.activation(of, PS[:, 7], ACT.Identity,
                                                 bias=col("bv2", h)).then_inc(s_["o_free_head"], 1)
                            act.wait_ge(s_["o_free_head"], h + 1)
                            if h >= G2 and h % G2 == 0:
                                act.wait_ge(s_["a_full"], A_AT["wo", h // G2 - 1, T - 1] + 1)
                            nc.scalar.activation(op[:, 0, h % G2], of, ACT.Copy).then_inc(s_["o_hi"], 1)
                        if 1 <= s <= H2:
                            h = s - 1
                            for u in range(2):
                                src = full_b()
                                act.wait_ge(s_["nmax2"], 2 * h + u + 1)
                                for j in range(2):
                                    t = 2 * u + j
                                    sem = (s_["exp2"], 1) if j == 0 else Bf.one()
                                    nc.scalar.activation(pf[:, t, 0:P * (t + 1)], src[:, j, 0:P * (t + 1)], ACT.Exp,
                                                         bias=nbs[:, t:t + 1], scale=SCALE2,
                                                         accum_out=sm[:, h % 2, t:t + 1]).then_inc(*sem)
                        for n in SPLIT_IN_STEP.get(s, []) if split else []:
                            chunk_hi(n)
                    if not main:
                        return
                    inv_root(STATS_MOE)
                    for k in range(KC):
                        act.wait_ge(s_["a_free"], A_HT3 + k + 1)
                        nc.scalar.activation(ht[:, 0, k], h2f[:, k], ACT.Copy).then_inc(s_["ht_hi"], 1)
                    for i in range(2):
                        act.wait_ge(s_["router_in"], i + 1)
                        nc.scalar.activation(gt[:, 1 + 2 * i], gt[:, 2 * i], ACT.Exp).then_inc(s_["router_exp"], 1)
                    act.wait_ge(s_["a_full"], A_LOGITS + 1)
                    act.wait_ge(s_["ht_lo"], 2 * KC)
                    for e in range(NEXP):
                        for i in range(KC):
                            src = full_b()
                            if e:
                                act.wait_ge(s_["hm_lo"], KC * (e - 1) + i + 1)
                            nc.scalar.activation(gf[:, i], src[:, 0], ACT.Gelu,
                                                 bias=col("be1", KC * e + i)).then_inc(*Bf.one())
                            if e >= 2:
                                act.wait_ge(s_["a_full"], a_expert(e - 2) + T)
                            act.wait_ge(*Bf.now())
                            nc.scalar.activation(hm[:, e % 2, 0, i], gf[:, i], ACT.Copy).then_inc(s_["hm_hi"], 1)
                        if e == 2 and after is not None:
                            inv_root(STATS_AFTER)
                        decays(STEPS + e)
                        if e + 1 < NEXP:
                            load_states(STEPS + 1 + e)
                        elif after is not None:
                            features_next()
                        for n in SPLIT_IN_EXPERT[e] if split else []:
                            chunk_hi(n)

                @block.gpsimd
                def _(pool):
                    def chunk_lo(n):
                        pool.wait_ge(s_["ch_hi"], n + 1)
                        nc.gpsimd.tensor_tensor(pair[:, n % NPAIR, 1], raw[:, n % NRAW], pair[:, n % NPAIR, 0],
                                                ALU.subtract).then_inc(s_["ch_lo"], 1)

                    def add_bias(dst, o, rows):
                        if rows:
                            pool.wait_ge(s_["ln_rows"], rows)
                        for t in range(T):
                            nc.gpsimd.tensor_tensor(dst[:, t], dst[:, t], brow[:, o:o + D],
                                                    ALU.add).then_inc(s_["bias_in"], 1)

                    def features_lo(f32, n):
                        for k in range(KC - 1):
                            pool.wait_ge(s_["ht_hi"], KC * n + k + 1)
                            nc.gpsimd.tensor_tensor(ht[:, 1, k], f32[:, k], ht[:, 0, k],
                                                    ALU.subtract).then_inc(s_["ht_lo"], 1)

                    if main:
                        nc.gpsimd.memset(vaug[:, :, :, HD1:2 * HD1], 1.0).then_inc(s_["ones"], 1)
                        pool.wait_ge(s_["ones"], 1)
                        nc.gpsimd.memset(kst[KM:KM + 32], 1.0).then_inc(s_["ones"], 1)
                        pool.wait_ge(s_["ones"], 2)
                        add_bias(xt, 0, 0)
                        for n in range(NPAIR if split else 0):
                            chunk_lo(n)
                    if ssm is not None:
                        pool.wait_ge(s_["cx_hi"], 1)
                        nc.gpsimd.tensor_tensor(cx[:, 1], cxf, cx[:, 0], ALU.subtract).then_inc(s_["cx_lo"], 1)
                    if main:
                        for g in range(G1):
                            pool.wait_ge(s_["on_hi"], g + 1)
                            nc.gpsimd.tensor_tensor(onp[:, g % 2, 1, g // 2], on[:, g % 2], onp[:, g % 2, 0, g // 2],
                                                    ALU.subtract).then_inc(s_["on_lo"], 1)
                        features_lo(h1f, 0)
                        add_bias(hid, D, ROWS_HID)

                    def add_product(i):
                        u = i % NU
                        pool.wait_ge(s_["prod_done"], i + 1)
                        if i >= NU:
                            pool.wait_ge(s_["y_acc"], i - NU + 1)
                        y = ys[:, NE * u:NE * (u + 1)]
                        nc.gpsimd.tensor_tensor(y, y, bx_at(i), ALU.add).then_inc(s_["y_acc"], 1)

                    def inputs(units):
                        for i in units:
                            s, u = divmod(i, NU)
                            if main and i >= 2:
                                add_product(i - 2)
                            pool.wait_ge(s_[f"b_in{s % 2}"], 16 * (s // 2 + 1))
                            if i == 0:
                                pool.wait_ge(s_["du_done"], EC)
                                if main:
                                    pool.wait_ge(s_["y_init"], EC)
                            if i >= n_bx:
                                pool.wait_ge(s_["y_acc"], i - n_bx + 1)
                            nc.gpsimd.tensor_tensor(
                                bx_at(i), du[:, NE * u:NE * (u + 1)],
                                bb[:, s % 2].unsqueeze(1).to_broadcast([P, NE, S]),
                                ALU.mult).then_inc(s_["bx_done"], 1)

                    for s in range(STEPS):
                        inputs(scans[s][:1])
                        if main and s < H2 and not split:
                            for w in range(2):
                                pool.wait_ge(s_["rope_in"], 2 * s + w + 1)
                                pool.wait_ge(s_["a_free"], A_AT["qk", s, w] + 1)
                                nc.gpsimd.tensor_tensor(halves(rp[:, w]), halves(rp[:, w]), rother[w],
                                                        ALU.add).then_inc(s_["rope_f"], 1)
                        for n in SPLIT_IN_STEP.get(s - 1, []) if split else []:
                            chunk_lo(n)
                        inputs(scans[s][1:])
                        if not main:
                            continue
                        if s < H2:
                            for w in range(2):
                                pool.wait_ge(s_["rope_hi"], 2 * s + w + 1)
                                nc.gpsimd.tensor_tensor(qr[:, s % 2, w, 1], rp[:, w], qr[:, s % 2, w, 0],
                                                        ALU.subtract).then_inc(s_["rope_lo"], 1)
                        if s >= 3:
                            h = s - 3
                            pool.wait_ge(s_["o_hi"], h + 1)
                            nc.gpsimd.tensor_tensor(op[:, 1, h % G2], of, op[:, 0, h % G2],
                                                    ALU.subtract).then_inc(s_["o_lo"], 1)
                    if not main:
                        return
                    for n in SPLIT_IN_STEP[STEPS - 1] if split else []:
                        chunk_lo(n)
                    pool.wait_ge(s_["ln_rows"], ROWS_MOE)
                    for t in range(T):
                        nc.gpsimd.tensor_tensor(hid[:, t], hid[:, t], xt[:, t], ALU.add).then_inc(s_["x_added"], 1)
                    features_lo(h2f, 1)
                    for e in range(NEXP):
                        for i in range(KC):
                            pool.wait_ge(s_["hm_hi"], KC * e + i + 1)
                            nc.gpsimd.tensor_tensor(hm[:, e % 2, 1, i], gf[:, i], hm[:, e % 2, 0, i],
                                                    ALU.subtract).then_inc(s_["hm_lo"], 1)
                        inputs(scans[STEPS + e])
                        for n in SPLIT_IN_EXPERT[e] if split else []:
                            chunk_lo(n)

                    if main and ssm is not None:
                        add_product(NUNIT - 2)
                        add_product(NUNIT - 1)

                @block.vector
                def _(dve):
                    Af, own = Count(s_["a_free"]), Count(s_["dve_own"])
                    stats, rows = Count(s_["ln_stats"]), Count(s_["ln_rows"])
                    norms = [0]

                    def full_a():
                        dve.wait_ge(s_["a_full"], Af.n + 1)
                        return bank_a_at(Af.n)

                    def features_next():
                        for k in range(KC):
                            src = full_a()
                            dve.wait_ge(s_["next_hi"], k + 1)
                            nc.vector.tensor_tensor(ht[:, 1, k], src, ht[:, 0, k], ALU.subtract).then_inc(*Af.one())

                    def norm_tile(src, t):
                        nc.vector.bn_stats(bst[:, t], src[:, t]).then_inc(*own.one())

                    def zero_pads():
                        nc.vector.memset(xpad[:, :, 0:DC - 1], 0.0).then_inc(s_["pad_zero"], 1)

                    def add_tile(dst, t):
                        src = full_a()
                        nc.vector.tensor_tensor(dst[:, t], src, dst[:, t], ALU.add).then_inc(*Af.one())
                        dve.wait_ge(*Af.now())
                        norm_tile(dst, t)

                    def norm_stats(twice=False):
                        dve.wait_ge(*own.now())
                        for t in range(T):
                            nc.vector.bn_aggr(bmv[:, t], bst[:, t]).then_inc(*own.one())
                        dve.wait_ge(*own.now())
                        nc.vector.tensor_scalar(vv[:, 0], bmv[:, :, 1], EPS, None, ALU.add).then_inc(*stats.one())
                        if twice:
                            nc.vector.tensor_scalar(vv[:, 1], bmv[:, :, 1], 1.0 + EPS, EPS * EPS, ALU.mult,
                                                    ALU.add).then_inc(*stats.one())

                    def norm_root(w=1):
                        norms[0] += 1
                        dve.wait_ge(s_["ln_guess"], norms[0])
                        nc.vector.tensor_tensor(rn[:, 0:w], rs[:, 0:w], rs[:, 0:w], ALU.mult).then_inc(*own.one())
                        dve.wait_ge(*own.now())
                        nc.vector.tensor_tensor(rn[:, 0:w], vv[:, 0:w], rn[:, 0:w], ALU.mult).then_inc(*own.one())
                        dve.wait_ge(*own.now())
                        nc.vector.tensor_scalar(rn[:, 0:w], rn[:, 0:w], -0.5, 1.5, ALU.mult,
                                                ALU.add).then_inc(*own.one())
                        dve.wait_ge(*own.now())
                        nc.vector.tensor_tensor(rs[:, 0:w], rs[:, 0:w], rn[:, 0:w], ALU.mult).then_inc(*own.one())
                        dve.wait_ge(*own.now())

                    def norm_rows(src, dst, k=0):
                        for t in range(T):
                            nc.vector.tensor_scalar(dst[:, t], src[:, t], bmv[:, t, 0:1], rs[:, k, t:t + 1],
                                                    ALU.subtract, ALU.mult).then_inc(*rows.one())

                    def scaled_features(dst, name):
                        for k in range(KC):
                            src = full_a()
                            nc.vector.tensor_scalar(dst[:, k], src, col(name + "_w", k), col(name + "_b", k),
                                                    ALU.mult, ALU.add).then_inc(*Af.one())

                    def last_features_lo(f32, n):
                        dve.wait_ge(s_["ht_hi"], KC * (n + 1))
                        nc.vector.tensor_tensor(ht[:, 1, KC - 1], f32[:, KC - 1], ht[:, 0, KC - 1],
                                                ALU.subtract).then_inc(s_["ht_lo"], 1)

                    if main:
                        for i in range(QC + 1):
                            dve.wait_ge(s_["q_part"], 2 * i + 1)
                            if i >= 2:
                                dve.wait_ge(s_["q_parts"], i - 1)
                            nc.vector.tensor_tensor(qres[:, i % 2], qf[:, i % 2], qparts(i)[:, 0],
                                                    ALU.subtract).then_inc(s_["q_rest"], 1)
                            dve.wait_ge(s_["q_part"], 2 * i + 2)
                            nc.vector.tensor_tensor(qparts(i)[:, 2], qres[:, i % 2], qparts(i)[:, 1],
                                                    ALU.subtract).then_inc(s_["q_parts"], 1)

                        src = full_a()
                        for t in range(T):
                            sem = Af.one() if t == T - 1 else own.one()
                            nc.vector.tensor_tensor(
                                vaug[:, t, :, 0:HD1], src[:, P * t:P * (t + 1)].rearrange("p (g d) -> p g d", d=HD1),
                                brow[:, 2 * D:2 * D + P].rearrange("p (g d) -> p g d", d=HD1),
                                ALU.add).then_inc(*sem)

                        def normalise(g, r):
                            turned = rec[:, g % 2].rearrange("p (b c) -> p b c", c=32)
                            if r == 0:
                                dve.wait_ge(s_["pv1"], T * (g + 1))
                                nc.vector.transpose(rec[:, g % 2], PS[:, 6 + g % 2]).then_inc(s_["o_free_norm"], 1)
                            elif r == 1:
                                dve.wait_ge(s_["o_free_norm"], g + 1)
                                nc.vector.reciprocal(rcol[:].unsqueeze(2), turned[:, :, HD1:HD1 + 1]).then_inc(*own.one())
                            elif r == 2:
                                dve.wait_ge(*own.now())
                                nc.vector.tensor_tensor(turned, turned,
                                                        rcol[:].unsqueeze(2).to_broadcast([P, S // 32, 32]),
                                                        ALU.mult).then_inc(*own.one())
                            else:
                                dve.wait_ge(*own.now())
                                if g >= 2:
                                    dve.wait_ge(s_["on_lo"], g - 1)
                                nc.vector.transpose(on[:, g % 2], rec[:, g % 2]).then_inc(s_["on_done"], 1)

                        def split_maxima(c):
                            src = full_a()
                            n = HPC * T
                            if c >= 2:
                                dve.wait_ge(s_[f"m_in{c % 2}"], 48 * (c // 2))
                            nc.vector.tensor_copy(mpt[0:n, c % 2, 0], src[0:n, 0:P]).then_inc(*own.one())
                            dve.wait_ge(*own.now())
                            nc.vector.tensor_tensor(mf[0:n, 0], src[0:n, 0:P], mpt[0:n, c % 2, 0],
                                                    ALU.subtract).then_inc(*Af.one())
                            dve.wait_ge(*Af.now())
                            nc.vector.tensor_copy(mpt[0:n, c % 2, 1], mf[0:n, 0]).then_inc(*own.one())
                            dve.wait_ge(*own.now())
                            nc.vector.tensor_tensor(mf[0:n, 1], mf[0:n, 0], mpt[0:n, c % 2, 1],
                                                    ALU.subtract).then_inc(*own.one())
                            dve.wait_ge(*own.now())
                            nc.vector.tensor_copy(mpt[0:n, c % 2, 2], mf[0:n, 1]).then_inc(s_["m_parts"], 1)

                        norm_at = JCOLS + T + 1
                        for j in range(norm_at + T * (G1 - 1) + 2):
                            if j == norm_at and ssm is not None:
                                for i in range(QC + 1):
                                    dve.wait_ge(s_[f"stk_out{i}"], 16)
                                zero_pads()
                            if j % JC == 0 and 0 < j <= JC * QC:
                                split_maxima(j // JC - 1)
                            g, r = divmod(j - norm_at, T)
                            for q in range(2):
                                if j < JC * QC:
                                    for i in range(JROWS // 2):
                                        src = full_a()
                                        i += JROWS * j + JROWS // 2 * q
                                        c, i = divmod(i, HPC * T)
                                        nc.vector.tensor_reduce(nm1[:, c % 2, i:i + 1], src, AX.X, ALU.max,
                                                                negate=True).then_inc(*Af.one())
                                if g >= 0 and r < 2:
                                    normalise(g, 2 * r + q)

                    def conv(e):
                        dve.wait_ge(s_["b_free"], B_SSM + e + 1)
                        if e >= 2:
                            dve.wait_ge(s_["u_done"], e - 1)
                        a = acc[:, e % 2]
                        nc.vector.tensor_scalar(a, xpad[:, e % 2, 0:S], col("conv_w", DC * e), col("conv_b", e),
                                                ALU.mult, ALU.add).then_inc(*own.one())
                        for j in range(1, DC):
                            dve.wait_ge(*own.now())
                            sem = (s_["conv_done"], 1) if j == DC - 1 else own.one()
                            nc.vector.scalar_tensor_tensor(a, xpad[:, e % 2, j:j + S], col("conv_w", DC * e + j),
                                                           a, ALU.mult, ALU.add).then_inc(*sem)

                    def delta(e):
                        dve.wait_ge(s_["sp_log"], e + 1)
                        k = e % 2
                        nc.vector.tensor_tensor(dl[:, e], spt[:, k, 2], spt[:, k, 0],
                                                ALU.add).then_inc(s_["delta_done"], 1)
                        dve.wait_ge(s_["delta_done"], e + 1)
                        nc.vector.tensor_tensor(du[:, e], dl[:, e], us[:, e], ALU.mult).then_inc(s_["du_done"], 1)

                    if ssm is not None:
                        if not main:
                            dve.wait_ge(s_["x_in"], 16)
                            for t in range(T):
                                norm_tile(xt, t)
                            norm_stats()
                            norm_root()
                            norm_rows(xt, xn)
                            zero_pads()
                        for e in range(EC):
                            conv(e)
                    if main:
                        dve.wait_ge(s_["bias_in"], T)
                        for t in range(T):
                            add_tile(xt, t)
                        norm_stats()
                        norm_root()
                        norm_rows(xt, xn)
                        if ssm is not None:
                            nc.vector.memset(da[:, :, :, 0:1], 0.0).then_inc(*own.one())
                        for e in range(EC):
                            dve.wait_ge(s_["z_silu"], e + 1)
                            nc.vector.tensor_tensor(ys[:, e], ys[:, e], xn[:, e], ALU.mult).then_inc(s_["gated"], 1)
                        for t in range(T):
                            add_tile(xt, t)
                        norm_stats(twice=True)
                    if ssm is not None:
                        delta(0)
                        delta(1)
                    if main:
                        norm_root(2)
                        norm_rows(xt, xn, 1)
                        scaled_features(h1f, "ln1")
                        norm_rows(xt, hid)
                        last_features_lo(h1f, 0)
                    if ssm is not None:
                        delta(2)
                        if not main:
                            nc.vector.memset(da[:, :, :, 0:1], 0.0).then_inc(*own.one())
                        for e in range(EC if main else 0):
                            nc.vector.tensor_scalar(ys[:, e], us[:, e], col("ssm_d", e), None,
                                                    ALU.mult).then_inc(s_["y_init"], 1)
                        delta(3)
                        if not main:
                            features_next()

                    def scan(i):
                        s = i // NU
                        k = i % 2
                        dve.wait_ge(s_["bx_done"], i + 1)
                        dve.wait_ge(s_["da_done"], NE * (i + 1))
                        flat = bx_at(i).rearrange("p e n -> p (e n)")
                        nc.vector.tensor_tensor_scan(flat, da[:, k].rearrange("p e n -> p (e n)"), flat, 0.0,
                                                     ALU.mult, ALU.add).then_inc(*own.one())
                        dve.wait_ge(*own.now())
                        dve.wait_ge(s_[f"c_in{s % 2}"], 16 * (s // 2 + 1))
                        nc.vector.tensor_tensor(bx_at(i), bx_at(i), cb[:, s % 2].unsqueeze(1).to_broadcast([P, NE, S]),
                                                ALU.mult).then_inc(s_["prod_done"], 1)

                    def diagonals(h):
                        dve.wait_ge(s_["b_free"], B_SC2 + 2 * (h + 1))
                        nc.vector.reciprocal(rc[:], sm[:, h % 2]).then_inc(*own.one())
                        dve.wait_ge(*own.now())
                        nc.vector.tensor_tensor(dg, identf[:].unsqueeze(1).to_broadcast([P, T, P]),
                                                rc[:].unsqueeze(2).to_broadcast([P, T, P]),
                                                ALU.mult).then_inc(s_["p_norm"], 1)

                    def v_lo(g, units):
                        for t in range(T):
                            if t == 1 and len(units) > 1:
                                scan(units.pop(0))
                            src = full_a()
                            dve.wait_ge(s_["v_hi"], T * g + t + 1)
                            nc.vector.tensor_tensor(vp[:, g % 2, 1, t], src, vp[:, g % 2, 0, t],
                                                    ALU.subtract).then_inc(*Af.one())

                    def rope_in(s, w):
                        src = full_a()
                        if s:
                            dve.wait_ge(s_["rope_lo"], 2 * (s - 1) + w + 1)
                        bias = col("bk2" if w else "bq2", s)
                        nc.vector.scalar_tensor_tensor(rp[:, w], src, bias, ropet[:, 0], ALU.add,
                                                       ALU.mult).then_inc(*own.one())
                        half = P // 2
                        for a, z in ((0, half), (half, 0)):
                            sem = Af.one() if z == 0 else (s_["rope_in"], 1)
                            nc.vector.scalar_tensor_tensor(
                                rother[w][a:a + half], halves(src)[z:z + half], bias[z:z + half],
                                halves(ropet[:, 1])[z:z + half], ALU.add, ALU.mult).then_inc(*sem)
                        if split:
                            dve.wait_ge(s_["rope_in"], 2 * s + w + 1)
                            dve.wait_ge(*Af.now())
                            nc.vector.tensor_tensor(halves(rp[:, w]), halves(rp[:, w]), rother[w],
                                                    ALU.add).then_inc(s_["rope_f"], 1)

                    def turned_lo(h, kt):
                        src = full_a()
                        dve.wait_ge(s_["pt_hi"], T * h + kt + 1)
                        nc.vector.tensor_tensor(pt[:, 1, kt, P * kt:S], src[:, P * kt:S],
                                                pt[:, 0, kt, P * kt:S], ALU.subtract).then_inc(*Af.one())

                    def row_maxima(h):
                        for u in range(2):
                            dve.wait_ge(s_["b_full"], B_SC2 + 2 * h + u + 1)
                            src = bank_b_at(B_SC2 + 2 * h + u)
                            for j in range(2):
                                t = 2 * u + j
                                nc.vector.tensor_reduce(nmx[:, t:t + 1], src[:, j, 0:P * (t + 1)], AX.X, ALU.max,
                                                        negate=True).then_inc(*own.one())
                            dve.wait_ge(*own.now())
                            nc.vector.tensor_scalar(nbs[:, 2 * u:2 * u + 2], nmx[:, 2 * u:2 * u + 2], SCALE2, None,
                                                    ALU.mult).then_inc(s_["nmax2"], 1)

                    def add_out(g, t):
                        if t == 0:
                            if g:
                                dve.wait_ge(s_["a_free"], A_AT["wo", g - 1, T - 1] + 1)
                            else:
                                dve.wait_ge(s_["bias_in"], 2 * T)
                        src = full_a()
                        nc.vector.tensor_tensor(hid[:, t], src, hid[:, t], ALU.add).then_inc(*Af.one())

                    for s in range(STEPS if main else 0):
                        units = list(scans[s])
                        if s < H2:
                            if s % G2 == 0:
                                v_lo(s // G2, units)
                            rope_in(s, 0)
                        if 2 <= s < H2 + 2:
                            diagonals(s - 2)
                        if s < H2:
                            rope_in(s, 1)
                        for t in range(T):
                            if 2 <= s < H2 + 2:
                                turned_lo(s - 2, t)
                            if t == 0 and s % G2 and units:
                                scan(units.pop(0))
                            if s in WO_STEP:
                                if t and units:
                                    scan(units.pop(0))
                                add_out(WO_STEP[s], t)
                                if s == STEPS - 1:
                                    dve.wait_ge(*Af.now())
                                    norm_tile(hid, t)
                        if 1 <= s <= H2:
                            row_maxima(s - 1)
                        for i in units:
                            scan(i)
                    if not main:
                        for i in range(NUNIT):
                            scan(i)
                        for e in range(EC):
                            dve.wait_ge(s_["y_acc"], NUNIT)
                            nc.vector.scalar_tensor_tensor(ys[:, e], us[:, e], col("ssm_d", e), PS[:, Y_BANKS[e]],
                                                           ALU.mult, ALU.add).then_inc(*own.one())
                        return

                    norm_stats()
                    norm_root()
                    norm_rows(hid, xn)
                    scaled_features(h2f, "ln2")
                    last_features_lo(h2f, 1)
                    src = full_a()

                    def step(ins, sem=None):
                        sem = sem or own.one()
                        ins.then_inc(*sem)
                        dve.wait_ge(sem[0], 1 if sem[0] is not own.sem else own.n)

                    def over_e(a):
                        return a.unsqueeze(2).to_broadcast([P, T, NEXP])

                    tt, tr = nc.vector.tensor_tensor, nc.vector.tensor_reduce
                    nc.vector.tensor_copy(gt[:, 4], src[:, 0:T * NEXP].rearrange("p (t e) -> p t e",
                                                                                e=NEXP)).then_inc(*Af.one())
                    dve.wait_ge(*Af.now())
                    step(tr(gv[:, 0], gt[:, 4], AX.X, ALU.max))
                    tt(gt[:, 0], gt[:, 4], over_e(gv[:, 0]), ALU.subtract).then_inc(s_["router_in"], 1)
                    dve.wait_ge(s_["router_exp"], 1)
                    step(tr(gv[:, 1], gt[:, 1], AX.X, ALU.add))
                    step(nc.vector.reciprocal(gv[:, 1], gv[:, 1]))
                    step(tt(gt[:, 4], gt[:, 1], over_e(gv[:, 1]), ALU.mult))
                    for e in range(NEXP):
                        me = gt[:, 4, :, e:e + 1]
                        if e:
                            tt(gt[:, 5, :, 0:e], gt[:, 4, :, 0:e], me.to_broadcast([P, T, e]),
                               ALU.is_ge).then_inc(*own.one())
                        step(tt(gt[:, 5, :, e:NEXP], gt[:, 4, :, e:NEXP], me.to_broadcast([P, T, NEXP - e]),
                                ALU.is_gt))
                        step(tr(gt[:, 6, :, e:e + 1], gt[:, 5], AX.X, ALU.add))
                    step(nc.vector.tensor_scalar(gt[:, 6], gt[:, 6], 1.5, None, ALU.is_lt))
                    step(tr(gv[:, 2], gt[:, 4], AX.X, ALU.max))
                    tt(gt[:, 2], gt[:, 4], over_e(gv[:, 2]), ALU.subtract).then_inc(s_["router_in"], 1)
                    dve.wait_ge(s_["router_exp"], 2)
                    step(tt(gt[:, 5], gt[:, 3], gt[:, 6], ALU.mult))
                    step(tr(gv[:, 3], gt[:, 5], AX.X, ALU.add))
                    step(nc.vector.reciprocal(gv[:, 3], gv[:, 3]))
                    step(tt(gt[:, 7], gt[:, 5], over_e(gv[:, 3]), ALU.mult), (s_["comb"], 1))
                    src = full_a()
                    nc.vector.tensor_copy(combt[0:NEXP].rearrange("p t n -> p (t n)"), src[0:NEXP]).then_inc(*Af.one())
                    dve.wait_ge(s_["x_added"], T)
                    for t in range(T):
                        src = full_a()
                        nc.vector.tensor_tensor(hid[:, t], src, hid[:, t], ALU.add).then_inc(*Af.one())
                    for e in range(NEXP):
                        if e == 1 and after is not None:
                            dve.wait_ge(s_["x_in"], 16)
                            for t in range(T):
                                norm_tile(xt, t)
                            norm_stats()
                        for i in scans[STEPS + e]:
                            scan(i)
                        dve.wait_ge(*Af.now())
                        if e == NEXP - 1 and after is not None:
                            features_next()
                        for t in range(T):
                            src = full_a()
                            nc.vector.scalar_tensor_tensor(hid[:, t], src, gt[:, 7, t, e:e + 1], hid[:, t],
                                                           ALU.mult, ALU.add).then_inc(*Af.one())
                        if e == 1 and after is not None:
                            norm_root()
                            norm_rows(xt, xn)
                    assert Af.n == a_expert(NEXP - 1) + T

        run(0, main=False, ssm=0)
        fresh()
        run(0, main=True, ssm=1, split=True)
        fresh()
        with nc.Fori(1, B - 1) as b:
            run(b, main=True, ssm=b + 1)
            fresh()
        run(B - 1, main=True, ssm=None)


def kernel(x, ctx_1024, L0_attn_w_qkv, L0_attn_b_qkv, L0_attn_w_out, L0_attn_b_out, L0_xattn_in_proj_w,
           L0_xattn_conv_w, L0_xattn_conv_b, L0_xattn_x_proj_w, L0_xattn_dt_proj_w, L0_xattn_dt_proj_b,
           L0_xattn_A_log, L0_xattn_D, L0_ffn_wq, L0_ffn_bq, L0_ffn_wk, L0_ffn_bk, L0_ffn_wv, L0_ffn_bv,
           L0_ffn_wo, L0_ffn_bo, L0_ffn_ln1_w, L0_ffn_ln1_b, L0_ffn_ln2_w, L0_ffn_ln2_b, L0_ffn_w_gate,
           L0_ffn_we1, L0_ffn_be1, L0_ffn_we2, L0_ffn_be2):
    import numpy as np
    import concourse.bacc as bacc
    from concourse.bass_utils import run_bass_kernel_spmd

    def tiles(w):
        w = np.asarray(w)
        return np.ascontiguousarray(w.reshape(-1, P, w.shape[1]).transpose(1, 0, 2).reshape(P, -1))

    def cols(v):
        return np.asarray(v).reshape(-1, P).T

    bq = np.asarray(L0_attn_b_qkv)
    fields = {
        "bq1": cols(bq[:D]), "bk1": cols(bq[D:D + P]), "conv_w": tiles(L0_xattn_conv_w),
        "conv_b": cols(L0_xattn_conv_b), "dt_b": cols(L0_xattn_dt_proj_b), "a_log": tiles(L0_xattn_A_log),
        "ssm_d": cols(L0_xattn_D), "ln1_w": cols(L0_ffn_ln1_w), "ln1_b": cols(L0_ffn_ln1_b),
        "ln2_w": cols(L0_ffn_ln2_w), "ln2_b": cols(L0_ffn_ln2_b), "bq2": cols(L0_ffn_bq),
        "bk2": cols(L0_ffn_bk), "bv2": cols(L0_ffn_bv), "be1": cols(np.asarray(L0_ffn_be1).reshape(-1)),
        "one": np.ones((P, 1), np.float32),
        "w_gate": tiles(L0_ffn_w_gate),
    }
    assert list(fields) == list(PCOLS)
    wq, wk, wv, wo = (np.asarray(w) for w in (L0_ffn_wq, L0_ffn_wk, L0_ffn_wv, L0_ffn_wo))
    chunks = [tiles(wv[:, D * g:D * (g + 1)]) for g in range(H2 // G2)]
    for p in range(H2 // 2):
        a, b = 2 * p * HD2, (2 * p + 1) * HD2
        chunks.append(tiles(np.concatenate([wq[:, a:a + HD2], wk[:, a:a + HD2],
                                            wq[:, b:b + HD2], wk[:, b:b + HD2]], axis=1)))
    chunks += [tiles(wo[D * g:D * (g + 1)]) for g in range(H2 // G2)]
    chunks += [tiles(w) for w in np.asarray(L0_ffn_we1)] + [tiles(w) for w in np.asarray(L0_ffn_we2)]

    freq = (np.float32(1.0) / np.float32(10000.0) ** (np.arange(0, HD2, 2, dtype=np.float32) / np.float32(HD2)))
    angle = freq[:, None].astype(np.float32) * np.arange(S, dtype=np.float32)[None, :]
    angle = np.concatenate([angle, angle], axis=0)
    sign = np.where(np.arange(P) < P // 2, 1.0, -1.0).astype(np.float32)[:, None]
    rope = np.stack([np.cos(angle), np.sin(angle) * sign], axis=1).astype(np.float32)
    causal = np.triu(np.full((P, P), -1e30, np.float32), 1)

    arrays = {
        "x": np.ascontiguousarray(np.asarray(x).reshape(B, T, P, D).transpose(0, 2, 1, 3)),
        "ctx_t": np.ascontiguousarray(np.asarray(ctx_1024).transpose(0, 2, 1).reshape(B, DM // P, P, S)
                                      .transpose(0, 2, 1, 3)),
        "w_qkv": tiles(np.asarray(L0_attn_w_qkv).T),
        "w_out": tiles(np.asarray(L0_attn_w_out).T),
        "in_w": tiles(np.asarray(L0_xattn_in_proj_w).T),
        "xp_w": tiles(np.asarray(L0_xattn_x_proj_w).T).reshape(P, EC, DR + 2 * DS),
        "dt_w": np.ascontiguousarray(np.asarray(L0_xattn_dt_proj_w).T),
        "params": np.ascontiguousarray(np.concatenate(list(fields.values()), axis=1)),
        "bias_rows": np.concatenate([np.asarray(L0_attn_b_out), np.asarray(L0_ffn_bo), bq[D + P:]])[None, :],
        "be2": np.asarray(L0_ffn_be2),
        "chunks": np.stack(chunks),
        "ident": np.eye(P, dtype=np.float32),
        "causal": causal,
        "rope": rope,
    }
    nc = bacc.Bacc("TRN2", target_bir_lowering=False, num_devices=1)
    aps = {n: nc.dram_tensor(n, a.shape, mybir.dt.from_np(a.dtype), kind="ExternalInput").ap()
           for n, a in arrays.items()}
    aps["out"] = nc.dram_tensor("out", (B, P, T, D), F32, kind="ExternalOutput").ap()
    build(nc, **aps)
    r = run_bass_kernel_spmd(nc, [arrays], core_ids=[0])
    return r.results[0]["out"].transpose(0, 2, 1, 3).reshape(B, S, D)
```
